# Optimizing a Trainium2 kernel written in Bass

```python
import numpy as np
import jax
import jax.numpy as jnp

def _softmax(x, axis=-1):
    return jax.nn.softmax(x, axis=axis)
def _gelu(x):
    return jax.nn.gelu(x, approximate=True)
def _silu(x):
    return jax.nn.silu(x)
def _sigmoid(x):
    return jax.nn.sigmoid(x)
def _layernorm(x, axis=-1, eps=1e-5):
    m = jnp.mean(x, axis=axis, keepdims=True)
    v = jnp.var(x, axis=axis, keepdims=True)
    return (x - m) / jnp.sqrt(v + eps)
def _scatter_add(tgt, idx, src, axis=0):
    return tgt.at[idx].add(src)
def _segment_sum(src, seg, n):
    return jax.ops.segment_sum(src, seg, n)

kernel_name = 'mk_conv_preact_d2_conv_nchw64_480066'

def setup_inputs(seed: int = 0):
    np.random.seed(seed)
    _w = jnp.asarray
    def _rec_inputs():
        import jax
        import jax.numpy as jnp
        _gk = jax.random.key(seed)
        x = -0.000125 + 0.9999 * jax.random.normal(jax.random.fold_in(_gk, 1), (8, 64, 256, 256), jnp.float32)
        return x
    x = _rec_inputs()
    def _L0_conv_setup():
        import jax, jax.numpy as jnp
        import numpy as np
        EPS = 1e-05

        def _shift1(x):
            c = x.shape[-1]
            q = c // 4
            g0 = jnp.concatenate([x[:, :1, :, :q], x[:, :-1, :, :q]], axis=1)
            g1 = jnp.concatenate([x[:, 1:, :, q:2 * q], x[:, -1:, :, q:2 * q]], axis=1)
            g2 = jnp.concatenate([x[:, :, :1, 2 * q:3 * q], x[:, :, :-1, 2 * q:3 * q]], axis=2)
            g3 = jnp.concatenate([x[:, :, 1:, 3 * q:], x[:, :, -1:, 3 * q:]], axis=2)
            return jnp.concatenate([g0, g1, g2, g3], axis=-1)

        def _shift2(x):
            c = x.shape[-1]
            q = c // 4
            g0 = jnp.concatenate([x[:, :, :1, :q], x[:, :, :-1, :q]], axis=2)
            g1 = jnp.concatenate([x[:, :, 1:, q:2 * q], x[:, :, -1:, q:2 * q]], axis=2)
            g2 = jnp.concatenate([x[:, :1, :, 2 * q:3 * q], x[:, :-1, :, 2 * q:3 * q]], axis=1)
            g3 = jnp.concatenate([x[:, 1:, :, 3 * q:], x[:, -1:, :, 3 * q:]], axis=1)
            return jnp.concatenate([g0, g1, g2, g3], axis=-1)
        key = jax.random.key(seed)
        ks = jax.random.split(key, 8)
        B, C, W, H = (8, 64, 256, 256)
        s = 1.0 / np.sqrt(C)
        return {'x': jax.random.normal(ks[0], (B, C, W, H), dtype=jnp.float32), 'mlp1_w': jax.random.uniform(ks[1], (3 * C, C), jnp.float32, -s, s), 'mlp1_b': jax.random.uniform(ks[2], (3 * C,), jnp.float32, -s, s), 'mlp2_w': jax.random.uniform(ks[3], (C, C), jnp.float32, -s, s), 'mlp2_b': jax.random.uniform(ks[4], (C,), jnp.float32, -s, s), 'sa1_w': jax.random.uniform(ks[5], (C, C), jnp.float32, -s, s), 'sa2_w': jax.random.uniform(ks[6], (2 * C, C), jnp.float32, -s, s), 'bn_gamma': jnp.ones((C,), jnp.float32), 'bn_beta': jnp.zeros((C,), jnp.float32)}
    _L0_conv_all = _L0_conv_setup()
    _L0_conv_in = {k: v for k, v in _L0_conv_all.items() if k in ('mlp1_w', 'mlp1_b', 'mlp2_w', 'mlp2_b', 'sa1_w', 'sa2_w', 'bn_gamma', 'bn_beta', )}
    del _L0_conv_all

    def _L1_conv_setup():
        import jax, jax.numpy as jnp
        import numpy as np
        B, CIN, COUT, H, W, M1, M2 = (8, 64, 64, 256, 256, 32, 32)
        key = jax.random.key(seed)
        kx, k1r, k1i, k2r, k2i = jax.random.split(key, 5)
        scale = 1.0 / (CIN * COUT)
        x = jax.random.normal(kx, (B, CIN, H, W), dtype=jnp.float32)
        wshape = (CIN, COUT, M1, M2)
        u = lambda k: jax.random.uniform(k, wshape, jnp.float32, -scale, scale)
        return {'x': x, 'w1_real': u(k1r), 'w1_imag': u(k1i), 'w2_real': u(k2r), 'w2_imag': u(k2i)}
    _L1_conv_all = _L1_conv_setup()
    _L1_conv_in = {k: v for k, v in _L1_conv_all.items() if k in ('w1_real', 'w1_imag', 'w2_real', 'w2_imag', )}
    del _L1_conv_all

    return {
        "x": x,
        "L0_conv_mlp1_w": _L0_conv_in["mlp1_w"],
        "L0_conv_mlp1_b": _L0_conv_in["mlp1_b"],
        "L0_conv_mlp2_w": _L0_conv_in["mlp2_w"],
        "L0_conv_mlp2_b": _L0_conv_in["mlp2_b"],
        "L0_conv_sa1_w": _L0_conv_in["sa1_w"],
        "L0_conv_sa2_w": _L0_conv_in["sa2_w"],
        "L0_conv_bn_gamma": _L0_conv_in["bn_gamma"],
        "L0_conv_bn_beta": _L0_conv_in["bn_beta"],
        "L1_conv_w1_real": _L1_conv_in["w1_real"],
        "L1_conv_w1_imag": _L1_conv_in["w1_imag"],
        "L1_conv_w2_real": _L1_conv_in["w2_real"],
        "L1_conv_w2_imag": _L1_conv_in["w2_imag"],
    }

def reference(x, L0_conv_mlp1_w, L0_conv_mlp1_b, L0_conv_mlp2_w, L0_conv_mlp2_b, L0_conv_sa1_w, L0_conv_sa2_w, L0_conv_bn_gamma, L0_conv_bn_beta, L1_conv_w1_real, L1_conv_w1_imag, L1_conv_w2_real, L1_conv_w2_imag):
    import jax
    import jax.numpy as jnp
    def _L0_conv_ref(x, mlp1_w, mlp1_b, mlp2_w, mlp2_b, sa1_w, sa2_w, bn_gamma, bn_beta):
        import jax, jax.numpy as jnp
        import numpy as np
        EPS = 1e-05

        def _shift1(x):
            c = x.shape[-1]
            q = c // 4
            g0 = jnp.concatenate([x[:, :1, :, :q], x[:, :-1, :, :q]], axis=1)
            g1 = jnp.concatenate([x[:, 1:, :, q:2 * q], x[:, -1:, :, q:2 * q]], axis=1)
            g2 = jnp.concatenate([x[:, :, :1, 2 * q:3 * q], x[:, :, :-1, 2 * q:3 * q]], axis=2)
            g3 = jnp.concatenate([x[:, :, 1:, 3 * q:], x[:, :, -1:, 3 * q:]], axis=2)
            return jnp.concatenate([g0, g1, g2, g3], axis=-1)

        def _shift2(x):
            c = x.shape[-1]
            q = c // 4
            g0 = jnp.concatenate([x[:, :, :1, :q], x[:, :, :-1, :q]], axis=2)
            g1 = jnp.concatenate([x[:, :, 1:, q:2 * q], x[:, :, -1:, q:2 * q]], axis=2)
            g2 = jnp.concatenate([x[:, :1, :, 2 * q:3 * q], x[:, :-1, :, 2 * q:3 * q]], axis=1)
            g3 = jnp.concatenate([x[:, 1:, :, 3 * q:], x[:, -1:, :, 3 * q:]], axis=1)
            return jnp.concatenate([g0, g1, g2, g3], axis=-1)
        b, c, w, h = x.shape
        xp = jnp.transpose(x, (0, 2, 3, 1))
        y = jnp.einsum('bwhc,dc->bwhd', xp, mlp1_w) + mlp1_b
        x1 = _shift1(y[..., :c])
        x2 = _shift2(y[..., c:2 * c])
        mean = jnp.mean(x, axis=(0, 2, 3))
        var = jnp.var(x, axis=(0, 2, 3))
        xn = (x - mean[:, None, None]) * jax.lax.rsqrt(var + EPS)[:, None, None]
        xn = xn * bn_gamma[:, None, None] + bn_beta[:, None, None]
        wbn = jax.lax.stop_gradient(jnp.abs(bn_gamma) / jnp.sum(jnp.abs(bn_gamma)))
        x3 = jax.nn.sigmoid(xn * wbn[:, None, None]) * x
        a = jnp.sum(x1, axis=(1, 2)) + jnp.sum(x2, axis=(1, 2))
        hat = jnp.einsum('bc,dc->bd', jax.nn.gelu(jnp.einsum('bc,dc->bd', a, sa1_w), approximate=False), sa2_w)
        bar = jax.nn.softmax(hat.reshape(b, 2, c), axis=1)
        out = bar[:, 0][:, None, None, :] * x1 + bar[:, 1][:, None, None, :] * x2
        o = jnp.einsum('bwhc,dc->bwhd', out, mlp2_w) + mlp2_b
        o = jnp.transpose(o, (0, 3, 1, 2)) * x3
        return o

    def _L1_conv_ref(x, w1_real, w1_imag, w2_real, w2_imag):
        import jax, jax.numpy as jnp
        import numpy as np
        B, CIN, COUT, H, W, M1, M2 = (8, 64, 64, 256, 256, 32, 32)
        w1 = jax.lax.complex(w1_real, w1_imag)
        w2 = jax.lax.complex(w2_real, w2_imag)
        m1, m2 = (w1.shape[2], w1.shape[3])
        b, _, h, w = x.shape
        wf = w // 2 + 1
        x_ft = jnp.fft.rfft2(x)
        top = jnp.einsum('bixy,ioxy->boxy', x_ft[:, :, :m1, :m2], w1)
        bot = jnp.einsum('bixy,ioxy->boxy', x_ft[:, :, -m1:, :m2], w2)
        out_ft = jnp.zeros((b, w1.shape[1], h, wf), dtype=top.dtype)
        out_ft = out_ft.at[:, :, :m1, :m2].set(top)
        out_ft = out_ft.at[:, :, -m1:, :m2].set(bot)
        return jnp.fft.irfft2(out_ft, s=(h, w))

    def _gn(v, G=32, eps=1e-5):
        B_, C_, H_, W_ = v.shape
        g = v.reshape(B_, G, C_ // G, H_, W_)
        m = jnp.mean(g, axis=(2, 3, 4), keepdims=True)
        s = jnp.var(g, axis=(2, 3, 4), keepdims=True)
        return ((g - m) / jnp.sqrt(s + eps)).reshape(v.shape)

    def _ln_c(v, eps=1e-6):
        m = jnp.mean(v, axis=1, keepdims=True)
        s = jnp.var(v, axis=1, keepdims=True)
        return (v - m) / jnp.sqrt(s + eps)

    def _ln_t(v, eps=1e-5):
        m = jnp.mean(v, axis=-1, keepdims=True)
        s = jnp.var(v, axis=-1, keepdims=True)
        return (v - m) / jnp.sqrt(s + eps)

    def _to_tokens(v):
        B_, C_, H_, W_ = v.shape
        return v.reshape(B_, C_, H_ * W_).transpose(0, 2, 1)
    def _from_tokens(t, like):
        B_, C_, H_, W_ = like.shape
        return t.transpose(0, 2, 1).reshape(B_, C_, H_, W_)

    x = x + _L0_conv_ref(_gn(x), L0_conv_mlp1_w, L0_conv_mlp1_b, L0_conv_mlp2_w, L0_conv_mlp2_b, L0_conv_sa1_w, L0_conv_sa2_w, L0_conv_bn_gamma, L0_conv_bn_beta)
    x = x + _L1_conv_ref(_gn(x), L1_conv_w1_real, L1_conv_w1_imag, L1_conv_w2_real, L1_conv_w2_imag)
    return x


_drawn_inputs = setup_inputs


def setup_inputs(seed=0):
    import zlib

    import numpy as np

    out = dict(_drawn_inputs(seed))
    spreads = {'L0_conv_bn_gamma': (1.0, 0.6), 'L0_conv_bn_beta': (0.0, 2.0)}
    factors = {'L1_conv_w1_real': 200.0,
     'L1_conv_w1_imag': 200.0,
     'L1_conv_w2_real': 200.0,
     'L1_conv_w2_imag': 200.0}
    for name, (base, spread) in spreads.items():
        noise = np.random.default_rng([zlib.crc32(name.encode()), seed]).standard_normal(out[name].shape)
        drawn = base * np.exp(spread * noise) if base else spread * noise
        out[name] = jnp.asarray(drawn.astype(out[name].dtype))
    for name, factor in factors.items():
        out[name] = (out[name] * factor).astype(out[name].dtype)
    return out
```

```python
from contextlib import ExitStack

import concourse.bass as bass
from concourse import mybir
import numpy as np

F32 = mybir.dt.float32
ACT = mybir.ActivationFunctionType
ALU = mybir.AluOpType
AX_X = mybir.AxisListType.X

P = 128
B, C, H, W = 8, 64, 256, 256
M1, M2 = 32, 32
NPIX = H * W
EPS = 1e-5
HALF = H // 2
NS = 4
DIRS = ((0, 1, 2, 3), (2, 3, 0, 1))

TR = 16
NT = HALF // TR
SP_ = 8
SC = SP_ * W
MR = 32
LAYOUT = ((0, 0, 2), (1, 0, 1), (0, 1, 0), (1, 1, 3))
PITCH = W + 1
NM = M1 + 1
KX = 2 * M1
CG = 8
NG = C // CG
RK = KX * M2

OFF = {}


def constants():
    parts = []

    def put(name, a):
        a = np.asarray(a, np.float64)
        full = np.zeros((P, a.shape[1]))
        full[: a.shape[0]] = a
        OFF[name] = (sum(q.shape[1] for q in parts), a.shape[1])
        parts.append(full)

    p = np.arange(P)
    c = p % C
    put("ident", np.eye(P))
    put("group", 0.25 * (c[:, None] // 2 == c[None, :] // 2))
    put("chan", 0.5 * (c[:, None] == c[None, :]))
    put("halfones", np.full((P, P), 0.5))
    put("ones", np.ones((P, P)))
    dmask = np.zeros((P, NS))
    for branch in range(2):
        for q in range(4):
            dmask[branch * C + q * 16: branch * C + (q + 1) * 16, DIRS[branch][q]] = 1
    put("dmask", dmask)
    put("rowsel", np.stack([1.0 * (p < C), -1.0 * (p >= C)], 1))
    put("sign", np.stack([np.where(p < C, 1.0, -1.0)] * 2, 1))
    put("npix", np.full((1, B), float(NPIX)))
    th = 2 * np.pi / H
    row = np.arange(H)
    k = np.arange(NM)
    cs = np.concatenate([np.cos(th * np.outer(row, k)), np.sin(th * np.outer(row, k))], 1)
    put("frow", cs.reshape(2, P, 2 * NM).transpose(1, 0, 2).reshape(P, -1))
    col = np.arange(W)
    a = 2 * np.pi / W * np.outer(col, np.arange(M2))
    cc, ss = np.cos(a), np.sin(a)
    fc = np.concatenate([cc, -ss, cc, -ss], 1)
    fs = np.concatenate([-ss, -cc, ss, cc], 1)
    fcol = np.stack([fc, fs], 1).reshape(2, P, 2, 4 * M2).transpose(1, 0, 2, 3)
    put("fcol", fcol.reshape(P, -1))
    kx = np.concatenate([np.arange(M1), np.arange(-M1, 0)])
    ar = th * np.outer(kx, row)
    put("irow", np.concatenate([np.cos(ar), -np.sin(ar)], 0))
    wt = np.where(np.arange(M2) == 0, 1.0, 2.0)[:, None] / NPIX
    ac = 2 * np.pi / W * np.outer(np.arange(M2), col)
    ih = np.concatenate([wt * np.cos(ac), -wt * np.sin(ac)], 0)
    put("icol", np.block([[ih, np.zeros_like(ih)], [np.zeros_like(ih), ih]]))
    return np.concatenate(parts, 1).astype(np.float32)


CONST = constants()


def program(nc, x, w1m, b1m, w2m, b2m, sa1, sa2, gamma, beta, wr1, wi1, wr2, wi2, const, out):
    top = ExitStack()
    with top:
        def sem(name):
            return top.enter_context(nc.semaphore(name))

        x1 = nc.dram_tensor("x1_scratch", (B, C, H, W), F32, kind="Internal").ap()
        xd = nc.dram_tensor("modes_in", (P, B, 2, KX, M2), F32, kind="Internal").ap()
        yd = nc.dram_tensor("modes_out", (2 * B, KX, M2, C), F32, kind="Internal").ap()
        x_bc = x.rearrange("b c h w -> (b c) (h w)")
        x_rows = x.rearrange("b c h w -> (b c) h w")
        x1_bc = x1.rearrange("b c h w -> (b c) (h w)")
        x1_rows = x1.rearrange("b c h w -> h (b c) w")
        out_rows = out.rearrange("b c h w -> h (b c) w")

        psum = top.enter_context(nc.psum_tensor("psum", [P, 4096], F32))

        def bank(n, cols=512, parts=P, first=0):
            return psum[first:first + parts, n * 512:n * 512 + cols]

        def sb(ctx, name, shape):
            return ctx.enter_context(nc.sbuf_tensor(name, shape, F32))

        def table(ctx, names):
            t = sb(ctx, "tab_" + "_".join(names), [P, sum(OFF[n][1] for n in names)])
            at, got = 0, {}
            for n in names:
                o, k = OFF[n]
                got[n] = (t[:, at:at + k], const[:, o:o + k])
                at += k
            return got

        params = sb(top, "params", [P, B + 1, 4])
        wall = sb(top, "wall", [P, B + 1, P])
        sums = sb(top, "sums", [P, B * 2 * NT])
        sqs = sb(top, "sqs", [P, B * 2 * NT])
        norm2 = sb(top, "norm2", [P, 2, B])
        means = sb(top, "means", [P, B])

        ph = ExitStack()
        with ph:
            XT = [sb(ph, f"stat_x{i}", [P, TR * W]) for i in range(2)]
            stats = sb(ph, "stats", [P, B * NT * 8 * 6])
            mv = sb(ph, "mv", [P, B, 2])
            ecol = sb(ph, "ecol", [P, B * NT * 2])
            erow = sb(ph, "erow", [P, B * 2])
            junk = sb(ph, "junk", [P, W])
            names = ["ident", "group", "chan", "halfones", "ones", "dmask", "rowsel", "npix"]
            T = table(ph, names)
            ident, group, chan, halfones, ones, dmask, rowsel, npix = (T[n][0] for n in names)
            w1d = sb(ph, "w1d", [P, 2, C])
            w2d = sb(ph, "w2d", [C, 2, C])
            sa1s = sb(ph, "sa1s", [C, C])
            sa2s = sb(ph, "sa2s", [P, C])
            b1c = sb(ph, "b1c", [P, 1])
            b1r = sb(ph, "b1r", [1, P])
            vec = sb(ph, "vec", [P, 3])
            w1t = sb(ph, "w1t", [C, P])
            w2t = sb(ph, "w2t", [P, 2, C])
            sa1t = sb(ph, "sa1t", [C, C])
            sa2t = sb(ph, "sa2t", [C, P])
            sm = sb(ph, "sm", [P, 32, B])
            col = sb(ph, "col", [P, 16])
            td = sb(ph, "td", [P, NS, B])
            asb = sb(ph, "asb", [B, C])
            at = sb(ph, "at", [C, B])
            gt = sb(ph, "gt", [C, B])
            soft = sb(ph, "soft", [B, 6, C])
            bart = sb(ph, "bart", [P, B])
            diag = sb(ph, "diag", [C, B, C])
            w2s = sb(ph, "w2s", [P, B, C])
            mb = sb(ph, "mb", [P, B, NS])
            rhs = sb(ph, "rhs", [P, B, NS, C])

            s_x = [sem(f"stat_loaded{i}") for i in range(2)]
            stat_dve, stat_act = sem("stat_dve_done"), sem("stat_act_done")
            edge_order = sem("edge_order")
            weights = sem("weights_loaded")

            with nc.Block() as block:
                @block.sync
                def _(sp):
                    with sp.Fori(0, B) as b:
                        for t in range(NT):
                            sp.wait_ge(stat_dve, b * NT + t + 1)
                            sp.wait_ge(stat_act, b * NT + t + 1)
                            for s in range(2):
                                r0 = (s * HALF + t * TR) * W
                                sp.dma_start(XT[t % 2][s * C:(s + 1) * C, :],
                                             x_bc[bass.ds(b * C, C), r0:r0 + TR * W]
                                             ).then_inc(s_x[t % 2], 16)

                @block.gpsimd
                def _(pool):
                    for n in names:
                        pool.dma_start(T[n][0], T[n][1]).then_inc(weights, 16)
                    for j in range(2):
                        pool.dma_start(w1d[:, j, :], w1m[0:P, :]).then_inc(weights, 16)
                        pool.dma_start(w2d[:, j, :], w2m).then_inc(weights, 16)
                        for n, v in enumerate((b2m, gamma, beta)):
                            pool.dma_start(vec[j * C:(j + 1) * C, n:n + 1],
                                           v.rearrange("(p a) -> p a", a=1)).then_inc(weights, 16)
                    pool.dma_start(sa1s[:, :], sa1).then_inc(weights, 16)
                    pool.dma_start(sa2s[:, :], sa2).then_inc(weights, 16)
                    pool.dma_start(b1c[:, :], b1m[0:P].rearrange("(p a) -> p a", a=1)).then_inc(weights, 16)
                    pool.dma_start(b1r[:, :], b1m[0:P].rearrange("(a p) -> a p", a=1)).then_inc(weights, 16)
                    pool.memset(wall[:, B, :], 0.0)
                    pool.memset(params[:, B, :], 0.0)
                    pool.wait_ge(weights, 16 * (len(names) + 14))

                @block.scalar
                def _(act):
                    act.sem_inc(stat_act, 2)
                    act.sem_inc(edge_order, 1)
                    with act.Fori(0, B) as b:
                        k = 0
                        for t in range(NT):
                            act.wait_ge(s_x[t % 2], b * (NT // 2 * 32) + (t // 2 + 1) * 32)
                            xt = XT[t % 2][:, :].rearrange("p (r w) -> p r w", w=W)
                            todo = [(xt[:, :, 0], ecol, b * (NT * 2) + t * 2, TR),
                                    (xt[:, :, W - 1], ecol, b * (NT * 2) + t * 2 + 1, TR)]
                            if t == 0:
                                todo.append((xt[:, 0, :], erow, b * 2, W))
                            if t == NT - 1:
                                todo.append((xt[:, TR - 1, :], erow, b * 2 + 1, W))
                            for src, dst, idx, width in todo:
                                act.wait_ge(edge_order, b * (NT * 2 + 2) + k + 1)
                                act.activation(junk[:, 0:width], src, ACT.Copy,
                                               accum_out=dst[:, bass.ds(idx, 1)]).then_inc(edge_order, 1)
                                k += 1
                            act.wait_ge(edge_order, b * (NT * 2 + 2) + k + 1)
                            act.sem_inc(stat_act, 1)

                @block.vector
                def _(dve):
                    dve.sem_inc(stat_dve, 2)
                    with dve.Fori(0, B) as b:
                        for t in range(NT):
                            dve.wait_ge(s_x[t % 2], b * (NT // 2 * 32) + (t // 2 + 1) * 32)
                            for q in range(8):
                                last = nc.vector.bn_stats(stats[:, bass.ds(b * (NT * 48) + (t * 8 + q) * 6, 6)],
                                                          XT[t % 2][:, q * 512:(q + 1) * 512])
                            last.then_inc(stat_dve, 1)
                    dve.wait_ge(stat_dve, 2 + B * NT)
                    for b in range(B):
                        nc.vector.bn_aggr(mv[:, b, :], stats[:, b * NT * 48:(b + 1) * NT * 48])

            STEPS = ("transposes", "evac_w", "group_mean", "dev", "dev2", "devar", "group_var", "veps",
                     "std", "rstd", "nmean", "edges", "cdiff", "rsel", "rdiff", "cdiffr",
                     "rdiffr", "chan_sums", "cs_copy", "bmean", "bmean8", "var_r", "dev_c", "var_rr", "dev_c2",
                     "bvar", "bsum", "absg1", "absg2", "bn_sums", "bveps", "bstd", "brstd", "wbn", "gwbn",
                     "kscale", "A", "mr", "mrb", "Bneg", "Bias", "npsum", "td", "pooled", "pool_copy", "pool_t",
                     "at", "squeeze", "gelu", "excite", "h0", "hmax", "l0", "exps", "esum", "rsum", "bar",
                     "bar_t", "bart", "shift_in", "z", "zb", "mask", "w2s", "shift_out", "cb", "cbr", "rhs",
                     "mats", "wall")

            def at_(name):
                return STEPS.index(name)

            prep = sem("prep")
            r, nmean, mr = sm[:, 6, :], sm[:, 8, :], sm[:, 11, :]
            k1 = col[:, 12:13]
            mean, var = mv[:, :, 0], mv[:, :, 1]
            with nc.Block() as block:
                @block.tensor
                def _(pe):
                    nc.tensor.transpose(bank(0, P, C), w1d[:, 0, :], ident)
                    nc.tensor.transpose(bank(1, C), w2d[:, :, :].rearrange("p a c -> p (a c)"), ident[0:C, 0:C])
                    nc.tensor.transpose(bank(2, C, C), sa1s[:, :], ident[0:C, 0:C])
                    nc.tensor.transpose(bank(3, P, C), sa2s[:, :], ident).then_inc(prep, 1)
                    pe.wait_ge(prep, at_("group_mean"))
                    nc.tensor.matmul(bank(4, B), group, sm[:, 0, :], start=True, stop=True).then_inc(prep, 1)
                    pe.wait_ge(prep, at_("group_var"))
                    nc.tensor.matmul(bank(5, B), group, sm[:, 3, :], start=True, stop=True).then_inc(prep, 1)
                    pe.wait_ge(prep, at_("chan_sums"))
                    nc.tensor.matmul(bank(6, 3 * B), chan, sm[:, 8:11, :].rearrange("p a b -> p (a b)"),
                                     start=True, stop=True).then_inc(prep, 1)
                    pe.wait_ge(prep, at_("bn_sums"))
                    nc.tensor.matmul(psum[:, 3584:3585], chan, col[:, 4:5], start=True, stop=True)
                    nc.tensor.matmul(psum[:, 3585:3586], halfones, col[:, 6:7], start=True,
                                     stop=True).then_inc(prep, 1)
                    pe.wait_ge(prep, at_("pooled"))
                    for q in range(4):
                        j = slice(q * 16, q * 16 + 16)
                        k = slice(C + q * 16, C + q * 16 + 16)
                        o = psum[0:B, j]
                        nc.tensor.matmul(o, td[0:C, DIRS[0][q], :], w1t[:, j], start=True, stop=False)
                        nc.tensor.matmul(o, td[0:C, DIRS[1][q], :], w1t[:, k], start=False, stop=False)
                        nc.tensor.matmul(o, npix[0:1, :], b1r[:, j], start=False, stop=False)
                        last = nc.tensor.matmul(o, npix[0:1, :], b1r[:, k], start=False, stop=True)
                    last.then_inc(prep, 1)
                    pe.wait_ge(prep, at_("pool_t"))
                    nc.tensor.transpose(bank(1, B, C), asb[:, :], ident[0:B, 0:B]).then_inc(prep, 1)
                    pe.wait_ge(prep, at_("squeeze"))
                    nc.tensor.matmul(bank(2, B, C), sa1t[:, :], at[:, :], start=True, stop=True).then_inc(prep, 1)
                    pe.wait_ge(prep, at_("excite"))
                    nc.tensor.matmul(bank(3, P, B), gt[:, :], sa2t[:, :], start=True, stop=True).then_inc(prep, 1)
                    pe.wait_ge(prep, at_("bar_t"))
                    nc.tensor.transpose(bank(0, B), soft[:, 1:3, :].rearrange("p a c -> p (a c)"),
                                        ident[0:B, 0:B]).then_inc(prep, 1)
                    pe.wait_ge(prep, at_("shift_in"))
                    nc.tensor.matmul(bank(1, B), w1t[:, :], sm[0:C, 12, :], start=True, stop=True)
                    nc.tensor.matmul(bank(2), ones[0:C, :], diag[:, :, :].rearrange("p b c -> p (b c)"),
                                     start=True, stop=True).then_inc(prep, 1)
                    pe.wait_ge(prep, at_("shift_out"))
                    nc.tensor.matmul(bank(3, B), w2t[:, :, :].rearrange("p a c -> p (a c)"), sm[:, 14, :],
                                     start=True, stop=True).then_inc(prep, 1)
                    pe.wait_ge(prep, at_("mats"))
                    for b in range(B):
                        last = nc.tensor.matmul(psum[:, b * 256:(b + 1) * 256],
                                                w1d[:, :, :].rearrange("p a c -> p (a c)"),
                                                rhs[:, b, :, :].rearrange("p d o -> p (d o)"),
                                                start=True, stop=True)
                    last.then_inc(prep, 1)

                @block.scalar
                def _(act):
                    act.wait_ge(prep, at_("std"))
                    act.activation(sm[:, 5, :], sm[:, 4, :], ACT.Sqrt).then_inc(prep, 1)
                    act.wait_ge(prep, at_("bstd"))
                    act.activation(col[:, 3:4], col[:, 2:3], ACT.Sqrt).then_inc(prep, 1)
                    act.wait_ge(prep, at_("gelu"))
                    act.activation(gt[:, :], bank(2, B, C), ACT.Gelu).then_inc(prep, 1)
                    act.wait_ge(prep, at_("exps"))
                    act.activation(soft[:, 3:5, :], soft[:, 1:3, :], ACT.Exp).then_inc(prep, 1)

                @block.vector
                def _(dve):
                    v = nc.vector
                    dve.wait_ge(prep, at_("evac_w"))
                    v.tensor_copy(w1t[:, :], bank(0, P, C))
                    v.tensor_copy(w2t[:, 0, :], bank(1, C))
                    v.tensor_copy(w2t[:, 1, :], bank(1, C))
                    v.tensor_copy(sa1t[:, :], bank(2, C, C))
                    v.tensor_copy(sa2t[:, :], bank(3, P, C))
                    v.tensor_copy(sm[:, 0, :], mean).then_inc(prep, 1)
                    dve.wait_ge(prep, at_("dev"))
                    v.scalar_tensor_tensor(out=sm[:, 1, :], in0=bank(4, B), scalar=-1.0, in1=sm[:, 0, :], op0=ALU.mult, op1=ALU.add).then_inc(prep, 1)
                    dve.wait_ge(prep, at_("dev2"))
                    v.tensor_tensor(sm[:, 2, :], sm[:, 1, :], sm[:, 1, :], ALU.mult).then_inc(prep, 1)
                    dve.wait_ge(prep, at_("devar"))
                    v.tensor_tensor(sm[:, 3, :], sm[:, 2, :], var, ALU.add).then_inc(prep, 1)
                    dve.wait_ge(prep, at_("veps"))
                    v.tensor_scalar(sm[:, 4, :], bank(5, B), EPS, None, ALU.add).then_inc(prep, 1)
                    dve.wait_ge(prep, at_("rstd"))
                    v.reciprocal(r, sm[:, 5, :]).then_inc(prep, 1)
                    dve.wait_ge(prep, at_("nmean"))
                    v.tensor_tensor(nmean, sm[:, 1, :], r, ALU.mult).then_inc(prep, 1)
                    dve.wait_ge(prep, at_("edges"))
                    v.reduce_sum(sm[:, 16:18, :], ecol[:, :].rearrange("p (b t e) -> p e b t", t=NT, e=2), axis=AX_X).then_inc(prep, 1)
                    dve.wait_ge(prep, at_("cdiff"))
                    v.tensor_tensor(sm[:, 18, :], sm[:, 16, :], sm[:, 17, :], ALU.subtract).then_inc(prep, 1)
                    dve.wait_ge(prep, at_("rsel"))
                    v.tensor_scalar(sm[:, 19, :], erow[:, 0::2], rowsel[:, 0:1], None, ALU.mult).then_inc(prep, 1)
                    dve.wait_ge(prep, at_("rdiff"))
                    v.scalar_tensor_tensor(out=sm[:, 20, :], in0=erow[:, 1::2], scalar=rowsel[:, 1:2], in1=sm[:, 19, :], op0=ALU.mult, op1=ALU.add).then_inc(prep, 1)
                    dve.wait_ge(prep, at_("cdiffr"))
                    v.tensor_tensor(sm[:, 9, :], sm[:, 18, :], r, ALU.mult).then_inc(prep, 1)
                    dve.wait_ge(prep, at_("rdiffr"))
                    v.tensor_tensor(sm[:, 10, :], sm[:, 20, :], r, ALU.mult).then_inc(prep, 1)
                    dve.wait_ge(prep, at_("cs_copy"))
                    v.tensor_copy(sm[:, 21:24, :].rearrange('p a b -> p (a b)'), bank(6, 3 * B)).then_inc(prep, 1)
                    dve.wait_ge(prep, at_("bmean"))
                    v.reduce_sum(col[:, 0:1], sm[:, 21, :], axis=AX_X).then_inc(prep, 1)
                    dve.wait_ge(prep, at_("bmean8"))
                    v.tensor_scalar(col[:, 1:2], col[:, 0:1], 1.0 / B, None, ALU.mult).then_inc(prep, 1)
                    dve.wait_ge(prep, at_("var_r"))
                    v.tensor_tensor(sm[:, 24, :], var, r, ALU.mult).then_inc(prep, 1)
                    dve.wait_ge(prep, at_("dev_c"))
                    v.tensor_scalar(sm[:, 25, :], nmean, col[:, 1:2], None, ALU.subtract).then_inc(prep, 1)
                    dve.wait_ge(prep, at_("var_rr"))
                    v.tensor_tensor(sm[:, 26, :], sm[:, 24, :], r, ALU.mult).then_inc(prep, 1)
                    dve.wait_ge(prep, at_("dev_c2"))
                    v.tensor_tensor(sm[:, 27, :], sm[:, 25, :], sm[:, 25, :], ALU.mult).then_inc(prep, 1)
                    dve.wait_ge(prep, at_("bvar"))
                    v.tensor_tensor(sm[:, 28, :], sm[:, 26, :], sm[:, 27, :], ALU.add).then_inc(prep, 1)
                    dve.wait_ge(prep, at_("bsum"))
                    v.reduce_sum(col[:, 4:5], sm[:, 28, :], axis=AX_X).then_inc(prep, 1)
                    dve.wait_ge(prep, at_("absg1"))
                    v.tensor_scalar(col[:, 5:6], vec[:, 1:2], -1.0, None, ALU.mult).then_inc(prep, 1)
                    dve.wait_ge(prep, at_("absg2"))
                    v.tensor_tensor(col[:, 6:7], col[:, 5:6], vec[:, 1:2], ALU.max).then_inc(prep, 1)
                    dve.wait_ge(prep, at_("bveps"))
                    v.tensor_scalar(col[:, 2:3], psum[:, 3584:3585], 1.0 / B, EPS, ALU.mult, ALU.add).then_inc(prep, 1)
                    dve.wait_ge(prep, at_("brstd"))
                    v.reciprocal(col[:, 11:12], col[:, 3:4]).then_inc(prep, 1)
                    dve.wait_ge(prep, at_("wbn"))
                    v.reciprocal(col[:, 7:8], psum[:, 3585:3586]).then_inc(prep, 1)
                    dve.wait_ge(prep, at_("gwbn"))
                    v.tensor_tensor(col[:, 8:9], col[:, 7:8], col[:, 6:7], ALU.mult).then_inc(prep, 1)
                    dve.wait_ge(prep, at_("kscale"))
                    v.tensor_tensor(col[:, 9:10], col[:, 8:9], vec[:, 1:2], ALU.mult)
                    v.tensor_tensor(col[:, 10:11], col[:, 8:9], vec[:, 2:3], ALU.mult).then_inc(prep, 1)
                    dve.wait_ge(prep, at_("A"))
                    v.tensor_tensor(k1, col[:, 11:12], col[:, 9:10], ALU.mult).then_inc(prep, 1)
                    dve.wait_ge(prep, at_("mr"))
                    v.tensor_scalar(params[:, 0:B, 0], r, k1, None, ALU.mult)
                    v.tensor_tensor(mr, bank(4, B), r, ALU.mult).then_inc(prep, 1)
                    dve.wait_ge(prep, at_("mrb"))
                    v.tensor_scalar(sm[:, 12, :], mr, -1.0, None, ALU.mult)
                    v.tensor_tensor(col[:, 13:14], k1, col[:, 1:2], ALU.mult).then_inc(prep, 1)
                    dve.wait_ge(prep, at_("Bneg"))
                    v.tensor_tensor(col[:, 14:15], col[:, 10:11], col[:, 13:14], ALU.subtract).then_inc(prep, 1)
                    dve.wait_ge(prep, at_("Bias"))
                    v.tensor_copy(params[:, 0:B, 1], col[:, 14:15].to_broadcast([P, B]))
                    v.tensor_copy(params[:, 0:B, 2], bank(4, B)).then_inc(prep, 1)
                    dve.wait_ge(prep, at_("npsum"))
                    v.tensor_scalar(sm[:, 31, :], sm[:, 21, :], float(NPIX), None, ALU.mult)
                    v.tensor_tensor(diag[:, :, :], ident[0:C, 0:C].unsqueeze(1).to_broadcast([C, B, C]),
                                    sm[0:C, 6, :].unsqueeze(2).to_broadcast([C, B, C]), ALU.mult).then_inc(prep, 1)
                    dve.wait_ge(prep, at_("td"))
                    for d, (edge, sg) in enumerate(((23, 2.0), (23, -2.0), (22, 2.0), (22, -2.0))):
                        last = v.scalar_tensor_tensor(out=td[:, d, :], in0=sm[:, edge, :], scalar=sg,
                                                      in1=sm[:, 31, :], op0=ALU.mult, op1=ALU.add)
                    last.then_inc(prep, 1)
                    dve.wait_ge(prep, at_("pool_copy"))
                    v.tensor_copy(asb[:, :], psum[0:B, 0:C]).then_inc(prep, 1)
                    dve.wait_ge(prep, at_("at"))
                    v.tensor_copy(at[:, :], bank(1, B, C)).then_inc(prep, 1)
                    dve.wait_ge(prep, at_("h0"))
                    v.tensor_copy(soft[:, 0, :], bank(3, C, B)).then_inc(prep, 1)
                    dve.wait_ge(prep, at_("hmax"))
                    v.tensor_tensor(soft[:, 5, :], bank(3, P, B)[:, C:P], soft[:, 0, :], ALU.max).then_inc(prep, 1)
                    dve.wait_ge(prep, at_("l0"))
                    v.tensor_tensor(soft[:, 1, :], soft[:, 0, :], soft[:, 5, :], ALU.subtract)
                    v.tensor_tensor(soft[:, 2, :], bank(3, P, B)[:, C:P], soft[:, 5, :], ALU.subtract).then_inc(prep, 1)
                    dve.wait_ge(prep, at_("esum"))
                    v.tensor_tensor(soft[:, 0, :], soft[:, 3, :], soft[:, 4, :], ALU.add).then_inc(prep, 1)
                    dve.wait_ge(prep, at_("rsum"))
                    v.reciprocal(soft[:, 5, :], soft[:, 0, :]).then_inc(prep, 1)
                    dve.wait_ge(prep, at_("bar"))
                    v.tensor_tensor(soft[:, 1, :], soft[:, 3, :], soft[:, 5, :], ALU.mult)
                    v.tensor_tensor(soft[:, 2, :], soft[:, 4, :], soft[:, 5, :], ALU.mult).then_inc(prep, 1)
                    dve.wait_ge(prep, at_("bart"))
                    v.tensor_copy(bart[:, :], bank(0, B)).then_inc(prep, 1)
                    dve.wait_ge(prep, at_("z"))
                    v.tensor_scalar(sm[:, 13, :], bank(1, B), b1c[:, :], None, ALU.add).then_inc(prep, 1)
                    dve.wait_ge(prep, at_("zb"))
                    v.tensor_tensor(sm[:, 14, :], sm[:, 13, :], bart[:, :], ALU.mult).then_inc(prep, 1)
                    dve.wait_ge(prep, at_("mask"))
                    v.tensor_tensor(mb[:, :, :], bart[:, :].unsqueeze(2).to_broadcast([P, B, NS]),
                                    dmask.unsqueeze(1).to_broadcast([P, B, NS]), ALU.mult).then_inc(prep, 1)
                    dve.wait_ge(prep, at_("w2s"))
                    v.tensor_tensor(w2s[:, :, :], bank(2).rearrange('p (b c) -> p b c', b=B),
                                    w2t[:, 0, :].unsqueeze(1).to_broadcast([P, B, C]), ALU.mult).then_inc(prep, 1)
                    dve.wait_ge(prep, at_("cb"))
                    v.tensor_scalar(sm[:, 15, :], bank(3, B), vec[:, 0:1], None, ALU.add).then_inc(prep, 1)
                    dve.wait_ge(prep, at_("cbr"))
                    v.tensor_tensor(params[:, 0:B, 3], sm[:, 15, :], r, ALU.mult).then_inc(prep, 1)
                    dve.wait_ge(prep, at_("rhs"))
                    for b in range(B):
                        last = v.tensor_tensor(rhs[:, b, :, :], w2s[:, b, :].unsqueeze(1).to_broadcast([P, NS, C]),
                                               mb[:, b, :].unsqueeze(2).to_broadcast([P, NS, C]), ALU.mult)
                    last.then_inc(prep, 1)
                    dve.wait_ge(prep, at_("wall"))
                    mats = psum[:, 0:B * 256].rearrange("p (b d o) -> p b d o", b=B, d=NS)
                    for b in range(B):
                        for half, slot, d in LAYOUT:
                            h = slice(half * C, (half + 1) * C)
                            v.tensor_scalar(wall[h, b, slot * C:(slot + 1) * C], mats[h, b, d, :],
                                            sm[h, 6, b:b + 1], None, ALU.mult)

        ph = ExitStack()
        with ph:
            XT = [sb(ph, f"mix_x{i}", [P, MR + 1, PITCH]) for i in range(2)]
            XC = [sb(ph, f"centred{i}", [P, SC]) for i in range(2)]
            G = [sb(ph, f"gated{i}", [P, SC]) for i in range(2)]
            XO = [sb(ph, f"mix_out{i}", [P, SC]) for i in range(2)]
            SQ = sb(ph, "square", [P, SC])
            one = sb(ph, "one", [P, MR + 1])
            wcur = [sb(ph, f"wcur{i}", [P, P]) for i in range(2)]
            pcur = [sb(ph, f"pcur{i}", [P, 6]) for i in range(2)]
            loaded = [sem(f"mix_loaded{i}") for i in range(2)]
            stored = [sem(f"mix_stored{i}") for i in range(2)]
            one_set = sem("mix_one_set")
            padded, batch_ready, xc_done = sem("mix_padded"), sem("mix_batch_ready"), sem("mix_xc")
            sig_done, conv_done, sq_done = sem("mix_sig"), sem("mix_conv"), sem("mix_sq")
            g_done, h_done, o_done = sem("mix_g"), sem("mix_h"), sem("mix_o")
            NTM = H // MR
            NB = 2 * NTM
            CR = NB
            x1_par = x1.rearrange("b c (r e) w -> (b c) r e w", e=2)

            with nc.Block() as block:
                @block.sync
                def _(sp):
                    with sp.Fori(0, B // 2) as i:
                        for j in range(2):
                            ch = bass.ds((i * 2 + j) * C, C)
                            for t in range(NTM):
                                T0 = j * NTM + t
                                sp.wait_ge(o_done, i * (2 * NB) + CR + 2 * T0 - 2)
                                for half in range(2):
                                    dst = XT[t % 2][half * C:(half + 1) * C, :, 1 - half:1 - half + W]
                                    r0 = t * MR - 1 + half
                                    lo, hi = max(r0, 0), min(r0 + MR + 1, H)
                                    sp.dma_start(dst[:, lo - r0:hi - r0, :], x_rows[ch, lo:hi, :]
                                                 ).then_inc(loaded[t % 2], 16)
                                if t == 0:
                                    sp.dma_start(XT[0][0:C, 0:1, 1:W + 1], x_rows[ch, 0:1, :]).then_inc(loaded[0], 16)
                                if t == NTM - 1:
                                    sp.dma_start(XT[1][C:P, MR:MR + 1, 0:W], x_rows[ch, H - 1:H, :]
                                                 ).then_inc(loaded[1], 16)
                    for k in range(2):
                        sp.wait_ge(stored[k], B * NTM * 32 + 16)

                @block.gpsimd
                def _(pool):
                    nc.gpsimd.memset(one[:, :], 1.0).then_inc(one_set, 1)
                    pool.wait_ge(one_set, 1)
                    with pool.Fori(0, B // 2) as i:
                        for j in range(2):
                            for t in range(NTM):
                                got = (t // 2 + 1) * 32 + (16 if t % 2 == 0 or t == NTM - 1 else 0)
                                pool.wait_ge(loaded[t % 2], i * (2 * (NTM * 16 + 16)) + j * (NTM * 16 + 16) + got)
                                for half, to, of in ((0, 0, 1), (1, W, W - 1)):
                                    h = slice(half * C, (half + 1) * C)
                                    last = nc.gpsimd.tensor_tensor(XT[t % 2][h, :, to], XT[t % 2][h, :, of],
                                                                   one[h, :], ALU.mult)
                                last.then_inc(padded, 1)

                @block.tensor
                def _(pe):
                    with pe.Fori(0, B // 2) as i:
                        for j in range(2):
                            pe.wait_ge(batch_ready, i * 2 + j + 1)
                            for t in range(NTM):
                                pe.wait_ge(padded, i * (2 * NTM) + j * NTM + t + 1)
                                for k in range(2):
                                    n = (j * NTM + t) * 2 + k
                                    pe.wait_ge(h_done, i * (2 * NB) + CR + n - 1)
                                    for m in range(2):
                                        for q in range(4):
                                            for par in range(2):
                                                r0 = 1 - m + par + 2 * (k * SP_ + q * 2)
                                                last = nc.tensor.matmul(bank(k * 4 + q, 512, C, par * C),
                                                                        wcur[j][:, m * C:(m + 1) * C],
                                                                        XT[t % 2][:, r0:r0 + 3:2, m:m + W],
                                                                        start=(m == 0), stop=(m == 1))
                                    last.then_inc(conv_done, 1)

                @block.scalar
                def _(act):
                    act.sem_inc(sq_done, CR)
                    for k in range(2):
                        act.sem_inc(stored[k], 16)
                    with act.Fori(0, B // 2) as i:
                        def gate(n):
                            j, t, k = n // NB, n // 2 % NTM, n % 2
                            if n % NB == 0:
                                act.wait_ge(batch_ready, i * 2 + j + 1)
                            act.wait_ge(padded, i * (2 * NTM) + n // 2 + 1)
                            act.wait_ge(o_done, i * (2 * NB) + CR + n - 1)
                            for half in range(2):
                                h = slice(half * C, (half + 1) * C)
                                r0 = 1 + 2 * k * SP_
                                last = nc.scalar.activation(
                                    XC[k][h, :].rearrange("p (r w) -> p r w", w=W),
                                    XT[t % 2][h, r0:r0 + 2 * SP_ - 1:2, 1 - half:1 - half + W],
                                    ACT.Identity, bias=pcur[j][h, 4:5])
                            last.then_inc(xc_done, 1)
                            act.wait_ge(xc_done, i * (2 * NB) + n + 1)
                            nc.scalar.activation(G[k][:, :], XC[k][:, :], ACT.Sigmoid,
                                                 bias=pcur[j][:, 1:2], scale=pcur[j][:, 0:1]).then_inc(sig_done, 1)

                        gate(0)
                        for n in range(2 * NB):
                            if n + 1 < 2 * NB:
                                gate(n + 1)
                            j, t, k = n // NB, n // 2 % NTM, n % 2
                            act.wait_ge(o_done, i * (2 * NB) + CR + n + 1)
                            y0 = (t * 2 + k) * SP_
                            for par in range(2):
                                act.dma_start(x1_par[bass.ds((i * 2 + j) * C, C), y0:y0 + SP_, par, :],
                                              XO[k][par * C:(par + 1) * C, :].rearrange("p (r w) -> p r w", w=W)
                                              ).then_inc(stored[k], 16)
                            act.wait_ge(sq_done, i * (2 * NB) + CR + n)
                            nc.scalar.activation(SQ[:, :], XO[k][:, :], ACT.Square, bias=pcur[j][:, 4:5],
                                                 accum_out=sqs[:, bass.ds(i * (2 * NB) + n, 1)]).then_inc(sq_done, 1)

                @block.vector
                def _(dve):
                    def take(b, j):
                        nc.vector.tensor_copy(wcur[j][:, :], wall[:, bass.ds(b, 1), :].rearrange("p a k -> p (a k)"))
                        nc.vector.tensor_copy(pcur[j][:, 0:4], params[:, bass.ds(b, 1), :].rearrange("p a k -> p (a k)"))
                        nc.vector.tensor_scalar(pcur[j][:, 4:5],
                                                params[:, bass.ds(b, 1), 2:3].rearrange("p a k -> p (a k)"),
                                                -1.0, None, ALU.mult).then_inc(batch_ready, 1)

                    dve.sem_inc(h_done, CR)
                    dve.sem_inc(o_done, CR)
                    take(0, 0)
                    dve.wait_ge(batch_ready, 1)
                    with dve.Fori(0, B // 2) as i:
                        for j in range(2):
                            for t in range(NTM):
                                for k in range(2):
                                    n = (j * NTM + t) * 2 + k
                                    dve.wait_ge(sig_done, i * (2 * NB) + n + 1)
                                    nc.vector.tensor_tensor(G[k][:, :], XC[k][:, :], G[k][:, :],
                                                            ALU.mult).then_inc(g_done, 1)
                                    dve.wait_ge(conv_done, i * (2 * NB) + n + 1)
                                    dve.wait_ge(g_done, i * (2 * NB) + n + 1)
                                    nc.vector.scalar_tensor_tensor(out=G[k][:, :], in0=psum[:, k * SC:(k + 1) * SC],
                                                                   scalar=pcur[j][:, 3:4], in1=G[k][:, :],
                                                                   op0=ALU.add, op1=ALU.mult).then_inc(h_done, 1)
                                    dve.wait_ge(h_done, i * (2 * NB) + CR + n + 1)
                                    dve.wait_ge(stored[k], i * (NB * 32) + n // 2 * 32 + 16)
                                    dve.wait_ge(sq_done, i * (2 * NB) + CR + n - 1)
                                    nc.vector.scalar_tensor_tensor(out=XO[k][:, :], in0=XC[k][:, :],
                                                                   scalar=pcur[j][:, 2:3], in1=G[k][:, :],
                                                                   op0=ALU.add, op1=ALU.add,
                                                                   accum_out=sums[:, bass.ds(i * (2 * NB) + n, 1)]
                                                                   ).then_inc(o_done, 1)
                                    if t == NTM // 2 and k == 1:
                                        take(i * 2 + j + 1, 1 - j)
                                        dve.wait_ge(batch_ready, i * 2 + j + 2)

        ph = ExitStack()
        with ph:
            T = table(ph, ["group"])
            sv = sb(ph, "norm2_values", [P, 10, B])
            n2_tab, n2 = sem("norm2_table"), sem("norm2_steps")
            with nc.Block() as block:
                @block.sync
                def _(sp):
                    sp.dma_start(*T["group"]).then_inc(n2_tab, 16)

                @block.tensor
                def _(pe):
                    pe.wait_ge(n2_tab, 16)
                    pe.wait_ge(n2, 2)
                    nc.tensor.matmul(bank(0, 2 * B), T["group"][0], sv[:, 2:4, :].rearrange("p a b -> p (a b)"),
                                     start=True, stop=True).then_inc(n2, 1)

                @block.scalar
                def _(act):
                    act.wait_ge(n2, 6)
                    nc.scalar.activation(sv[:, 7, :], sv[:, 6, :], ACT.Sqrt).then_inc(n2, 1)

                @block.vector
                def _(dve):
                    v = nc.vector
                    inv = 1.0 / (HALF * W)
                    v.reduce_sum(sv[:, 0, :], sums[:, :].rearrange("p (b n) -> p b n", b=B), axis=AX_X)
                    v.reduce_sum(sv[:, 1, :], sqs[:, :].rearrange("p (b n) -> p b n", b=B), axis=AX_X).then_inc(n2, 1)
                    dve.wait_ge(n2, 1)
                    v.scalar_tensor_tensor(out=sv[:, 2, :], in0=sv[:, 0, :], scalar=inv, in1=params[:, 0:B, 2],
                                           op0=ALU.mult, op1=ALU.subtract)
                    v.tensor_scalar(sv[:, 3, :], sv[:, 1, :], inv, None, ALU.mult).then_inc(n2, 1)
                    dve.wait_ge(n2, 3)
                    v.tensor_copy(sv[:, 4, :], bank(0, B))
                    v.tensor_tensor(sv[:, 9, :], params[:, 0:B, 2], bank(0, B), ALU.add).then_inc(n2, 1)
                    dve.wait_ge(n2, 4)
                    v.tensor_tensor(sv[:, 5, :], sv[:, 4, :], sv[:, 4, :], ALU.mult).then_inc(n2, 1)
                    dve.wait_ge(n2, 5)
                    v.scalar_tensor_tensor(out=sv[:, 6, :], in0=bank(0, 2 * B)[:, B:], scalar=EPS, in1=sv[:, 5, :],
                                           op0=ALU.add, op1=ALU.subtract).then_inc(n2, 1)
                    dve.wait_ge(n2, 7)
                    v.reciprocal(norm2[:, 0, :], sv[:, 7, :]).then_inc(n2, 1)
                    dve.wait_ge(n2, 8)
                    v.scalar_tensor_tensor(out=norm2[:, 1, :], in0=sv[:, 9, :], scalar=-float(NPIX),
                                           in1=norm2[:, 0, :], op0=ALU.mult, op1=ALU.mult)

        ph = ExitStack()
        with ph:
            T = table(ph, ["ident", "frow", "fcol"])
            ident = T["ident"][0]
            frow = T["frow"][0].rearrange("p (a m) -> p a m", a=2)
            fcol = T["fcol"][0].rearrange("p (a k m) -> p a k m", a=2, k=2)
            XW = [sb(ph, f"fwd_x{i}", [P, 2, CG, W]) for i in range(2)]
            RS = [sb(ph, f"fwd_rows{i}", [2 * NM, 512]) for i in range(2)]
            A = [sb(ph, f"fwd_cols{i}", [P, 2, 2 * NM, C]) for i in range(2)]
            XB = sb(ph, "fwd_modes", [C, 3, KX, M2])
            ncur = [sb(ph, f"ncur{i}", [P, 2]) for i in range(2)]
            tab, loaded = sem("fwd_tables"), [sem(f"fwd_loaded{i}") for i in range(2)]
            row_done, row_out, tr_done, tr_out = (sem("fwd_" + n) for n in ("row", "row_out", "tr", "tr_out"))
            col_done, col_act, col_dve = (sem("fwd_" + n) for n in ("col", "col_act", "col_dve"))
            cur, neg_done, modes_stored, modes_free = (sem("fwd_" + n) for n in ("cur", "neg", "stored", "free"))
            NR = C // 2
            with nc.Block() as block:
                @block.sync
                def _(sp):
                    for n in ("ident", "frow", "fcol"):
                        sp.dma_start(*T[n]).then_inc(tab, 16)
                    with sp.Fori(0, B // 2) as i:
                        for j in range(2):
                            for g in range(NG):
                                G0 = j * NG + g
                                sp.wait_ge(row_done, i * (2 * NR) + 4 * G0 + 4)
                                for a in range(2):
                                    sp.dma_start(XW[g % 2][:, a, :, :],
                                                 x1_rows[a * P:(a + 1) * P, bass.ds((i * 2 + j) * C + g * CG, CG), :]
                                                 ).then_inc(loaded[g % 2], 16)

                @block.tensor
                def _(pe):
                    pe.sem_inc(row_done, 8)
                    pe.sem_inc(tr_done, 2)
                    pe.sem_inc(col_done, 10)
                    pe.wait_ge(tab, 48)
                    with pe.Fori(0, B // 2) as i:
                        def rows(n):
                            j, g, cp = n // NR, n // 4 % NG, n % 4
                            if cp == 0:
                                pe.wait_ge(loaded[g % 2], i * (NG * 32) + (j * (NG // 2) + g // 2 + 1) * 32)
                            pe.wait_ge(row_out, i * (2 * NR) + n + 1)
                            for a in range(2):
                                last = nc.tensor.matmul(bank(n % 2, 512, 2 * NM), frow[:, a, :],
                                                        XW[g % 2][:, a, 2 * cp:2 * cp + 2, :],
                                                        start=(a == 0), stop=(a == 1))
                            last.then_inc(row_done, 1)

                        def transposes(n):
                            pe.wait_ge(row_out, i * (2 * NR) + 2 + n + 1)
                            pe.wait_ge(tr_out, i * (2 * NR) + n + 1)
                            for q in range(4):
                                last = nc.tensor.transpose(psum[:, (2 + n % 2) * 512 + q * 2 * NM:
                                                                (2 + n % 2) * 512 + (q + 1) * 2 * NM],
                                                           RS[n % 2][:, q * P:(q + 1) * P],
                                                           ident[0:2 * NM, 0:2 * NM])
                            last.then_inc(tr_done, 1)

                        for j in range(2):
                            rows(j * NR)
                            for n in range(j * NR, (j + 1) * NR):
                                if n + 1 < (j + 1) * NR:
                                    rows(n + 1)
                                transposes(n)
                            pe.wait_ge(tr_out, i * (2 * NR) + 2 + (j + 1) * NR)
                            for m in range(5):
                                if m < 4:
                                    pe.wait_ge(col_act, i * 4 + j * 2 + 1)
                                    pe.wait_ge(col_dve, i * 6 + j * 3 + 1)
                                else:
                                    pe.wait_ge(col_act, i * 4 + j * 2 + 2)
                                for p in range(4 * m, min(4 * m + 4, 17)):
                                    wide = 2 if p < 16 else 1
                                    o = psum[0:wide * C, (4 + m % 4) * 512 + p % 4 * P:(4 + m % 4) * 512 + (p % 4 + 1) * P]
                                    for q in range(4):
                                        a, k = q // 2, q % 2
                                        mode = k * NM + 2 * p
                                        last = nc.tensor.matmul(
                                            o, A[j][:, a, mode:mode + wide, :].rearrange("p m c -> p (m c)"),
                                            fcol[:, a, k, :], start=(q == 0), stop=(q == 3))
                                last.then_inc(col_done, 1)

                def col_copies(m):
                    if m == 4:
                        return [(0, 0, 1, 1, 63)]
                    got = []
                    for par in range(2):
                        k = 8 * m + par
                        got.append((par, 0, 4, 0, k))
                        if k == 0:
                            got.append((par, 1, 3, 1, 31 + 2))
                        else:
                            got.append((par, 0, 4, 1, 31 + k))
                    return got

                def col_views(m, par, first, count, sign, pos):
                    src = psum[par * C:(par + 1) * C, (4 + m % 4) * 512:(5 + m % 4) * 512] \
                        .rearrange("p (s g r k) -> p s g r k", s=4, g=2, r=2)[:, first:first + count, sign, :, :]
                    dst = XB[:, 0:2, pos:pos + 2 * count - 1:2, :].rearrange("p r s k -> p s r k")
                    return dst, src

                @block.scalar
                def _(act):
                    act.sem_inc(row_out, 2)
                    act.sem_inc(col_act, 1)
                    with act.Fori(0, B // 2) as i:
                        for j in range(2):
                            for n in range(j * NR, (j + 1) * NR):
                                act.wait_ge(row_done, i * (2 * NR) + 8 + n + 1)
                                act.wait_ge(tr_done, i * (2 * NR) + n + 1)
                                nc.scalar.activation(RS[n % 2][:, :], bank(n % 2, 512, 2 * NM),
                                                     ACT.Copy).then_inc(row_out, 1)
                            act.wait_ge(cur, i * 2 + j + 1)
                            act.wait_ge(modes_free, i * 2 + j + 1)
                            for m in (0, 2):
                                act.wait_ge(col_done, i * 10 + j * 5 + 10 + m + 1)
                                for par, first, count, sign, pos in col_copies(m):
                                    dst, src = col_views(m, par, first, count, sign, pos)
                                    last = nc.scalar.activation(dst, src, ACT.Copy,
                                                                scale=ncur[j][par * C:(par + 1) * C, 0:1])
                                last.then_inc(col_act, 1)

                @block.vector
                def _(dve):
                    dve.sem_inc(tr_out, 2)
                    dve.sem_inc(col_dve, 1)
                    with dve.Fori(0, B // 2) as i:
                        for j in range(2):
                            dve.wait_ge(col_done, i * 10 + j * 5 + 5)
                            dve.wait_ge(col_act, i * 4 + 1)
                            nc.vector.tensor_copy(ncur[j][:, :], norm2[:, :, bass.ds(i * 2 + j, 1)]
                                                  .rearrange("p a b -> p (a b)")).then_inc(cur, 1)
                            for n in range(j * NR, (j + 1) * NR):
                                c0 = n % NR * 2
                                dve.wait_ge(tr_done, i * (2 * NR) + 2 + n + 1)
                                src = psum[:, (2 + n % 2) * 512:(2 + n % 2) * 512 + 8 * NM] \
                                    .rearrange("p (c a m) -> p c a m", c=2, a=2)
                                nc.vector.tensor_copy(A[j][:, :, :, c0:c0 + 2].rearrange("p a m c -> p c a m"),
                                                      src).then_inc(tr_out, 1)
                            dve.wait_ge(cur, i * 2 + j + 1)
                            dve.wait_ge(modes_free, i * 2 + j + 1)
                            for m in (1, 3, 4):
                                dve.wait_ge(col_done, i * 10 + j * 5 + 10 + m + 1)
                                for par, first, count, sign, pos in col_copies(m):
                                    dst, src = col_views(m, par, first, count, sign, pos)
                                    last = nc.vector.tensor_scalar(dst, src, ncur[j][par * C:(par + 1) * C, 0:1],
                                                                   None, ALU.mult)
                                last.then_inc(col_dve, 1)
                            dve.wait_ge(col_act, i * 4 + j * 2 + 3)
                            dve.wait_ge(col_dve, i * 6 + j * 3 + 4)
                            nc.vector.tensor_tensor(XB[:, 0, 0, 0:1], XB[:, 0, 0, 0:1], ncur[j][0:C, 1:2], ALU.add)
                            nc.vector.tensor_scalar(XB[:, 2, :, :], XB[:, 1, :, :], -1.0, None,
                                                    ALU.mult).then_inc(neg_done, 1)

                @block.gpsimd
                def _(pool):
                    pool.sem_inc(modes_free, 1)
                    with pool.Fori(0, B // 2) as i:
                        for j in range(2):
                            pool.wait_ge(neg_done, i * 2 + j + 1)
                            b = i * 2 + j
                            for p0, r, q, w in ((0, 0, 0, 2), (C, 0, 2, 1), (C, 1, 0, 1)):
                                pool.dma_start(
                                    xd[p0:p0 + C, bass.ds(b, 1), r:r + w, :, :].rearrange("p b r k m -> p (b r k m)"),
                                    XB[:, q:q + w, :, :].rearrange("p r k m -> p (r k m)")).then_inc(modes_stored, 16)
                            pool.wait_ge(modes_stored, i * 96 + j * 48 + 48)
                            pool.sem_inc(modes_free, 1)
                    pool.wait_ge(modes_stored, B * 48)

        ph = ExitStack()
        with ph:
            WT = [sb(ph, f"mode_w{i}", [P, C, P]) for i in range(2)]
            XM = [sb(ph, f"mode_x{i}", [P, 2 * B, P]) for i in range(2)]
            YS = [sb(ph, f"mode_y{i}", [P, M2 * C]) for i in range(2)]
            loaded = [sem(f"mode_loaded{i}") for i in range(2)]
            stored = [sem(f"mode_stored{i}") for i in range(2)]
            mixed, out_act, out_dve, zero = sem("mode_mixed"), sem("mode_out_act"), sem("mode_out_dve"), sem("mode_zero")
            views = [[a.rearrange("i o x y -> i o (x y)") for a in pair] for pair in ((wr1, wi1), (wr2, wi2))]
            xm = xd.rearrange("p b r k m -> p (b r) (k m)")
            with nc.Block() as block:
                @block.sync
                def _(sp):
                    for s in range(2):
                        with sp.Fori(0, 4) as i:
                            for j in range(2):
                                sp.wait_ge(mixed, (i * 2 + j) + 8 * s + 1)
                                cw = i * 2 + j
                                for q in range(2):
                                    sp.dma_start(WT[j][q * C:(q + 1) * C, :, :],
                                                 views[s][q][:, :, bass.ds(cw * P, P)]).then_inc(loaded[j], 16)
                                pos = cw * P if s == 0 else cw * (-P) + (KX - 4) * M2
                                sp.dma_start(XM[j][:, :, :], xm[:, :, bass.ds(pos, P)]).then_inc(loaded[j], 16)

                @block.tensor
                def _(pe):
                    pe.sem_inc(mixed, 2)
                    pe.wait_ge(zero, 1)
                    for s in range(2):
                        with pe.Fori(0, 4) as i:
                            for j in range(2):
                                pe.wait_ge(loaded[j], i * 48 + 48 * (4 * s + 1))
                                pe.wait_ge(out_act, i * 2 + j + 8 * s + 1)
                                pe.wait_ge(out_dve, i * 2 + j + 8 * s + 1)
                                for ky in range(M2):
                                    for k in range(4):
                                        kx = k if s == 0 else 3 - k
                                        at = j * 2048 + ky * C
                                        last = nc.tensor.matmul(psum[32 * k:32 * k + 2 * B, at:at + C],
                                                                XM[j][:, :, kx * M2 + ky],
                                                                WT[j][:, :, k * M2 + ky], start=True, stop=True)
                                last.then_inc(mixed, 1)

                @block.scalar
                def _(act):
                    act.sem_inc(out_act, 2)
                    for j in range(2):
                        act.sem_inc(stored[j], 16)
                    for s in range(2):
                        with act.Fori(0, 4) as i:
                            for j in range(2):
                                act.wait_ge(mixed, i * 2 + j + 8 * s + 3)
                                act.wait_ge(stored[j], i * 64 + 256 * s + 16)
                                nc.scalar.activation(YS[j][:, 0:1024], psum[:, j * 2048:j * 2048 + 1024],
                                                     ACT.Copy).then_inc(out_act, 1)
                                act.wait_ge(out_act, i * 2 + j + 8 * s + 3)
                                act.wait_ge(out_dve, i * 2 + j + 8 * s + 3)
                                for k in range(4):
                                    act.dma_start(yd[:, bass.ds((i * 2 + j) * 4 + 32 * s + k, 1), :, :]
                                                  .rearrange("q k m c -> q (k m c)"),
                                                  YS[j][32 * k:32 * k + 2 * B, :]).then_inc(stored[j], 16)
                    for j in range(2):
                        act.wait_ge(stored[j], 8 * 64 + 16)

                @block.vector
                def _(dve):
                    dve.sem_inc(out_dve, 2)
                    nc.vector.memset(psum[:, :], 0.0).then_inc(zero, 1)
                    for s in range(2):
                        with dve.Fori(0, 4) as i:
                            for j in range(2):
                                dve.wait_ge(mixed, i * 2 + j + 8 * s + 3)
                                dve.wait_ge(stored[j], i * 64 + 256 * s + 16)
                                nc.vector.tensor_copy(YS[j][:, 1024:2048], psum[:, j * 2048 + 1024:j * 2048 + 2048]
                                                      ).then_inc(out_dve, 1)

        ph = ExitStack()
        with ph:
            T = table(ph, ["irow", "icol", "sign"])
            irow, icol, sign = (T[n][0] for n in ("irow", "icol", "sign"))
            NX = 4
            XW = [sb(ph, f"inv_x{i}", [P, 2, CG, W]) for i in range(NX)]
            YA = sb(ph, "inv_ya", [P, M2, C])
            YB = sb(ph, "inv_yb", [P, M2, C])
            YY = [sb(ph, f"inv_yy{i}", [P, C, 2, M2]) for i in range(2)]
            TS = [sb(ph, f"inv_t{i}", [P, W]) for i in range(2)]
            tab, y_loaded = sem("inv_tables"), sem("inv_y_loaded")
            loaded = [sem(f"inv_loaded{i}") for i in range(NX)]
            stored = [sem(f"inv_stored{i}") for i in range(NX)]
            x_free = sem("inv_x_free")
            y_ready, row_done, row_out, col_done, added = (sem("inv_" + n) for n in ("y", "row", "row_out", "col", "added"))
            NR = C // 2
            out_rows_ = out_rows
            with nc.Block() as block:
                @block.sync
                def _(sp):
                    for n in ("irow", "icol", "sign"):
                        sp.dma_start(*T[n]).then_inc(tab, 16)
                    with sp.Fori(0, B // 2) as i:
                        for j in range(2):
                            b = i * 2 + j
                            sp.wait_ge(y_ready, b + 1)
                            for n, dst in enumerate((YA, YB)):
                                for half in range(2):
                                    q = half if n == 0 else 1 - half
                                    sp.dma_start(dst[half * C:(half + 1) * C, :, :],
                                                 yd[bass.ds(b * 2 + q, 1), :, :, :].rearrange("q k m c -> (q k) m c")
                                                 ).then_inc(y_loaded, 16)
                            for g in range(NG):
                                G0 = j * NG + g
                                sp.wait_ge(x_free, i * (2 * NG) + G0 + 1)
                                for a in range(2):
                                    sp.dma_start(XW[g % NX][:, a, :, :],
                                                 x1_rows[a * P:(a + 1) * P, bass.ds(b * C + g * CG, CG), :]
                                                 ).then_inc(loaded[g % NX], 16)

                @block.tensor
                def _(pe):
                    pe.sem_inc(row_done, 2 * NR)
                    pe.sem_inc(col_done, 2)
                    pe.wait_ge(tab, 48)
                    with pe.Fori(0, B // 2) as i:
                        def rows(n):
                            j, o = n // NR, n % NR * 2
                            if n % NR == 0:
                                pe.wait_ge(y_ready, i * 2 + j + 2)
                            pe.wait_ge(row_out, i * (2 * NR) + n + 1)
                            nc.tensor.matmul(bank(6 + n % 2, W),
                                             YY[j][:, o:o + 2, :, :].rearrange("p o r k -> p (o r k)"),
                                             irow, start=True, stop=True).then_inc(row_done, 1)

                        def cols(n):
                            pe.wait_ge(row_out, i * (2 * NR) + 2 + n + 1)
                            pe.wait_ge(added, i * (2 * NR) + n + 1)
                            for a in range(2):
                                last = nc.tensor.matmul(bank(n % 2 * 2 + a), TS[n % 2][:, a * P:(a + 1) * P], icol,
                                                        start=True, stop=True)
                            last.then_inc(col_done, 1)

                        rows(0)
                        for n in range(2 * NR):
                            if n + 1 < 2 * NR:
                                rows(n + 1)
                            cols(n)

                @block.scalar
                def _(act):
                    act.sem_inc(row_out, 2)
                    act.sem_inc(y_ready, 1)
                    act.wait_ge(tab, 48)
                    with act.Fori(0, B // 2) as i:
                        for j in range(2):
                            act.wait_ge(y_loaded, (i * 2 + j) * 64 + 64)
                            act.wait_ge(row_done, i * (2 * NR) + j * NR + NR)
                            nc.scalar.activation(YY[j][:, :, 0, :], YA[:, :, :].rearrange("p k c -> p c k"), ACT.Copy)
                            nc.scalar.activation(YY[j][:, :, 1, :], YB[:, :, :].rearrange("p k c -> p c k"), ACT.Copy,
                                                 scale=sign[:, 0:1]).then_inc(y_ready, 1)
                            for n in range(j * NR, (j + 1) * NR):
                                act.wait_ge(row_done, i * (2 * NR) + 2 * NR + n + 1)
                                act.wait_ge(col_done, i * (2 * NR) + n + 1)
                                nc.scalar.activation(TS[n % 2][:, :], bank(6 + n % 2, W), ACT.Copy).then_inc(row_out, 1)

                @block.vector
                def _(dve):
                    dve.sem_inc(added, 2)
                    with dve.Fori(0, B // 2) as i:
                        for n in range(2 * NR):
                            G0, cp = n // 4, n % 4
                            xw = XW[G0 % NX][:, :, 2 * cp:2 * cp + 2, :].rearrange("p a c w -> p a (c w)")
                            if cp == 0:
                                dve.wait_ge(loaded[G0 % NX], i * (2 * NG // NX * 32) + G0 // NX * 32 + 32)
                            dve.wait_ge(col_done, i * (2 * NR) + 2 + n + 1)
                            nc.vector.tensor_tensor(xw, xw, psum[:, n % 2 * 1024:n % 2 * 1024 + 1024]
                                                    .rearrange("p (a k) -> p a k", a=2), ALU.add).then_inc(added, 1)

                @block.gpsimd
                def _(pool):
                    pool.sem_inc(x_free, NX)
                    with pool.Fori(0, B // 2) as i:
                        for G0 in range(2 * NG + 1):
                            if G0 < 2 * NG:
                                pool.wait_ge(added, i * (2 * NR) + 2 + 4 * (G0 + 1))
                                for a in range(2):
                                    pool.dma_start(out_rows[a * P:(a + 1) * P, bass.ds(i * 2 * C + G0 * CG, CG), :],
                                                   XW[G0 % NX][:, a, :, :]).then_inc(stored[G0 % NX], 16)
                            if G0 >= 1:
                                G1 = G0 - 1
                                pool.wait_ge(stored[G1 % NX], i * (2 * NG // NX * 32) + (G1 // NX + 1) * 32)
                                pool.sem_inc(x_free, 1)
                    for q in range(NX):
                        pool.wait_ge(stored[q], B * NG // NX * 32)


_INS = ["x", "L0_conv_mlp1_w", "L0_conv_mlp1_b", "L0_conv_mlp2_w", "L0_conv_mlp2_b", "L0_conv_sa1_w",
        "L0_conv_sa2_w", "L0_conv_bn_gamma", "L0_conv_bn_beta", "L1_conv_w1_real", "L1_conv_w1_imag",
        "L1_conv_w2_real", "L1_conv_w2_imag"]


def kernel(**inputs):
    import numpy as _np
    import concourse.bacc as _bacc
    from concourse.bass_utils import run_bass_kernel_spmd as _run

    nc = _bacc.Bacc("TRN2", target_bir_lowering=False, num_devices=1)
    arrays, args = {}, []
    for name in _INS:
        a = _np.ascontiguousarray(inputs[name])
        arrays[name] = a
        args.append(nc.dram_tensor(name, a.shape, F32, kind="ExternalInput").ap())
    arrays["tables"] = CONST
    args.append(nc.dram_tensor("tables", CONST.shape, F32, kind="ExternalInput").ap())
    args.append(nc.dram_tensor("out", (B, C, H, W), F32, kind="ExternalOutput").ap())
    program(nc, *args)
    r = _run(nc, [arrays], core_ids=[0])
    return r.results[0]["out"]
```

```python
from contextlib import ExitStack

import concourse.bass as bass
from concourse import mybir
import numpy as np

F32 = mybir.dt.float32
ACT = mybir.ActivationFunctionType
ALU = mybir.AluOpType
AX_X = mybir.AxisListType.X

P = 128
B, C, H, W = 8, 64, 256, 256
M1, M2 = 32, 32
NPIX = H * W
EPS = 1e-5
HALF = H // 2
NS = 4
DIRS = ((0, 1, 2, 3), (2, 3, 0, 1))

TR = 16
NT = HALF // TR
SP_ = 8
SC = SP_ * W
MR = 2 * SP_
LAYOUT = ((0, 0, 2), (1, 0, 1), (0, 1, 0), (1, 1, 3))
PITCH = W + 1
NM = M1 + 1
NP = (NM + 1) // 2
KX = 2 * M1
CG = 8
NG = C // CG
RK = KX * M2

OFF = {}


def constants():
    parts = []

    def put(name, a):
        a = np.asarray(a, np.float64)
        full = np.zeros((P, a.shape[1]))
        full[: a.shape[0]] = a
        OFF[name] = (sum(q.shape[1] for q in parts), a.shape[1])
        parts.append(full)

    p = np.arange(P)
    c = p % C
    put("ident", np.eye(P))
    put("group", 0.25 * (c[:, None] // 2 == c[None, :] // 2))
    put("chan", 0.5 * (c[:, None] == c[None, :]))
    put("halfones", np.full((P, P), 0.5))
    put("ones", np.ones((P, P)))
    dmask = np.zeros((P, NS))
    for branch in range(2):
        for q in range(4):
            dmask[branch * C + q * 16: branch * C + (q + 1) * 16, DIRS[branch][q]] = 1
    put("dmask", dmask)
    put("rowsel", np.stack([1.0 * (p < C), -1.0 * (p >= C)], 1))
    put("sign", np.stack([np.where(p < C, 1.0, -1.0)] * 2, 1))
    put("npix", np.full((1, B), float(NPIX)))
    th = 2 * np.pi / H
    row = np.arange(H)
    frow = np.zeros((P, 2, C))
    for par in range(2):
        k = np.arange(par, NM, 2)
        a = th * np.outer(np.arange(P), k)
        frow[:, par, :len(k)] = np.cos(a)
        frow[:, par, NP:NP + len(k)] = np.sin(a)
    put("frow", frow.reshape(P, -1))
    col = np.arange(W)
    a = 2 * np.pi / W * np.outer(col, np.arange(M2))
    cc, ss = np.cos(a), np.sin(a)
    fc = np.concatenate([cc, -ss, cc, -ss], 1)
    fs = np.concatenate([-ss, -cc, ss, cc], 1)
    fcol = np.stack([fc, fs], 1).reshape(2, P, 2, 4 * M2).transpose(1, 0, 2, 3)
    put("fcol", fcol.reshape(P, -1))
    kx = np.concatenate([np.arange(M1), np.arange(-M1, 0)])
    ar = th * np.outer(kx, row)
    put("irow", np.concatenate([np.cos(ar), -np.sin(ar)], 0))
    wt = np.where(np.arange(M2) == 0, 1.0, 2.0)[:, None] / NPIX
    ac = 2 * np.pi / W * np.outer(np.arange(M2), col)
    ih = np.concatenate([wt * np.cos(ac), -wt * np.sin(ac)], 0)
    put("icol", np.block([[ih, np.zeros_like(ih)], [np.zeros_like(ih), ih]]))
    return np.concatenate(parts, 1).astype(np.float32)


CONST = constants()


def program(nc, x, w1m, b1m, w2m, b2m, sa1, sa2, gamma, beta, wr1, wi1, wr2, wi2, const, out):
    top = ExitStack()
    with top:
        def sem(name):
            return top.enter_context(nc.semaphore(name))

        x1 = nc.dram_tensor("x1_scratch", (B, C, H, W), F32, kind="Internal").ap()
        xd = nc.dram_tensor("modes_in", (P, B, 2, KX, M2), F32, kind="Internal").ap()
        yd = nc.dram_tensor("modes_out", (2 * B, KX, M2, C), F32, kind="Internal").ap()
        x_bc = x.rearrange("b c h w -> (b c) (h w)")
        x_rows = x.rearrange("b c h w -> (b c) h w")
        x1_bc = x1.rearrange("b c h w -> (b c) (h w)")
        x1_rows = x1.rearrange("b c h w -> h (b c) w")
        out_rows = out.rearrange("b c h w -> h (b c) w")

        psum = top.enter_context(nc.psum_tensor("psum", [P, 4096], F32))

        def bank(n, cols=512, parts=P, first=0):
            return psum[first:first + parts, n * 512:n * 512 + cols]

        def sb(ctx, name, shape):
            return ctx.enter_context(nc.sbuf_tensor(name, shape, F32))

        def table(ctx, names):
            t = sb(ctx, "tab_" + "_".join(names), [P, sum(OFF[n][1] for n in names)])
            at, got = 0, {}
            for n in names:
                o, k = OFF[n]
                got[n] = (t[:, at:at + k], const[:, o:o + k])
                at += k
            return got

        params = sb(top, "params", [P, B + 1, 4])
        wall = sb(top, "wall", [P, B + 1, P])
        sums = sb(top, "sums", [P, B * 2 * NT])
        sqs = sb(top, "sqs", [P, B * 2 * NT])
        norm2 = sb(top, "norm2", [P, 2, B])
        means = sb(top, "means", [P, B])

        ph = ExitStack()
        with ph:
            XT = [sb(ph, f"stat_x{i}", [P, TR * W]) for i in range(2)]
            stats = sb(ph, "stats", [P, B * NT * 8 * 6])
            mv = sb(ph, "mv", [P, B, 2])
            ecol = sb(ph, "ecol", [P, B * NT * 2])
            erow = sb(ph, "erow", [P, B * 2])
            junk = sb(ph, "junk", [P, W])
            names = ["ident", "group", "chan", "halfones", "ones", "dmask", "rowsel", "npix"]
            T = table(ph, names)
            ident, group, chan, halfones, ones, dmask, rowsel, npix = (T[n][0] for n in names)
            w1d = sb(ph, "w1d", [P, 2, C])
            w2d = sb(ph, "w2d", [C, 2, C])
            sa1s = sb(ph, "sa1s", [C, C])
            sa2s = sb(ph, "sa2s", [P, C])
            b1c = sb(ph, "b1c", [P, 1])
            b1r = sb(ph, "b1r", [1, P])
            vec = sb(ph, "vec", [P, 3])
            w1t = sb(ph, "w1t", [C, P])
            w2t = sb(ph, "w2t", [P, 2, C])
            sa1t = sb(ph, "sa1t", [C, C])
            sa2t = sb(ph, "sa2t", [C, P])
            sm = sb(ph, "sm", [P, 32, B])
            col = sb(ph, "col", [P, 16])
            td = sb(ph, "td", [P, NS, B])
            asb = sb(ph, "asb", [B, C])
            at = sb(ph, "at", [C, B])
            gt = sb(ph, "gt", [C, B])
            soft = sb(ph, "soft", [B, 6, C])
            bart = sb(ph, "bart", [P, B])
            diag = sb(ph, "diag", [C, B, C])
            w2s = sb(ph, "w2s", [P, B, C])
            mb = sb(ph, "mb", [P, B, NS])
            rhs = sb(ph, "rhs", [P, B, NS, C])

            s_x = [sem(f"stat_loaded{i}") for i in range(2)]
            stat_dve, stat_act = sem("stat_dve_done"), sem("stat_act_done")
            edge_order = sem("edge_order")
            weights = sem("weights_loaded")

            with nc.Block() as block:
                @block.sync
                def _(sp):
                    with sp.Fori(0, B) as b:
                        for t in range(NT):
                            sp.wait_ge(stat_dve, b * NT + t + 1)
                            sp.wait_ge(stat_act, b * NT + t + 1)
                            for s in range(2):
                                r0 = (s * HALF + t * TR) * W
                                sp.dma_start(XT[t % 2][s * C:(s + 1) * C, :],
                                             x_bc[bass.ds(b * C, C), r0:r0 + TR * W]
                                             ).then_inc(s_x[t % 2], 16)

                @block.gpsimd
                def _(pool):
                    for n in names:
                        pool.dma_start(T[n][0], T[n][1]).then_inc(weights, 16)
                    for j in range(2):
                        pool.dma_start(w1d[:, j, :], w1m[0:P, :]).then_inc(weights, 16)
                        pool.dma_start(w2d[:, j, :], w2m).then_inc(weights, 16)
                        for n, v in enumerate((b2m, gamma, beta)):
                            pool.dma_start(vec[j * C:(j + 1) * C, n:n + 1],
                                           v.rearrange("(p a) -> p a", a=1)).then_inc(weights, 16)
                    pool.dma_start(sa1s[:, :], sa1).then_inc(weights, 16)
                    pool.dma_start(sa2s[:, :], sa2).then_inc(weights, 16)
                    pool.dma_start(b1c[:, :], b1m[0:P].rearrange("(p a) -> p a", a=1)).then_inc(weights, 16)
                    pool.dma_start(b1r[:, :], b1m[0:P].rearrange("(a p) -> a p", a=1)).then_inc(weights, 16)
                    pool.memset(wall[:, B, :], 0.0)
                    pool.memset(params[:, B, :], 0.0)
                    pool.wait_ge(weights, 16 * (len(names) + 14))

                @block.scalar
                def _(act):
                    act.sem_inc(stat_act, 2)
                    act.sem_inc(edge_order, 1)
                    with act.Fori(0, B) as b:
                        k = 0
                        for t in range(NT):
                            act.wait_ge(s_x[t % 2], b * (NT // 2 * 32) + (t // 2 + 1) * 32)
                            xt = XT[t % 2][:, :].rearrange("p (r w) -> p r w", w=W)
                            todo = [(xt[:, :, 0], ecol, b * (NT * 2) + t * 2, TR),
                                    (xt[:, :, W - 1], ecol, b * (NT * 2) + t * 2 + 1, TR)]
                            if t == 0:
                                todo.append((xt[:, 0, :], erow, b * 2, W))
                            if t == NT - 1:
                                todo.append((xt[:, TR - 1, :], erow, b * 2 + 1, W))
                            for src, dst, idx, width in todo:
                                act.wait_ge(edge_order, b * (NT * 2 + 2) + k + 1)
                                act.activation(junk[:, 0:width], src, ACT.Copy,
                                               accum_out=dst[:, bass.ds(idx, 1)]).then_inc(edge_order, 1)
                                k += 1
                            act.wait_ge(edge_order, b * (NT * 2 + 2) + k + 1)
                            act.sem_inc(stat_act, 1)

                @block.vector
                def _(dve):
                    dve.sem_inc(stat_dve, 2)
                    with dve.Fori(0, B) as b:
                        for t in range(NT):
                            dve.wait_ge(s_x[t % 2], b * (NT // 2 * 32) + (t // 2 + 1) * 32)
                            for q in range(8):
                                last = nc.vector.bn_stats(stats[:, bass.ds(b * (NT * 48) + (t * 8 + q) * 6, 6)],
                                                          XT[t % 2][:, q * 512:(q + 1) * 512])
                            last.then_inc(stat_dve, 1)
                    dve.wait_ge(stat_dve, 2 + B * NT)
                    for b in range(B):
                        nc.vector.bn_aggr(mv[:, b, :], stats[:, b * NT * 48:(b + 1) * NT * 48])

            STEPS = ("transposes", "evac_w", "group_mean", "dev", "dev2", "devar", "group_var", "veps",
                     "std", "rstd", "nmean", "edges", "cdiff", "rsel", "rdiff", "cdiffr",
                     "rdiffr", "chan_sums", "cs_copy", "bmean", "bmean8", "var_r", "dev_c", "var_rr", "dev_c2",
                     "bvar", "bsum", "absg1", "absg2", "bn_sums", "bveps", "bstd", "brstd", "wbn", "gwbn",
                     "kscale", "A", "mr", "mrb", "Bneg", "Bias", "npsum", "td", "pooled", "pool_copy", "pool_t",
                     "at", "squeeze", "gelu", "excite", "h0", "hmax", "l0", "exps", "esum", "rsum", "bar",
                     "bar_t", "bart", "shift_in", "z", "zb", "mask", "w2s", "shift_out", "cb", "cbr", "rhs",
                     "mats", "wall")

            def at_(name):
                return STEPS.index(name)

            prep = sem("prep")
            r, nmean, mr = sm[:, 6, :], sm[:, 8, :], sm[:, 11, :]
            k1 = col[:, 12:13]
            mean, var = mv[:, :, 0], mv[:, :, 1]
            with nc.Block() as block:
                @block.tensor
                def _(pe):
                    nc.tensor.transpose(bank(0, P, C), w1d[:, 0, :], ident)
                    nc.tensor.transpose(bank(1, C), w2d[:, :, :].rearrange("p a c -> p (a c)"), ident[0:C, 0:C])
                    nc.tensor.transpose(bank(2, C, C), sa1s[:, :], ident[0:C, 0:C])
                    nc.tensor.transpose(bank(3, P, C), sa2s[:, :], ident).then_inc(prep, 1)
                    pe.wait_ge(prep, at_("group_mean"))
                    nc.tensor.matmul(bank(4, B), group, sm[:, 0, :], start=True, stop=True).then_inc(prep, 1)
                    pe.wait_ge(prep, at_("group_var"))
                    nc.tensor.matmul(bank(5, B), group, sm[:, 3, :], start=True, stop=True).then_inc(prep, 1)
                    pe.wait_ge(prep, at_("chan_sums"))
                    nc.tensor.matmul(bank(6, 3 * B), chan, sm[:, 8:11, :].rearrange("p a b -> p (a b)"),
                                     start=True, stop=True).then_inc(prep, 1)
                    pe.wait_ge(prep, at_("bn_sums"))
                    nc.tensor.matmul(psum[:, 3584:3585], chan, col[:, 4:5], start=True, stop=True)
                    nc.tensor.matmul(psum[:, 3585:3586], halfones, col[:, 6:7], start=True,
                                     stop=True).then_inc(prep, 1)
                    pe.wait_ge(prep, at_("pooled"))
                    for q in range(4):
                        j = slice(q * 16, q * 16 + 16)
                        k = slice(C + q * 16, C + q * 16 + 16)
                        o = psum[0:B, j]
                        nc.tensor.matmul(o, td[0:C, DIRS[0][q], :], w1t[:, j], start=True, stop=False)
                        nc.tensor.matmul(o, td[0:C, DIRS[1][q], :], w1t[:, k], start=False, stop=False)
                        nc.tensor.matmul(o, npix[0:1, :], b1r[:, j], start=False, stop=False)
                        last = nc.tensor.matmul(o, npix[0:1, :], b1r[:, k], start=False, stop=True)
                    last.then_inc(prep, 1)
                    pe.wait_ge(prep, at_("pool_t"))
                    nc.tensor.transpose(bank(1, B, C), asb[:, :], ident[0:B, 0:B]).then_inc(prep, 1)
                    pe.wait_ge(prep, at_("squeeze"))
                    nc.tensor.matmul(bank(2, B, C), sa1t[:, :], at[:, :], start=True, stop=True).then_inc(prep, 1)
                    pe.wait_ge(prep, at_("excite"))
                    nc.tensor.matmul(bank(3, P, B), gt[:, :], sa2t[:, :], start=True, stop=True).then_inc(prep, 1)
                    pe.wait_ge(prep, at_("bar_t"))
                    nc.tensor.transpose(bank(0, B), soft[:, 1:3, :].rearrange("p a c -> p (a c)"),
                                        ident[0:B, 0:B]).then_inc(prep, 1)
                    pe.wait_ge(prep, at_("shift_in"))
                    nc.tensor.matmul(bank(1, B), w1t[:, :], sm[0:C, 12, :], start=True, stop=True)
                    nc.tensor.matmul(bank(2), ones[0:C, :], diag[:, :, :].rearrange("p b c -> p (b c)"),
                                     start=True, stop=True).then_inc(prep, 1)
                    pe.wait_ge(prep, at_("shift_out"))
                    nc.tensor.matmul(bank(3, B), w2t[:, :, :].rearrange("p a c -> p (a c)"), sm[:, 14, :],
                                     start=True, stop=True).then_inc(prep, 1)
                    pe.wait_ge(prep, at_("mats"))
                    for b in range(B):
                        last = nc.tensor.matmul(psum[:, b * 256:(b + 1) * 256],
                                                w1d[:, :, :].rearrange("p a c -> p (a c)"),
                                                rhs[:, b, :, :].rearrange("p d o -> p (d o)"),
                                                start=True, stop=True)
                    last.then_inc(prep, 1)

                @block.scalar
                def _(act):
                    act.wait_ge(prep, at_("std"))
                    act.activation(sm[:, 5, :], sm[:, 4, :], ACT.Sqrt).then_inc(prep, 1)
                    act.wait_ge(prep, at_("bstd"))
                    act.activation(col[:, 3:4], col[:, 2:3], ACT.Sqrt).then_inc(prep, 1)
                    act.wait_ge(prep, at_("gelu"))
                    act.activation(gt[:, :], bank(2, B, C), ACT.Gelu).then_inc(prep, 1)
                    act.wait_ge(prep, at_("exps"))
                    act.activation(soft[:, 3:5, :], soft[:, 1:3, :], ACT.Exp).then_inc(prep, 1)

                @block.vector
                def _(dve):
                    v = nc.vector
                    dve.wait_ge(prep, at_("evac_w"))
                    v.tensor_copy(w1t[:, :], bank(0, P, C))
                    v.tensor_copy(w2t[:, 0, :], bank(1, C))
                    v.tensor_copy(w2t[:, 1, :], bank(1, C))
                    v.tensor_copy(sa1t[:, :], bank(2, C, C))
                    v.tensor_copy(sa2t[:, :], bank(3, P, C))
                    v.tensor_copy(sm[:, 0, :], mean).then_inc(prep, 1)
                    dve.wait_ge(prep, at_("dev"))
                    v.scalar_tensor_tensor(out=sm[:, 1, :], in0=bank(4, B), scalar=-1.0, in1=sm[:, 0, :], op0=ALU.mult, op1=ALU.add).then_inc(prep, 1)
                    dve.wait_ge(prep, at_("dev2"))
                    v.tensor_tensor(sm[:, 2, :], sm[:, 1, :], sm[:, 1, :], ALU.mult).then_inc(prep, 1)
                    dve.wait_ge(prep, at_("devar"))
                    v.tensor_tensor(sm[:, 3, :], sm[:, 2, :], var, ALU.add).then_inc(prep, 1)
                    dve.wait_ge(prep, at_("veps"))
                    v.tensor_scalar(sm[:, 4, :], bank(5, B), EPS, None, ALU.add).then_inc(prep, 1)
                    dve.wait_ge(prep, at_("rstd"))
                    v.reciprocal(r, sm[:, 5, :]).then_inc(prep, 1)
                    dve.wait_ge(prep, at_("nmean"))
                    v.tensor_tensor(nmean, sm[:, 1, :], r, ALU.mult).then_inc(prep, 1)
                    dve.wait_ge(prep, at_("edges"))
                    v.reduce_sum(sm[:, 16:18, :], ecol[:, :].rearrange("p (b t e) -> p e b t", t=NT, e=2), axis=AX_X).then_inc(prep, 1)
                    dve.wait_ge(prep, at_("cdiff"))
                    v.tensor_tensor(sm[:, 18, :], sm[:, 16, :], sm[:, 17, :], ALU.subtract).then_inc(prep, 1)
                    dve.wait_ge(prep, at_("rsel"))
                    v.tensor_scalar(sm[:, 19, :], erow[:, 0::2], rowsel[:, 0:1], None, ALU.mult).then_inc(prep, 1)
                    dve.wait_ge(prep, at_("rdiff"))
                    v.scalar_tensor_tensor(out=sm[:, 20, :], in0=erow[:, 1::2], scalar=rowsel[:, 1:2], in1=sm[:, 19, :], op0=ALU.mult, op1=ALU.add).then_inc(prep, 1)
                    dve.wait_ge(prep, at_("cdiffr"))
                    v.tensor_tensor(sm[:, 9, :], sm[:, 18, :], r, ALU.mult).then_inc(prep, 1)
                    dve.wait_ge(prep, at_("rdiffr"))
                    v.tensor_tensor(sm[:, 10, :], sm[:, 20, :], r, ALU.mult).then_inc(prep, 1)
                    dve.wait_ge(prep, at_("cs_copy"))
                    v.tensor_copy(sm[:, 21:24, :].rearrange('p a b -> p (a b)'), bank(6, 3 * B)).then_inc(prep, 1)
                    dve.wait_ge(prep, at_("bmean"))
                    v.reduce_sum(col[:, 0:1], sm[:, 21, :], axis=AX_X).then_inc(prep, 1)
                    dve.wait_ge(prep, at_("bmean8"))
                    v.tensor_scalar(col[:, 1:2], col[:, 0:1], 1.0 / B, None, ALU.mult).then_inc(prep, 1)
                    dve.wait_ge(prep, at_("var_r"))
                    v.tensor_tensor(sm[:, 24, :], var, r, ALU.mult).then_inc(prep, 1)
                    dve.wait_ge(prep, at_("dev_c"))
                    v.tensor_scalar(sm[:, 25, :], nmean, col[:, 1:2], None, ALU.subtract).then_inc(prep, 1)
                    dve.wait_ge(prep, at_("var_rr"))
                    v.tensor_tensor(sm[:, 26, :], sm[:, 24, :], r, ALU.mult).then_inc(prep, 1)
                    dve.wait_ge(prep, at_("dev_c2"))
                    v.tensor_tensor(sm[:, 27, :], sm[:, 25, :], sm[:, 25, :], ALU.mult).then_inc(prep, 1)
                    dve.wait_ge(prep, at_("bvar"))
                    v.tensor_tensor(sm[:, 28, :], sm[:, 26, :], sm[:, 27, :], ALU.add).then_inc(prep, 1)
                    dve.wait_ge(prep, at_("bsum"))
                    v.reduce_sum(col[:, 4:5], sm[:, 28, :], axis=AX_X).then_inc(prep, 1)
                    dve.wait_ge(prep, at_("absg1"))
                    v.tensor_scalar(col[:, 5:6], vec[:, 1:2], -1.0, None, ALU.mult).then_inc(prep, 1)
                    dve.wait_ge(prep, at_("absg2"))
                    v.tensor_tensor(col[:, 6:7], col[:, 5:6], vec[:, 1:2], ALU.max).then_inc(prep, 1)
                    dve.wait_ge(prep, at_("bveps"))
                    v.tensor_scalar(col[:, 2:3], psum[:, 3584:3585], 1.0 / B, EPS, ALU.mult, ALU.add).then_inc(prep, 1)
                    dve.wait_ge(prep, at_("brstd"))
                    v.reciprocal(col[:, 11:12], col[:, 3:4]).then_inc(prep, 1)
                    dve.wait_ge(prep, at_("wbn"))
                    v.reciprocal(col[:, 7:8], psum[:, 3585:3586]).then_inc(prep, 1)
                    dve.wait_ge(prep, at_("gwbn"))
                    v.tensor_tensor(col[:, 8:9], col[:, 7:8], col[:, 6:7], ALU.mult).then_inc(prep, 1)
                    dve.wait_ge(prep, at_("kscale"))
                    v.tensor_tensor(col[:, 9:10], col[:, 8:9], vec[:, 1:2], ALU.mult)
                    v.tensor_tensor(col[:, 10:11], col[:, 8:9], vec[:, 2:3], ALU.mult).then_inc(prep, 1)
                    dve.wait_ge(prep, at_("A"))
                    v.tensor_tensor(k1, col[:, 11:12], col[:, 9:10], ALU.mult).then_inc(prep, 1)
                    dve.wait_ge(prep, at_("mr"))
                    v.tensor_scalar(params[:, 0:B, 0], r, k1, None, ALU.mult)
                    v.tensor_tensor(mr, bank(4, B), r, ALU.mult).then_inc(prep, 1)
                    dve.wait_ge(prep, at_("mrb"))
                    v.tensor_scalar(sm[:, 12, :], mr, -1.0, None, ALU.mult)
                    v.tensor_tensor(col[:, 13:14], k1, col[:, 1:2], ALU.mult).then_inc(prep, 1)
                    dve.wait_ge(prep, at_("Bneg"))
                    v.tensor_tensor(col[:, 14:15], col[:, 10:11], col[:, 13:14], ALU.subtract).then_inc(prep, 1)
                    dve.wait_ge(prep, at_("Bias"))
                    v.tensor_copy(params[:, 0:B, 1], col[:, 14:15].to_broadcast([P, B]))
                    v.tensor_copy(params[:, 0:B, 2], bank(4, B)).then_inc(prep, 1)
                    dve.wait_ge(prep, at_("npsum"))
                    v.tensor_scalar(sm[:, 31, :], sm[:, 21, :], float(NPIX), None, ALU.mult)
                    v.tensor_tensor(diag[:, :, :], ident[0:C, 0:C].unsqueeze(1).to_broadcast([C, B, C]),
                                    sm[0:C, 6, :].unsqueeze(2).to_broadcast([C, B, C]), ALU.mult).then_inc(prep, 1)
                    dve.wait_ge(prep, at_("td"))
                    for d, (edge, sg) in enumerate(((23, 2.0), (23, -2.0), (22, 2.0), (22, -2.0))):
                        last = v.scalar_tensor_tensor(out=td[:, d, :], in0=sm[:, edge, :], scalar=sg,
                                                      in1=sm[:, 31, :], op0=ALU.mult, op1=ALU.add)
                    last.then_inc(prep, 1)
                    dve.wait_ge(prep, at_("pool_copy"))
                    v.tensor_copy(asb[:, :], psum[0:B, 0:C]).then_inc(prep, 1)
                    dve.wait_ge(prep, at_("at"))
                    v.tensor_copy(at[:, :], bank(1, B, C)).then_inc(prep, 1)
                    dve.wait_ge(prep, at_("h0"))
                    v.tensor_copy(soft[:, 0, :], bank(3, C, B)).then_inc(prep, 1)
                    dve.wait_ge(prep, at_("hmax"))
                    v.tensor_tensor(soft[:, 5, :], bank(3, P, B)[:, C:P], soft[:, 0, :], ALU.max).then_inc(prep, 1)
                    dve.wait_ge(prep, at_("l0"))
                    v.tensor_tensor(soft[:, 1, :], soft[:, 0, :], soft[:, 5, :], ALU.subtract)
                    v.tensor_tensor(soft[:, 2, :], bank(3, P, B)[:, C:P], soft[:, 5, :], ALU.subtract).then_inc(prep, 1)
                    dve.wait_ge(prep, at_("esum"))
                    v.tensor_tensor(soft[:, 0, :], soft[:, 3, :], soft[:, 4, :], ALU.add).then_inc(prep, 1)
                    dve.wait_ge(prep, at_("rsum"))
                    v.reciprocal(soft[:, 5, :], soft[:, 0, :]).then_inc(prep, 1)
                    dve.wait_ge(prep, at_("bar"))
                    v.tensor_tensor(soft[:, 1, :], soft[:, 3, :], soft[:, 5, :], ALU.mult)
                    v.tensor_tensor(soft[:, 2, :], soft[:, 4, :], soft[:, 5, :], ALU.mult).then_inc(prep, 1)
                    dve.wait_ge(prep, at_("bart"))
                    v.tensor_copy(bart[:, :], bank(0, B)).then_inc(prep, 1)
                    dve.wait_ge(prep, at_("z"))
                    v.tensor_scalar(sm[:, 13, :], bank(1, B), b1c[:, :], None, ALU.add).then_inc(prep, 1)
                    dve.wait_ge(prep, at_("zb"))
                    v.tensor_tensor(sm[:, 14, :], sm[:, 13, :], bart[:, :], ALU.mult).then_inc(prep, 1)
                    dve.wait_ge(prep, at_("mask"))
                    v.tensor_tensor(mb[:, :, :], bart[:, :].unsqueeze(2).to_broadcast([P, B, NS]),
                                    dmask.unsqueeze(1).to_broadcast([P, B, NS]), ALU.mult).then_inc(prep, 1)
                    dve.wait_ge(prep, at_("w2s"))
                    v.tensor_tensor(w2s[:, :, :], bank(2).rearrange('p (b c) -> p b c', b=B),
                                    w2t[:, 0, :].unsqueeze(1).to_broadcast([P, B, C]), ALU.mult).then_inc(prep, 1)
                    dve.wait_ge(prep, at_("cb"))
                    v.tensor_scalar(sm[:, 15, :], bank(3, B), vec[:, 0:1], None, ALU.add).then_inc(prep, 1)
                    dve.wait_ge(prep, at_("cbr"))
                    v.tensor_tensor(params[:, 0:B, 3], sm[:, 15, :], r, ALU.mult).then_inc(prep, 1)
                    dve.wait_ge(prep, at_("rhs"))
                    for b in range(B):
                        last = v.tensor_tensor(rhs[:, b, :, :], w2s[:, b, :].unsqueeze(1).to_broadcast([P, NS, C]),
                                               mb[:, b, :].unsqueeze(2).to_broadcast([P, NS, C]), ALU.mult)
                    last.then_inc(prep, 1)
                    dve.wait_ge(prep, at_("wall"))
                    mats = psum[:, 0:B * 256].rearrange("p (b d o) -> p b d o", b=B, d=NS)
                    for b in range(B):
                        for half, slot, d in LAYOUT:
                            h = slice(half * C, (half + 1) * C)
                            v.tensor_scalar(wall[h, b, slot * C:(slot + 1) * C], mats[h, b, d, :],
                                            sm[h, 6, b:b + 1], None, ALU.mult)

        ph = ExitStack()
        with ph:
            NX = 4
            XT = [sb(ph, f"mix_x{i}", [P, MR + 1, PITCH]) for i in range(NX)]
            XC = [sb(ph, f"centred{i}", [P, SC]) for i in range(2)]
            G = [sb(ph, f"gated{i}", [P, SC]) for i in range(2)]
            XO = [sb(ph, f"mix_out{i}", [P, SC]) for i in range(2)]
            SQ = sb(ph, "square", [P, SC])
            one = sb(ph, "one", [P, MR + 1])
            wcur = [sb(ph, f"wcur{i}", [P, P]) for i in range(2)]
            pcur = [sb(ph, f"pcur{i}", [P, 6]) for i in range(2)]
            loaded = [sem(f"mix_loaded{i}") for i in range(NX)]
            stored = [sem(f"mix_stored{i}") for i in range(2)]
            one_set = sem("mix_one_set")
            doubled, padded, batch_ready = sem("mix_doubled"), sem("mix_padded"), sem("mix_batch_ready")
            xc_done, sig_done, conv_done, sq_done = (sem("mix_" + n) for n in ("xc", "sig", "conv", "sq"))
            g_dve, g_pool, h_done, o_done = (sem("mix_" + n) for n in ("g_dve", "g_pool", "h", "o"))
            NB = H // MR
            NI = 2 * NB
            ITER = B // 2
            x1_par = x1.rearrange("b c (r e) w -> (b c) r e w", e=2)

            def on_pool(n):
                return n % 2 == 1

            def bytes_of(i, n):
                q, t = n % NX, n % NB
                edge = 16 if q in (0, NX - 1) else 0
                batch = NB // NX * 32 + edge
                return i * (2 * batch) + n // NB * batch + (t // NX + 1) * 32 + (edge if q == 0 or t == NB - 1 else 0)

            def iterations(engine, body):
                with engine.Fori(0, ITER - 1) as i:
                    body(i, False)
                body(ITER - 1, True)

            with nc.Block() as block:
                @block.sync
                def _(sp):
                    with sp.Fori(0, ITER) as i:
                        for n in range(NI):
                            ch = bass.ds((i * 2 + n // NB) * C, C)
                            t, xt = n % NB, XT[n % NX]
                            sp.wait_ge(conv_done, i * NI + n + 1)
                            sp.wait_ge(xc_done, i * NI + n + 1)
                            r0 = t * MR - 1
                            lo = max(r0, 0)
                            sp.dma_start(xt[0:C, lo - r0:MR // 2 + 1, 1:W + 1],
                                         x_rows[ch, lo:r0 + MR // 2 + 1, :]).then_inc(loaded[n % NX], 16)
                            hi = min(r0 + MR + 2, H)
                            sp.dma_start(xt[C:P, MR // 2:hi - r0 - 1, 0:W],
                                         x_rows[ch, r0 + 1 + MR // 2:hi, :]).then_inc(loaded[n % NX], 16)
                            if t == 0:
                                sp.dma_start(xt[0:C, 0:1, 1:W + 1], x_rows[ch, 0:1, :]).then_inc(loaded[n % NX], 16)
                            if t == NB - 1:
                                sp.dma_start(xt[C:P, MR:MR + 1, 0:W], x_rows[ch, H - 1:H, :]
                                             ).then_inc(loaded[n % NX], 16)
                    for k in range(2):
                        sp.wait_ge(stored[k], B * NB // 2 * 32 + 16)

                @block.gpsimd
                def _(pool):
                    nc.gpsimd.memset(one[:, :], 1.0).then_inc(one_set, 1)
                    pool.wait_ge(one_set, 1)

                    def pad(i, n):
                        pool.wait_ge(doubled, i * NI + n + 1)
                        for half, to, of in ((0, 0, 1), (1, W, W - 1)):
                            h = slice(half * C, (half + 1) * C)
                            last = nc.gpsimd.tensor_tensor(XT[n % NX][h, :, to], XT[n % NX][h, :, of],
                                                           one[h, :], ALU.mult)
                        last.then_inc(padded, 1)

                    pad(0, 0)
                    pad(0, 1)

                    def body(i, final):
                        for n in range(NI):
                            if on_pool(n):
                                k = n % 2
                                pool.wait_ge(padded, i * NI + n + 2 - (final and n == NI - 1))
                                pool.wait_ge(sig_done, i * NI + n + 1)
                                nc.gpsimd.tensor_tensor(G[k][:, :], XC[k][:, :], G[k][:, :],
                                                        ALU.mult).then_inc(g_pool, 1)
                            if not (final and n + 2 >= NI):
                                if on_pool(n):
                                    pool.wait_ge(g_pool, i * NB + (n + 1) // 2)
                                pad(i, n + 2)

                    iterations(pool, body)

                @block.tensor
                def _(pe):
                    pe.sem_inc(conv_done, NX)
                    with pe.Fori(0, ITER) as i:
                        for n in range(NI):
                            j, k = n // NB, n % 2
                            if n % NB == 0:
                                pe.wait_ge(batch_ready, i * 2 + j + 1)
                            pe.wait_ge(padded, i * NI + n + 1)
                            pe.wait_ge(h_done, i * NI + n + 1)
                            for m in range(2):
                                for q in range(4):
                                    for par in range(2):
                                        r0 = 1 - m + par + q * 4
                                        last = nc.tensor.matmul(bank(k * 4 + q, 512, C, par * C),
                                                                wcur[j][:, m * C:(m + 1) * C],
                                                                XT[n % NX][:, r0:r0 + 3:2, m:m + W],
                                                                start=(m == 0), stop=(m == 1))
                            last.then_inc(conv_done, 1)

                @block.scalar
                def _(act):
                    act.sem_inc(sq_done, 2)
                    act.sem_inc(xc_done, NX)
                    for k in range(2):
                        act.sem_inc(stored[k], 16)

                    def gate(i, n):
                        j, k = n // NB % 2, n % 2
                        if n % NB == 0:
                            act.wait_ge(batch_ready, i * 2 + n // NB + 1)
                        act.wait_ge(padded, i * NI + n + 1)
                        act.wait_ge(o_done, i * NI + n + 1)
                        for half in range(2):
                            h = slice(half * C, (half + 1) * C)
                            last = nc.scalar.activation(
                                XC[k][h, :].rearrange("p (r w) -> p r w", w=W),
                                XT[n % NX][h, 1:MR:2, 1 - half:1 - half + W],
                                ACT.Identity, bias=pcur[j][h, 4:5])
                        last.then_inc(xc_done, 1)
                        act.wait_ge(xc_done, i * NI + NX + n + 1)
                        nc.scalar.activation(G[k][:, :], XC[k][:, :], ACT.Sigmoid,
                                             bias=pcur[j][:, 1:2], scale=pcur[j][:, 0:1]).then_inc(sig_done, 1)

                    gate(0, 0)
                    gate(0, 1)

                    def body(i, final):
                        for n in range(NI):
                            j, k, y0 = n // NB, n % 2, n % NB * SP_
                            act.wait_ge(o_done, i * NI + 2 + n + 1)
                            for par in range(2):
                                act.dma_start(x1_par[bass.ds((i * 2 + j) * C, C), y0:y0 + SP_, par, :],
                                              XO[k][par * C:(par + 1) * C, :].rearrange("p (r w) -> p r w", w=W)
                                              ).then_inc(stored[k], 16)
                            if not (final and n + 2 >= NI):
                                gate(i, n + 2)
                            act.wait_ge(sq_done, i * NI + n + 2)
                            nc.scalar.activation(SQ[:, :], XO[k][:, :], ACT.Square, bias=pcur[j][:, 4:5],
                                                 accum_out=sqs[:, bass.ds(i * NI + n, 1)]).then_inc(sq_done, 1)

                    iterations(act, body)

                @block.vector
                def _(dve):
                    def take(b, j):
                        nc.vector.tensor_copy(wcur[j][:, :], wall[:, bass.ds(b, 1), :].rearrange("p a k -> p (a k)"))
                        nc.vector.tensor_copy(pcur[j][:, 0:4], params[:, bass.ds(b, 1), :].rearrange("p a k -> p (a k)"))
                        nc.vector.tensor_scalar(pcur[j][:, 4:5],
                                                params[:, bass.ds(b, 1), 2:3].rearrange("p a k -> p (a k)"),
                                                -1.0, None, ALU.mult).then_inc(batch_ready, 1)

                    def double(i, n):
                        dve.wait_ge(loaded[n % NX], bytes_of(i, n))
                        xt, h = XT[n % NX], MR // 2
                        nc.vector.tensor_copy(xt[C:P, 0:h, 0:W], xt[0:C, 1:h + 1, 1:W + 1])
                        nc.vector.tensor_copy(xt[0:C, h + 1:MR + 1, 1:W + 1], xt[C:P, h:MR, 0:W]).then_inc(doubled, 1)

                    dve.sem_inc(h_done, 2)
                    dve.sem_inc(o_done, 2)
                    take(0, 0)
                    dve.wait_ge(batch_ready, 1)
                    double(0, 0)
                    double(0, 1)

                    def body(i, final):
                        for n in range(NI):
                            j, k = n // NB, n % 2
                            if not (final and n + 2 >= NI):
                                double(i, n + 2)
                            if not on_pool(n):
                                dve.wait_ge(sig_done, i * NI + n + 1)
                                nc.vector.tensor_tensor(G[k][:, :], XC[k][:, :], G[k][:, :],
                                                        ALU.mult).then_inc(g_dve, 1)
                            dve.wait_ge(conv_done, i * NI + NX + n + 1)
                            if on_pool(n):
                                dve.wait_ge(g_pool, i * NB + n // 2 + 1)
                            else:
                                dve.wait_ge(g_dve, i * NB + n // 2 + 1)
                            nc.vector.scalar_tensor_tensor(out=G[k][:, :], in0=psum[:, k * SC:(k + 1) * SC],
                                                           scalar=pcur[j][:, 3:4], in1=G[k][:, :],
                                                           op0=ALU.add, op1=ALU.mult).then_inc(h_done, 1)
                            dve.wait_ge(h_done, i * NI + 2 + n + 1)
                            dve.wait_ge(stored[k], i * (NB * 32) + n // 2 * 32 + 16)
                            dve.wait_ge(sq_done, i * NI + n + 1)
                            nc.vector.scalar_tensor_tensor(out=XO[k][:, :], in0=XC[k][:, :],
                                                           scalar=pcur[j][:, 2:3], in1=G[k][:, :],
                                                           op0=ALU.add, op1=ALU.add,
                                                           accum_out=sums[:, bass.ds(i * NI + n, 1)]
                                                           ).then_inc(o_done, 1)
                            if n % NB == NB // 2:
                                take(i * 2 + j + 1, 1 - j)
                                dve.wait_ge(batch_ready, i * 2 + j + 2)

                    iterations(dve, body)

        ph = ExitStack()
        with ph:
            T = table(ph, ["group"])
            sv = sb(ph, "norm2_values", [P, 10, B])
            n2_tab, n2 = sem("norm2_table"), sem("norm2_steps")
            with nc.Block() as block:
                @block.sync
                def _(sp):
                    sp.dma_start(*T["group"]).then_inc(n2_tab, 16)

                @block.tensor
                def _(pe):
                    pe.wait_ge(n2_tab, 16)
                    pe.wait_ge(n2, 2)
                    nc.tensor.matmul(bank(0, 2 * B), T["group"][0], sv[:, 2:4, :].rearrange("p a b -> p (a b)"),
                                     start=True, stop=True).then_inc(n2, 1)

                @block.scalar
                def _(act):
                    act.wait_ge(n2, 6)
                    nc.scalar.activation(sv[:, 7, :], sv[:, 6, :], ACT.Sqrt).then_inc(n2, 1)

                @block.vector
                def _(dve):
                    v = nc.vector
                    inv = 1.0 / (HALF * W)
                    v.reduce_sum(sv[:, 0, :], sums[:, :].rearrange("p (b n) -> p b n", b=B), axis=AX_X)
                    v.reduce_sum(sv[:, 1, :], sqs[:, :].rearrange("p (b n) -> p b n", b=B), axis=AX_X).then_inc(n2, 1)
                    dve.wait_ge(n2, 1)
                    v.scalar_tensor_tensor(out=sv[:, 2, :], in0=sv[:, 0, :], scalar=inv, in1=params[:, 0:B, 2],
                                           op0=ALU.mult, op1=ALU.subtract)
                    v.tensor_scalar(sv[:, 3, :], sv[:, 1, :], inv, None, ALU.mult).then_inc(n2, 1)
                    dve.wait_ge(n2, 3)
                    v.tensor_copy(sv[:, 4, :], bank(0, B))
                    v.tensor_tensor(sv[:, 9, :], params[:, 0:B, 2], bank(0, B), ALU.add).then_inc(n2, 1)
                    dve.wait_ge(n2, 4)
                    v.tensor_tensor(sv[:, 5, :], sv[:, 4, :], sv[:, 4, :], ALU.mult).then_inc(n2, 1)
                    dve.wait_ge(n2, 5)
                    v.scalar_tensor_tensor(out=sv[:, 6, :], in0=bank(0, 2 * B)[:, B:], scalar=EPS, in1=sv[:, 5, :],
                                           op0=ALU.add, op1=ALU.subtract).then_inc(n2, 1)
                    dve.wait_ge(n2, 7)
                    v.reciprocal(norm2[:, 0, :], sv[:, 7, :]).then_inc(n2, 1)
                    dve.wait_ge(n2, 8)
                    v.scalar_tensor_tensor(out=norm2[:, 1, :], in0=sv[:, 9, :], scalar=-float(NPIX),
                                           in1=norm2[:, 0, :], op0=ALU.mult, op1=ALU.mult)

        ph = ExitStack()
        with ph:
            T = table(ph, ["ident", "frow", "fcol"])
            ident = T["ident"][0]
            frow = T["frow"][0].rearrange("p (a m) -> p a m", a=2)
            fcol = T["fcol"][0].rearrange("p (a k m) -> p a k m", a=2, k=2)
            XW = [sb(ph, f"fwd_x{i}", [P, 2, CG, W]) for i in range(2)]
            ED = [[sb(ph, f"fwd_{n}{i}", [P, CG, W]) for n in ("sum", "diff")] for i in range(2)]
            RS = [sb(ph, f"fwd_rows{i}", [P, 512]) for i in range(2)]
            A = [sb(ph, f"fwd_cols{i}", [P, 2, 4 * NP, C]) for i in range(2)]
            XB = sb(ph, "fwd_modes", [C, 3, KX, M2])
            ncur = [sb(ph, f"ncur{i}", [P, 2]) for i in range(2)]
            tab, loaded = sem("fwd_tables"), [sem(f"fwd_loaded{i}") for i in range(2)]
            sum_done, diff_done = sem("fwd_sum"), sem("fwd_diff")
            row_done, row_out, tr_done, tr_out = (sem("fwd_" + n) for n in ("row", "row_out", "tr", "tr_out"))
            col_done, col_act, col_dve = (sem("fwd_" + n) for n in ("col", "col_act", "col_dve"))
            cur, neg_done, modes_stored, modes_free = (sem("fwd_" + n) for n in ("cur", "neg", "stored", "free"))
            NR = C // 2
            with nc.Block() as block:
                @block.sync
                def _(sp):
                    for n in ("ident", "frow", "fcol"):
                        sp.dma_start(*T[n]).then_inc(tab, 16)
                    with sp.Fori(0, B // 2) as i:
                        for j in range(2):
                            for g in range(NG):
                                G0 = j * NG + g
                                sp.wait_ge(sum_done, i * (2 * NG) + G0 + 1)
                                sp.wait_ge(diff_done, i * (2 * NG) + G0 + 1)
                                for a in range(2):
                                    sp.dma_start(XW[g % 2][:, a, :, :],
                                                 x1_rows[a * P:(a + 1) * P, bass.ds((i * 2 + j) * C + g * CG, CG), :]
                                                 ).then_inc(loaded[g % 2], 16)

                @block.tensor
                def _(pe):
                    pe.sem_inc(row_done, 8)
                    pe.sem_inc(tr_done, 2)
                    pe.sem_inc(col_done, 10)
                    pe.wait_ge(tab, 48)
                    with pe.Fori(0, B // 2) as i:
                        def rows(n):
                            G0, cp = n // 4, n % 4
                            if cp == 0:
                                pe.wait_ge(sum_done, i * (2 * NG) + G0 + 3)
                                pe.wait_ge(diff_done, i * (2 * NG) + G0 + 3)
                            pe.wait_ge(row_out, i * (2 * NR) + n + 1)
                            for par in range(2):
                                last = nc.tensor.matmul(bank(n % 2, 512, C, par * C), frow[:, par, :],
                                                        ED[G0 % 2][par][:, 2 * cp:2 * cp + 2, :],
                                                        start=True, stop=True)
                            last.then_inc(row_done, 1)

                        def transposes(n):
                            pe.wait_ge(row_out, i * (2 * NR) + 2 + n + 1)
                            pe.wait_ge(tr_out, i * (2 * NR) + n + 1)
                            for q in range(4):
                                at = (2 + n % 2) * 512 + q * P
                                last = nc.tensor.transpose(psum[:, at:at + P], RS[n % 2][:, q * P:(q + 1) * P], ident)
                            last.then_inc(tr_done, 1)

                        for j in range(2):
                            rows(j * NR)
                            for n in range(j * NR, (j + 1) * NR):
                                if n + 1 < (j + 1) * NR:
                                    rows(n + 1)
                                transposes(n)
                            pe.wait_ge(tr_out, i * (2 * NR) + 2 + (j + 1) * NR)
                            for m in range(5):
                                if m < 4:
                                    pe.wait_ge(col_act, i * 4 + j * 2 + 1)
                                    pe.wait_ge(col_dve, i * 6 + j * 3 + 1)
                                else:
                                    pe.wait_ge(col_act, i * 4 + j * 2 + 2)
                                for p in range(4 * m, min(4 * m + 4, 17)):
                                    wide = 2 if p < 16 else 1
                                    o = psum[0:wide * C, (4 + m % 4) * 512 + p % 4 * P:(4 + m % 4) * 512 + (p % 4 + 1) * P]
                                    for q in range(4):
                                        a, k = q // 2, q % 2
                                        mode = k * 2 * NP + 2 * p
                                        last = nc.tensor.matmul(
                                            o, A[j][:, a, mode:mode + wide, :].rearrange("p m c -> p (m c)"),
                                            fcol[:, a, k, :], start=(q == 0), stop=(q == 3))
                                last.then_inc(col_done, 1)

                def col_copies(m):
                    if m == 4:
                        return [(0, 0, 1, 1, 63)]
                    got = []
                    for par in range(2):
                        k = 8 * m + par
                        got.append((par, 0, 4, 0, k))
                        if k == 0:
                            got.append((par, 1, 3, 1, 31 + 2))
                        else:
                            got.append((par, 0, 4, 1, 31 + k))
                    return got

                def col_views(m, par, first, count, sign, pos):
                    src = psum[par * C:(par + 1) * C, (4 + m % 4) * 512:(5 + m % 4) * 512] \
                        .rearrange("p (s g r k) -> p s g r k", s=4, g=2, r=2)[:, first:first + count, sign, :, :]
                    dst = XB[:, 0:2, pos:pos + 2 * count - 1:2, :].rearrange("p r s k -> p s r k")
                    return dst, src

                @block.scalar
                def _(act):
                    act.sem_inc(row_out, 2)
                    act.sem_inc(col_act, 1)
                    with act.Fori(0, B // 2) as i:
                        for j in range(2):
                            for n in range(j * NR, (j + 1) * NR):
                                act.wait_ge(row_done, i * (2 * NR) + 8 + n + 1)
                                act.wait_ge(tr_done, i * (2 * NR) + n + 1)
                                nc.scalar.activation(RS[n % 2][:, :], bank(n % 2), ACT.Copy).then_inc(row_out, 1)
                            act.wait_ge(cur, i * 2 + j + 1)
                            act.wait_ge(modes_free, i * 2 + j + 1)
                            for m in (0, 2):
                                act.wait_ge(col_done, i * 10 + j * 5 + 10 + m + 1)
                                for par, first, count, sign, pos in col_copies(m):
                                    dst, src = col_views(m, par, first, count, sign, pos)
                                    last = nc.scalar.activation(dst, src, ACT.Copy,
                                                                scale=ncur[j][par * C:(par + 1) * C, 0:1])
                                last.then_inc(col_act, 1)

                @block.vector
                def _(dve):
                    dve.sem_inc(tr_out, 2)
                    dve.sem_inc(col_dve, 1)
                    dve.sem_inc(sum_done, 2)
                    with dve.Fori(0, B // 2) as i:
                        def sums_of(G0):
                            dve.wait_ge(loaded[G0 % 2], i * (NG * 32) + (G0 // 2 + 1) * 32)
                            dve.wait_ge(row_done, i * (2 * NR) + 4 * G0 + 4)
                            nc.vector.tensor_tensor(ED[G0 % 2][0][:, :, :], XW[G0 % 2][:, 0, :, :],
                                                    XW[G0 % 2][:, 1, :, :], ALU.add).then_inc(sum_done, 1)

                        sums_of(0)
                        for j in range(2):
                            dve.wait_ge(col_done, i * 10 + j * 5 + 5)
                            dve.wait_ge(col_act, i * 4 + 1)
                            nc.vector.tensor_copy(ncur[j][:, :], norm2[:, :, bass.ds(i * 2 + j, 1)]
                                                  .rearrange("p a b -> p (a b)")).then_inc(cur, 1)
                            for n in range(j * NR, (j + 1) * NR):
                                if n % 4 == 1 and n // 4 + 1 < 2 * NG:
                                    sums_of(n // 4 + 1)
                                c0 = n % NR * 2
                                dve.wait_ge(tr_done, i * (2 * NR) + 2 + n + 1)
                                src = bank(2 + n % 2).rearrange("p (c a m) -> p c a m", c=2, a=2)
                                dst = A[j][:, :, :, c0:c0 + 2].rearrange("p a m c -> p c a m")
                                for par in range(2):
                                    last = nc.vector.tensor_copy(dst[:, :, :, par::2],
                                                                 src[:, :, :, par * C:par * C + 2 * NP])
                                last.then_inc(tr_out, 1)
                            dve.wait_ge(cur, i * 2 + j + 1)
                            dve.wait_ge(modes_free, i * 2 + j + 1)
                            for m in (1, 3, 4):
                                dve.wait_ge(col_done, i * 10 + j * 5 + 10 + m + 1)
                                for par, first, count, sign, pos in col_copies(m):
                                    dst, src = col_views(m, par, first, count, sign, pos)
                                    last = nc.vector.tensor_scalar(dst, src, ncur[j][par * C:(par + 1) * C, 0:1],
                                                                   None, ALU.mult)
                                last.then_inc(col_dve, 1)
                            dve.wait_ge(col_act, i * 4 + j * 2 + 3)
                            dve.wait_ge(col_dve, i * 6 + j * 3 + 4)
                            nc.vector.tensor_tensor(XB[:, 0, 0, 0:1], XB[:, 0, 0, 0:1], ncur[j][0:C, 1:2], ALU.add)
                            nc.vector.tensor_scalar(XB[:, 2, :, :], XB[:, 1, :, :], -1.0, None,
                                                    ALU.mult).then_inc(neg_done, 1)

                @block.gpsimd
                def _(pool):
                    pool.sem_inc(modes_free, 1)
                    pool.sem_inc(diff_done, 2)
                    with pool.Fori(0, B // 2) as i:
                        def diffs_of(G0):
                            pool.wait_ge(loaded[G0 % 2], i * (NG * 32) + (G0 // 2 + 1) * 32)
                            pool.wait_ge(row_done, i * (2 * NR) + 4 * G0 + 4)
                            nc.gpsimd.tensor_tensor(ED[G0 % 2][1][:, :, :], XW[G0 % 2][:, 0, :, :],
                                                    XW[G0 % 2][:, 1, :, :], ALU.subtract).then_inc(diff_done, 1)

                        for j in range(2):
                            for G0 in (range(NG + 2) if j == 0 else range(NG + 2, 2 * NG)):
                                diffs_of(G0)
                            pool.wait_ge(neg_done, i * 2 + j + 1)
                            b = i * 2 + j
                            for p0, r, q, w in ((0, 0, 0, 2), (C, 0, 2, 1), (C, 1, 0, 1)):
                                pool.dma_start(
                                    xd[p0:p0 + C, bass.ds(b, 1), r:r + w, :, :].rearrange("p b r k m -> p (b r k m)"),
                                    XB[:, q:q + w, :, :].rearrange("p r k m -> p (r k m)")).then_inc(modes_stored, 16)
                            pool.wait_ge(modes_stored, i * 96 + j * 48 + 48)
                            pool.sem_inc(modes_free, 1)
                    pool.wait_ge(modes_stored, B * 48)

        ph = ExitStack()
        with ph:
            WT = [sb(ph, f"mode_w{i}", [P, C, P]) for i in range(2)]
            XM = [sb(ph, f"mode_x{i}", [P, 2 * B, P]) for i in range(2)]
            YS = [sb(ph, f"mode_y{i}", [P, M2 * C]) for i in range(2)]
            loaded = [sem(f"mode_loaded{i}") for i in range(2)]
            stored = [sem(f"mode_stored{i}") for i in range(2)]
            mixed, out_act, out_dve, zero = sem("mode_mixed"), sem("mode_out_act"), sem("mode_out_dve"), sem("mode_zero")
            views = [[a.rearrange("i o x y -> i o (x y)") for a in pair] for pair in ((wr1, wi1), (wr2, wi2))]
            xm = xd.rearrange("p b r k m -> p (b r) (k m)")
            with nc.Block() as block:
                @block.sync
                def _(sp):
                    for s in range(2):
                        with sp.Fori(0, 4) as i:
                            for j in range(2):
                                sp.wait_ge(mixed, (i * 2 + j) + 8 * s + 1)
                                cw = i * 2 + j
                                for q in range(2):
                                    sp.dma_start(WT[j][q * C:(q + 1) * C, :, :],
                                                 views[s][q][:, :, bass.ds(cw * P, P)]).then_inc(loaded[j], 16)
                                pos = cw * P if s == 0 else cw * (-P) + (KX - 4) * M2
                                sp.dma_start(XM[j][:, :, :], xm[:, :, bass.ds(pos, P)]).then_inc(loaded[j], 16)

                @block.tensor
                def _(pe):
                    pe.sem_inc(mixed, 2)
                    pe.wait_ge(zero, 1)
                    for s in range(2):
                        with pe.Fori(0, 4) as i:
                            for j in range(2):
                                pe.wait_ge(loaded[j], i * 48 + 48 * (4 * s + 1))
                                pe.wait_ge(out_act, i * 2 + j + 8 * s + 1)
                                pe.wait_ge(out_dve, i * 2 + j + 8 * s + 1)
                                for ky in range(M2):
                                    for k in range(4):
                                        kx = k if s == 0 else 3 - k
                                        at = j * 2048 + ky * C
                                        last = nc.tensor.matmul(psum[32 * k:32 * k + 2 * B, at:at + C],
                                                                XM[j][:, :, kx * M2 + ky],
                                                                WT[j][:, :, k * M2 + ky], start=True, stop=True)
                                last.then_inc(mixed, 1)

                @block.scalar
                def _(act):
                    act.sem_inc(out_act, 2)
                    for j in range(2):
                        act.sem_inc(stored[j], 16)
                    for s in range(2):
                        with act.Fori(0, 4) as i:
                            for j in range(2):
                                act.wait_ge(mixed, i * 2 + j + 8 * s + 3)
                                act.wait_ge(stored[j], i * 64 + 256 * s + 16)
                                nc.scalar.activation(YS[j][:, 0:1024], psum[:, j * 2048:j * 2048 + 1024],
                                                     ACT.Copy).then_inc(out_act, 1)
                                act.wait_ge(out_act, i * 2 + j + 8 * s + 3)
                                act.wait_ge(out_dve, i * 2 + j + 8 * s + 3)
                                for k in range(4):
                                    act.dma_start(yd[:, bass.ds((i * 2 + j) * 4 + 32 * s + k, 1), :, :]
                                                  .rearrange("q k m c -> q (k m c)"),
                                                  YS[j][32 * k:32 * k + 2 * B, :]).then_inc(stored[j], 16)
                    for j in range(2):
                        act.wait_ge(stored[j], 8 * 64 + 16)

                @block.vector
                def _(dve):
                    dve.sem_inc(out_dve, 2)
                    nc.vector.memset(psum[:, :], 0.0).then_inc(zero, 1)
                    for s in range(2):
                        with dve.Fori(0, 4) as i:
                            for j in range(2):
                                dve.wait_ge(mixed, i * 2 + j + 8 * s + 3)
                                dve.wait_ge(stored[j], i * 64 + 256 * s + 16)
                                nc.vector.tensor_copy(YS[j][:, 1024:2048], psum[:, j * 2048 + 1024:j * 2048 + 2048]
                                                      ).then_inc(out_dve, 1)

        ph = ExitStack()
        with ph:
            T = table(ph, ["irow", "icol", "sign"])
            irow, icol, sign = (T[n][0] for n in ("irow", "icol", "sign"))
            NX = 4
            XW = [sb(ph, f"inv_x{i}", [P, 2, CG, W]) for i in range(NX)]
            YA = sb(ph, "inv_ya", [P, M2, C])
            YB = sb(ph, "inv_yb", [P, M2, C])
            YY = [sb(ph, f"inv_yy{i}", [P, C, 2, M2]) for i in range(2)]
            TS = [sb(ph, f"inv_t{i}", [P, W]) for i in range(2)]
            tab, y_loaded = sem("inv_tables"), sem("inv_y_loaded")
            loaded = [sem(f"inv_loaded{i}") for i in range(NX)]
            stored = [sem(f"inv_stored{i}") for i in range(NX)]
            x_free = sem("inv_x_free")
            y_ready, row_done, row_out, col_done, added = (sem("inv_" + n) for n in ("y", "row", "row_out", "col", "added"))
            NR = C // 2
            out_rows_ = out_rows
            with nc.Block() as block:
                @block.sync
                def _(sp):
                    for n in ("irow", "icol", "sign"):
                        sp.dma_start(*T[n]).then_inc(tab, 16)
                    with sp.Fori(0, B // 2) as i:
                        for j in range(2):
                            b = i * 2 + j
                            sp.wait_ge(y_ready, b + 1)
                            for n, dst in enumerate((YA, YB)):
                                for half in range(2):
                                    q = half if n == 0 else 1 - half
                                    sp.dma_start(dst[half * C:(half + 1) * C, :, :],
                                                 yd[bass.ds(b * 2 + q, 1), :, :, :].rearrange("q k m c -> (q k) m c")
                                                 ).then_inc(y_loaded, 16)
                            for g in range(NG):
                                G0 = j * NG + g
                                sp.wait_ge(x_free, i * (2 * NG) + G0 + 1)
                                for a in range(2):
                                    sp.dma_start(XW[g % NX][:, a, :, :],
                                                 x1_rows[a * P:(a + 1) * P, bass.ds(b * C + g * CG, CG), :]
                                                 ).then_inc(loaded[g % NX], 16)

                @block.tensor
                def _(pe):
                    pe.sem_inc(row_done, 2 * NR)
                    pe.sem_inc(col_done, 2)
                    pe.wait_ge(tab, 48)
                    with pe.Fori(0, B // 2) as i:
                        def rows(n):
                            j, o = n // NR, n % NR * 2
                            if n % NR == 0:
                                pe.wait_ge(y_ready, i * 2 + j + 2)
                            pe.wait_ge(row_out, i * (2 * NR) + n + 1)
                            nc.tensor.matmul(bank(6 + n % 2, W),
                                             YY[j][:, o:o + 2, :, :].rearrange("p o r k -> p (o r k)"),
                                             irow, start=True, stop=True).then_inc(row_done, 1)

                        def cols(n):
                            pe.wait_ge(row_out, i * (2 * NR) + 2 + n + 1)
                            pe.wait_ge(added, i * (2 * NR) + n + 1)
                            for a in range(2):
                                last = nc.tensor.matmul(bank(n % 2 * 2 + a), TS[n % 2][:, a * P:(a + 1) * P], icol,
                                                        start=True, stop=True)
                            last.then_inc(col_done, 1)

                        rows(0)
                        for n in range(2 * NR):
                            if n + 1 < 2 * NR:
                                rows(n + 1)
                            cols(n)

                @block.scalar
                def _(act):
                    act.sem_inc(row_out, 2)
                    act.sem_inc(y_ready, 1)
                    act.wait_ge(tab, 48)
                    with act.Fori(0, B // 2) as i:
                        for j in range(2):
                            act.wait_ge(y_loaded, (i * 2 + j) * 64 + 64)
                            act.wait_ge(row_done, i * (2 * NR) + j * NR + NR)
                            nc.scalar.activation(YY[j][:, :, 0, :], YA[:, :, :].rearrange("p k c -> p c k"), ACT.Copy)
                            nc.scalar.activation(YY[j][:, :, 1, :], YB[:, :, :].rearrange("p k c -> p c k"), ACT.Copy,
                                                 scale=sign[:, 0:1]).then_inc(y_ready, 1)
                            for n in range(j * NR, (j + 1) * NR):
                                act.wait_ge(row_done, i * (2 * NR) + 2 * NR + n + 1)
                                act.wait_ge(col_done, i * (2 * NR) + n + 1)
                                nc.scalar.activation(TS[n % 2][:, :], bank(6 + n % 2, W), ACT.Copy).then_inc(row_out, 1)

                @block.vector
                def _(dve):
                    dve.sem_inc(added, 2)
                    with dve.Fori(0, B // 2) as i:
                        for n in range(2 * NR):
                            G0, cp = n // 4, n % 4
                            xw = XW[G0 % NX][:, :, 2 * cp:2 * cp + 2, :].rearrange("p a c w -> p a (c w)")
                            if cp == 0:
                                dve.wait_ge(loaded[G0 % NX], i * (2 * NG // NX * 32) + G0 // NX * 32 + 32)
                            dve.wait_ge(col_done, i * (2 * NR) + 2 + n + 1)
                            nc.vector.tensor_tensor(xw, xw, psum[:, n % 2 * 1024:n % 2 * 1024 + 1024]
                                                    .rearrange("p (a k) -> p a k", a=2), ALU.add).then_inc(added, 1)

                @block.gpsimd
                def _(pool):
                    pool.sem_inc(x_free, NX)
                    with pool.Fori(0, B // 2) as i:
                        for G0 in range(2 * NG + 1):
                            if G0 < 2 * NG:
                                pool.wait_ge(added, i * (2 * NR) + 2 + 4 * (G0 + 1))
                                for a in range(2):
                                    pool.dma_start(out_rows[a * P:(a + 1) * P, bass.ds(i * 2 * C + G0 * CG, CG), :],
                                                   XW[G0 % NX][:, a, :, :]).then_inc(stored[G0 % NX], 16)
                            if G0 >= 1:
                                G1 = G0 - 1
                                pool.wait_ge(stored[G1 % NX], i * (2 * NG // NX * 32) + (G1 // NX + 1) * 32)
                                pool.sem_inc(x_free, 1)
                    for q in range(NX):
                        pool.wait_ge(stored[q], B * NG // NX * 32)


_INS = ["x", "L0_conv_mlp1_w", "L0_conv_mlp1_b", "L0_conv_mlp2_w", "L0_conv_mlp2_b", "L0_conv_sa1_w",
        "L0_conv_sa2_w", "L0_conv_bn_gamma", "L0_conv_bn_beta", "L1_conv_w1_real", "L1_conv_w1_imag",
        "L1_conv_w2_real", "L1_conv_w2_imag"]


def kernel(**inputs):
    import numpy as _np
    import concourse.bacc as _bacc
    from concourse.bass_utils import run_bass_kernel_spmd as _run

    nc = _bacc.Bacc("TRN2", target_bir_lowering=False, num_devices=1)
    arrays, args = {}, []
    for name in _INS:
        a = _np.ascontiguousarray(inputs[name])
        arrays[name] = a
        args.append(nc.dram_tensor(name, a.shape, F32, kind="ExternalInput").ap())
    arrays["tables"] = CONST
    args.append(nc.dram_tensor("tables", CONST.shape, F32, kind="ExternalInput").ap())
    args.append(nc.dram_tensor("out", (B, C, H, W), F32, kind="ExternalOutput").ap())
    program(nc, *args)
    r = _run(nc, [arrays], core_ids=[0])
    return r.results[0]["out"]
```

```python
from contextlib import ExitStack

import concourse.bass as bass
from concourse import mybir
import numpy as np

F32 = mybir.dt.float32
ACT = mybir.ActivationFunctionType
ALU = mybir.AluOpType
AX_X = mybir.AxisListType.X

P = 128
B, C, H, W = 8, 64, 256, 256
M1, M2 = 32, 32
NPIX = H * W
EPS = 1e-5
HALF = H // 2
NS = 4
DIRS = ((0, 1, 2, 3), (2, 3, 0, 1))

TR = 16
NT = HALF // TR
SP_ = 8
SC = SP_ * W
MR = 2 * SP_
LAYOUT = ((0, 0, 2), (1, 0, 1), (0, 1, 0), (1, 1, 3))
PITCH = W + 1
NM = M1 + 1
NP = (NM + 1) // 2
KX = 2 * M1
CG = 8
NG = C // CG

OFF = {}


def constants():
    parts = []

    def put(name, a):
        a = np.asarray(a, np.float64)
        full = np.zeros((P, a.shape[1]))
        full[: a.shape[0]] = a
        OFF[name] = (sum(q.shape[1] for q in parts), a.shape[1])
        parts.append(full)

    p = np.arange(P)
    c = p % C
    put("ident", np.eye(P))
    put("group", 0.25 * (c[:, None] // 2 == c[None, :] // 2))
    put("chan", 0.5 * (c[:, None] == c[None, :]))
    put("halfones", np.full((P, P), 0.5))
    put("ones", np.ones((P, P)))
    dmask = np.zeros((P, NS))
    for branch in range(2):
        for q in range(4):
            dmask[branch * C + q * 16: branch * C + (q + 1) * 16, DIRS[branch][q]] = 1
    put("dmask", dmask)
    put("rowsel", np.stack([1.0 * (p < C), -1.0 * (p >= C)], 1))
    put("sign", np.stack([np.where(p < C, 1.0, -1.0)] * 2, 1))
    put("npix", np.full((1, B), float(NPIX)))
    th = 2 * np.pi / H
    row = np.arange(H)
    frow = np.zeros((P, 2, C))
    for par in range(2):
        k = np.arange(par, NM, 2)
        a = th * np.outer(np.arange(P), k)
        frow[:, par, :len(k)] = np.cos(a)
        frow[:, par, NP:NP + len(k)] = np.sin(a)
    put("frow", frow.reshape(P, -1))
    col = np.arange(W)
    a = 2 * np.pi / W * np.outer(col, np.arange(M2))
    cc, ss = np.cos(a), np.sin(a)
    fc = np.concatenate([cc, -ss, cc, -ss], 1)
    fs = np.concatenate([-ss, -cc, ss, cc], 1)
    fcol = np.stack([fc, fs], 1).reshape(2, P, 2, 4 * M2).transpose(1, 0, 2, 3)
    put("fcol", fcol.reshape(P, -1))
    kx = np.concatenate([np.arange(M1), np.arange(-M1, 0)])
    ar = th * np.outer(kx, row)
    put("irow", np.concatenate([np.cos(ar), -np.sin(ar)], 0))
    wt = np.where(np.arange(M2) == 0, 1.0, 2.0)[:, None] / NPIX
    ac = 2 * np.pi / W * np.outer(np.arange(M2), col)
    ih = np.concatenate([wt * np.cos(ac), -wt * np.sin(ac)], 0)
    put("icol", np.block([[ih, np.zeros_like(ih)], [np.zeros_like(ih), ih]]))
    return np.concatenate(parts, 1).astype(np.float32)


CONST = constants()


def program(nc, x, w1m, b1m, w2m, b2m, sa1, sa2, gamma, beta, wr1, wi1, wr2, wi2, const, out):
    top = ExitStack()
    with top:
        def sem(name):
            return top.enter_context(nc.semaphore(name))

        x1 = nc.dram_tensor("x1_scratch", (B, C, H, W), F32, kind="Internal").ap()
        xd = nc.dram_tensor("modes_in", (P, B, 2, KX, M2), F32, kind="Internal").ap()
        yd = nc.dram_tensor("modes_out", (2 * B, KX, M2, C), F32, kind="Internal").ap()
        x_bc = x.rearrange("b c h w -> (b c) (h w)")
        x_rows = x.rearrange("b c h w -> (b c) h w")
        x1_rows = x1.rearrange("b c h w -> h (b c) w")
        out_rows = out.rearrange("b c h w -> h (b c) w")

        psum = top.enter_context(nc.psum_tensor("psum", [P, 4096], F32))

        def bank(n, cols=512, parts=P, first=0):
            return psum[first:first + parts, n * 512:n * 512 + cols]

        def sb(ctx, name, shape):
            return ctx.enter_context(nc.sbuf_tensor(name, shape, F32))

        def table(ctx, names):
            t = sb(ctx, "tab_" + "_".join(names), [P, sum(OFF[n][1] for n in names)])
            at, got = 0, {}
            for n in names:
                o, k = OFF[n]
                got[n] = (t[:, at:at + k], const[:, o:o + k])
                at += k
            return got

        params = sb(top, "params", [P, B + 1, 4])
        wall = sb(top, "wall", [P, B + 1, P])
        sums = sb(top, "sums", [P, B * 2 * NT])
        sqs = sb(top, "sqs", [P, B * 2 * NT])
        norm2 = sb(top, "norm2", [P, 2, B])
        mrow = sb(top, "mrow", [1, B * C])

        ph = ExitStack()
        with ph:
            NX = 4
            XT = [sb(ph, f"stat_x{i}", [P, TR * W]) for i in range(NX)]
            stats = sb(ph, "stats", [P, B * NT * 8 * 6])
            mv = sb(ph, "mv", [P, B, 2])
            ecol = sb(ph, "ecol", [P, B * NT * 2])
            erow = sb(ph, "erow", [P, B * 2])
            junk = sb(ph, "junk", [P, W])
            names = ["ident", "group", "chan", "halfones", "ones", "dmask", "rowsel", "npix"]
            T = table(ph, names)
            ident, group, chan, halfones, ones, dmask, rowsel, npix = (T[n][0] for n in names)
            w1d = sb(ph, "w1d", [P, 2, C])
            w2d = sb(ph, "w2d", [C, 2, C])
            sa1s = sb(ph, "sa1s", [C, C])
            sa2s = sb(ph, "sa2s", [P, C])
            b1c = sb(ph, "b1c", [P, 1])
            b1r = sb(ph, "b1r", [1, P])
            vec = sb(ph, "vec", [P, 3])
            w1t = sb(ph, "w1t", [C, P])
            w2t = sb(ph, "w2t", [P, 2, C])
            sa1t = sb(ph, "sa1t", [C, C])
            sa2t = sb(ph, "sa2t", [C, P])
            sm = sb(ph, "sm", [P, 32, B])
            col = sb(ph, "col", [P, 16])
            td = sb(ph, "td", [P, NS, B])
            asb = sb(ph, "asb", [B, C])
            at = sb(ph, "at", [C, B])
            gt = sb(ph, "gt", [C, B])
            soft = sb(ph, "soft", [B, 6, C])
            bart = sb(ph, "bart", [P, B])
            diag = sb(ph, "diag", [C, B, C])
            w2s = sb(ph, "w2s", [P, B, C])
            mb = sb(ph, "mb", [P, B, NS])
            rhs = sb(ph, "rhs", [P, B, NS, C])

            s_x = [sem(f"stat_loaded{i}") for i in range(NX)]
            stat_dve, stat_act = sem("stat_dve_done"), sem("stat_act_done")
            edge_order = sem("edge_order")
            weights = sem("weights_loaded")

            with nc.Block() as block:
                @block.sync
                def _(sp):
                    with sp.Fori(0, B) as b:
                        for t in range(NT):
                            sp.wait_ge(stat_dve, b * NT + t + 1)
                            sp.wait_ge(stat_act, b * NT + t + 1)
                            for s in range(2):
                                r0 = (s * HALF + t * TR) * W
                                sp.dma_start(XT[t % NX][s * C:(s + 1) * C, :],
                                             x_bc[bass.ds(b * C, C), r0:r0 + TR * W]
                                             ).then_inc(s_x[t % NX], 16)

                @block.gpsimd
                def _(pool):
                    for n in names:
                        pool.dma_start(T[n][0], T[n][1]).then_inc(weights, 16)
                    for j in range(2):
                        pool.dma_start(w1d[:, j, :], w1m[0:P, :]).then_inc(weights, 16)
                        pool.dma_start(w2d[:, j, :], w2m).then_inc(weights, 16)
                        for n, v in enumerate((b2m, gamma, beta)):
                            pool.dma_start(vec[j * C:(j + 1) * C, n:n + 1],
                                           v.rearrange("(p a) -> p a", a=1)).then_inc(weights, 16)
                    pool.dma_start(sa1s[:, :], sa1).then_inc(weights, 16)
                    pool.dma_start(sa2s[:, :], sa2).then_inc(weights, 16)
                    pool.dma_start(b1c[:, :], b1m[0:P].rearrange("(p a) -> p a", a=1)).then_inc(weights, 16)
                    pool.dma_start(b1r[:, :], b1m[0:P].rearrange("(a p) -> a p", a=1)).then_inc(weights, 16)
                    pool.memset(wall[:, B, :], 0.0)
                    pool.memset(params[:, B, :], 0.0)
                    pool.wait_ge(weights, 16 * (len(names) + 14))

                @block.scalar
                def _(act):
                    act.sem_inc(stat_act, NX)
                    act.sem_inc(edge_order, 1)
                    with act.Fori(0, B) as b:
                        k = 0
                        for t in range(NT):
                            act.wait_ge(s_x[t % NX], b * (NT // NX * 32) + (t // NX + 1) * 32)
                            xt = XT[t % NX][:, :].rearrange("p (r w) -> p r w", w=W)
                            todo = [(xt[:, :, 0], ecol, b * (NT * 2) + t * 2, TR),
                                    (xt[:, :, W - 1], ecol, b * (NT * 2) + t * 2 + 1, TR)]
                            if t == 0:
                                todo.append((xt[:, 0, :], erow, b * 2, W))
                            if t == NT - 1:
                                todo.append((xt[:, TR - 1, :], erow, b * 2 + 1, W))
                            for src, dst, idx, width in todo:
                                act.wait_ge(edge_order, b * (NT * 2 + 2) + k + 1)
                                act.activation(junk[:, 0:width], src, ACT.Copy,
                                               accum_out=dst[:, bass.ds(idx, 1)]).then_inc(edge_order, 1)
                                k += 1
                            act.wait_ge(edge_order, b * (NT * 2 + 2) + k + 1)
                            act.sem_inc(stat_act, 1)

                @block.vector
                def _(dve):
                    dve.sem_inc(stat_dve, NX)
                    with dve.Fori(0, B) as b:
                        for t in range(NT):
                            dve.wait_ge(s_x[t % NX], b * (NT // NX * 32) + (t // NX + 1) * 32)
                            for q in range(8):
                                last = nc.vector.bn_stats(stats[:, bass.ds(b * (NT * 48) + (t * 8 + q) * 6, 6)],
                                                          XT[t % NX][:, q * 512:(q + 1) * 512])
                            last.then_inc(stat_dve, 1)
                    dve.wait_ge(stat_dve, NX + B * NT)
                    for b in range(B):
                        nc.vector.bn_aggr(mv[:, b, :], stats[:, b * NT * 48:(b + 1) * NT * 48])

            STEPS = ("transposes", "evac_w", "group_mean", "dev", "dev2", "devar", "group_var", "veps",
                     "std", "rstd", "nmean", "edges", "cdiff", "rsel", "rdiff", "cdiffr",
                     "rdiffr", "chan_sums", "cs_copy", "bmean", "bmean8", "var_r", "dev_c", "var_rr", "dev_c2",
                     "bvar", "bsum", "absg1", "absg2", "bn_sums", "bveps", "bstd", "brstd", "wbn", "gwbn",
                     "kscale", "A", "mr", "mrb", "Bneg", "Bias", "npsum", "td", "pooled", "pool_copy", "pool_t",
                     "at", "squeeze", "gelu", "excite", "h0", "hmax", "l0", "exps", "esum", "rsum", "bar",
                     "bar_t", "bart", "shift_in", "z", "zb", "mask", "w2s", "shift_out", "cb", "cbr", "rhs",
                     "mats", "wall")

            def at_(name):
                return STEPS.index(name)

            prep = sem("prep")
            r, nmean, mr = sm[:, 6, :], sm[:, 8, :], sm[:, 11, :]
            k1 = col[:, 12:13]
            mean, var = mv[:, :, 0], mv[:, :, 1]
            with nc.Block() as block:
                @block.tensor
                def _(pe):
                    nc.tensor.transpose(bank(0, P, C), w1d[:, 0, :], ident)
                    nc.tensor.transpose(bank(1, C), w2d[:, :, :].rearrange("p a c -> p (a c)"), ident[0:C, 0:C])
                    nc.tensor.transpose(bank(2, C, C), sa1s[:, :], ident[0:C, 0:C])
                    nc.tensor.transpose(bank(3, P, C), sa2s[:, :], ident).then_inc(prep, 1)
                    pe.wait_ge(prep, at_("group_mean"))
                    nc.tensor.matmul(bank(4, B), group, sm[:, 0, :], start=True, stop=True).then_inc(prep, 1)
                    pe.wait_ge(prep, at_("group_var"))
                    nc.tensor.matmul(bank(5, B), group, sm[:, 3, :], start=True, stop=True).then_inc(prep, 1)
                    pe.wait_ge(prep, at_("chan_sums"))
                    nc.tensor.matmul(bank(6, 3 * B), chan, sm[:, 8:11, :].rearrange("p a b -> p (a b)"),
                                     start=True, stop=True).then_inc(prep, 1)
                    pe.wait_ge(prep, at_("bn_sums"))
                    nc.tensor.matmul(psum[:, 3584:3585], chan, col[:, 4:5], start=True, stop=True)
                    nc.tensor.matmul(psum[:, 3585:3586], halfones, col[:, 6:7], start=True,
                                     stop=True).then_inc(prep, 1)
                    pe.wait_ge(prep, at_("pooled"))
                    for q in range(4):
                        j = slice(q * 16, q * 16 + 16)
                        k = slice(C + q * 16, C + q * 16 + 16)
                        o = psum[0:B, j]
                        nc.tensor.matmul(o, td[0:C, DIRS[0][q], :], w1t[:, j], start=True, stop=False)
                        nc.tensor.matmul(o, td[0:C, DIRS[1][q], :], w1t[:, k], start=False, stop=False)
                        nc.tensor.matmul(o, npix[0:1, :], b1r[:, j], start=False, stop=False)
                        last = nc.tensor.matmul(o, npix[0:1, :], b1r[:, k], start=False, stop=True)
                    last.then_inc(prep, 1)
                    pe.wait_ge(prep, at_("pool_t"))
                    nc.tensor.transpose(bank(1, B, C), asb[:, :], ident[0:B, 0:B]).then_inc(prep, 1)
                    pe.wait_ge(prep, at_("squeeze"))
                    nc.tensor.matmul(bank(2, B, C), sa1t[:, :], at[:, :], start=True, stop=True).then_inc(prep, 1)
                    pe.wait_ge(prep, at_("excite"))
                    nc.tensor.matmul(bank(3, P, B), gt[:, :], sa2t[:, :], start=True, stop=True).then_inc(prep, 1)
                    pe.wait_ge(prep, at_("bar_t"))
                    nc.tensor.transpose(bank(0, B), soft[:, 1:3, :].rearrange("p a c -> p (a c)"),
                                        ident[0:B, 0:B]).then_inc(prep, 1)
                    pe.wait_ge(prep, at_("shift_in"))
                    nc.tensor.matmul(bank(1, B), w1t[:, :], sm[0:C, 12, :], start=True, stop=True)
                    nc.tensor.matmul(bank(2), ones[0:C, :], diag[:, :, :].rearrange("p b c -> p (b c)"),
                                     start=True, stop=True).then_inc(prep, 1)
                    pe.wait_ge(prep, at_("shift_out"))
                    nc.tensor.matmul(bank(3, B), w2t[:, :, :].rearrange("p a c -> p (a c)"), sm[:, 14, :],
                                     start=True, stop=True).then_inc(prep, 1)
                    pe.wait_ge(prep, at_("mats"))
                    for b in range(B):
                        last = nc.tensor.matmul(psum[:, b * 256:(b + 1) * 256],
                                                w1d[:, :, :].rearrange("p a c -> p (a c)"),
                                                rhs[:, b, :, :].rearrange("p d o -> p (d o)"),
                                                start=True, stop=True)
                    last.then_inc(prep, 1)

                @block.scalar
                def _(act):
                    act.wait_ge(prep, at_("std"))
                    act.activation(sm[:, 5, :], sm[:, 4, :], ACT.Sqrt).then_inc(prep, 1)
                    act.wait_ge(prep, at_("bstd"))
                    act.activation(col[:, 3:4], col[:, 2:3], ACT.Sqrt).then_inc(prep, 1)
                    act.wait_ge(prep, at_("gelu"))
                    act.activation(gt[:, :], bank(2, B, C), ACT.Gelu).then_inc(prep, 1)
                    act.wait_ge(prep, at_("exps"))
                    act.activation(soft[:, 3:5, :], soft[:, 1:3, :], ACT.Exp).then_inc(prep, 1)

                @block.vector
                def _(dve):
                    v = nc.vector
                    dve.wait_ge(prep, at_("evac_w"))
                    v.tensor_copy(w1t[:, :], bank(0, P, C))
                    v.tensor_copy(w2t[:, 0, :], bank(1, C))
                    v.tensor_copy(w2t[:, 1, :], bank(1, C))
                    v.tensor_copy(sa1t[:, :], bank(2, C, C))
                    v.tensor_copy(sa2t[:, :], bank(3, P, C))
                    v.tensor_copy(sm[:, 0, :], mean).then_inc(prep, 1)
                    dve.wait_ge(prep, at_("dev"))
                    v.scalar_tensor_tensor(out=sm[:, 1, :], in0=bank(4, B), scalar=-1.0, in1=sm[:, 0, :], op0=ALU.mult, op1=ALU.add).then_inc(prep, 1)
                    dve.wait_ge(prep, at_("dev2"))
                    v.tensor_tensor(sm[:, 2, :], sm[:, 1, :], sm[:, 1, :], ALU.mult).then_inc(prep, 1)
                    dve.wait_ge(prep, at_("devar"))
                    v.tensor_tensor(sm[:, 3, :], sm[:, 2, :], var, ALU.add).then_inc(prep, 1)
                    dve.wait_ge(prep, at_("veps"))
                    v.tensor_scalar(sm[:, 4, :], bank(5, B), EPS, None, ALU.add).then_inc(prep, 1)
                    dve.wait_ge(prep, at_("rstd"))
                    v.reciprocal(r, sm[:, 5, :]).then_inc(prep, 1)
                    dve.wait_ge(prep, at_("nmean"))
                    v.tensor_tensor(nmean, sm[:, 1, :], r, ALU.mult).then_inc(prep, 1)
                    dve.wait_ge(prep, at_("edges"))
                    v.reduce_sum(sm[:, 16:18, :], ecol[:, :].rearrange("p (b t e) -> p e b t", t=NT, e=2), axis=AX_X).then_inc(prep, 1)
                    dve.wait_ge(prep, at_("cdiff"))
                    v.tensor_tensor(sm[:, 18, :], sm[:, 16, :], sm[:, 17, :], ALU.subtract).then_inc(prep, 1)
                    dve.wait_ge(prep, at_("rsel"))
                    v.tensor_scalar(sm[:, 19, :], erow[:, 0::2], rowsel[:, 0:1], None, ALU.mult).then_inc(prep, 1)
                    dve.wait_ge(prep, at_("rdiff"))
                    v.scalar_tensor_tensor(out=sm[:, 20, :], in0=erow[:, 1::2], scalar=rowsel[:, 1:2], in1=sm[:, 19, :], op0=ALU.mult, op1=ALU.add).then_inc(prep, 1)
                    dve.wait_ge(prep, at_("cdiffr"))
                    v.tensor_tensor(sm[:, 9, :], sm[:, 18, :], r, ALU.mult).then_inc(prep, 1)
                    dve.wait_ge(prep, at_("rdiffr"))
                    v.tensor_tensor(sm[:, 10, :], sm[:, 20, :], r, ALU.mult).then_inc(prep, 1)
                    dve.wait_ge(prep, at_("cs_copy"))
                    v.tensor_copy(sm[:, 21:24, :].rearrange('p a b -> p (a b)'), bank(6, 3 * B)).then_inc(prep, 1)
                    dve.wait_ge(prep, at_("bmean"))
                    v.reduce_sum(col[:, 0:1], sm[:, 21, :], axis=AX_X).then_inc(prep, 1)
                    dve.wait_ge(prep, at_("bmean8"))
                    v.tensor_scalar(col[:, 1:2], col[:, 0:1], 1.0 / B, None, ALU.mult).then_inc(prep, 1)
                    dve.wait_ge(prep, at_("var_r"))
                    v.tensor_tensor(sm[:, 24, :], var, r, ALU.mult).then_inc(prep, 1)
                    dve.wait_ge(prep, at_("dev_c"))
                    v.tensor_scalar(sm[:, 25, :], nmean, col[:, 1:2], None, ALU.subtract).then_inc(prep, 1)
                    dve.wait_ge(prep, at_("var_rr"))
                    v.tensor_tensor(sm[:, 26, :], sm[:, 24, :], r, ALU.mult).then_inc(prep, 1)
                    dve.wait_ge(prep, at_("dev_c2"))
                    v.tensor_tensor(sm[:, 27, :], sm[:, 25, :], sm[:, 25, :], ALU.mult).then_inc(prep, 1)
                    dve.wait_ge(prep, at_("bvar"))
                    v.tensor_tensor(sm[:, 28, :], sm[:, 26, :], sm[:, 27, :], ALU.add).then_inc(prep, 1)
                    dve.wait_ge(prep, at_("bsum"))
                    v.reduce_sum(col[:, 4:5], sm[:, 28, :], axis=AX_X).then_inc(prep, 1)
                    dve.wait_ge(prep, at_("absg1"))
                    v.tensor_scalar(col[:, 5:6], vec[:, 1:2], -1.0, None, ALU.mult).then_inc(prep, 1)
                    dve.wait_ge(prep, at_("absg2"))
                    v.tensor_tensor(col[:, 6:7], col[:, 5:6], vec[:, 1:2], ALU.max).then_inc(prep, 1)
                    dve.wait_ge(prep, at_("bveps"))
                    v.tensor_scalar(col[:, 2:3], psum[:, 3584:3585], 1.0 / B, EPS, ALU.mult, ALU.add).then_inc(prep, 1)
                    dve.wait_ge(prep, at_("brstd"))
                    v.reciprocal(col[:, 11:12], col[:, 3:4]).then_inc(prep, 1)
                    dve.wait_ge(prep, at_("wbn"))
                    v.reciprocal(col[:, 7:8], psum[:, 3585:3586]).then_inc(prep, 1)
                    dve.wait_ge(prep, at_("gwbn"))
                    v.tensor_tensor(col[:, 8:9], col[:, 7:8], col[:, 6:7], ALU.mult).then_inc(prep, 1)
                    dve.wait_ge(prep, at_("kscale"))
                    v.tensor_tensor(col[:, 9:10], col[:, 8:9], vec[:, 1:2], ALU.mult)
                    v.tensor_tensor(col[:, 10:11], col[:, 8:9], vec[:, 2:3], ALU.mult).then_inc(prep, 1)
                    dve.wait_ge(prep, at_("A"))
                    v.tensor_tensor(k1, col[:, 11:12], col[:, 9:10], ALU.mult).then_inc(prep, 1)
                    dve.wait_ge(prep, at_("mr"))
                    v.tensor_scalar(params[:, 0:B, 0], r, k1, None, ALU.mult)
                    v.tensor_tensor(mr, bank(4, B), r, ALU.mult).then_inc(prep, 1)
                    dve.wait_ge(prep, at_("mrb"))
                    v.tensor_scalar(sm[:, 12, :], mr, -1.0, None, ALU.mult)
                    v.tensor_tensor(col[:, 13:14], k1, col[:, 1:2], ALU.mult).then_inc(prep, 1)
                    dve.wait_ge(prep, at_("Bneg"))
                    v.tensor_tensor(col[:, 14:15], col[:, 10:11], col[:, 13:14], ALU.subtract).then_inc(prep, 1)
                    dve.wait_ge(prep, at_("Bias"))
                    v.tensor_copy(params[:, 0:B, 1], col[:, 14:15].to_broadcast([P, B]))
                    v.tensor_copy(params[:, 0:B, 2], bank(4, B)).then_inc(prep, 1)
                    dve.wait_ge(prep, at_("npsum"))
                    v.tensor_scalar(sm[:, 31, :], sm[:, 21, :], float(NPIX), None, ALU.mult)
                    v.tensor_tensor(diag[:, :, :], ident[0:C, 0:C].unsqueeze(1).to_broadcast([C, B, C]),
                                    sm[0:C, 6, :].unsqueeze(2).to_broadcast([C, B, C]), ALU.mult).then_inc(prep, 1)
                    dve.wait_ge(prep, at_("td"))
                    for d, (edge, sg) in enumerate(((23, 2.0), (23, -2.0), (22, 2.0), (22, -2.0))):
                        last = v.scalar_tensor_tensor(out=td[:, d, :], in0=sm[:, edge, :], scalar=sg,
                                                      in1=sm[:, 31, :], op0=ALU.mult, op1=ALU.add)
                    last.then_inc(prep, 1)
                    dve.wait_ge(prep, at_("pool_copy"))
                    v.tensor_copy(asb[:, :], psum[0:B, 0:C]).then_inc(prep, 1)
                    dve.wait_ge(prep, at_("at"))
                    v.tensor_copy(at[:, :], bank(1, B, C)).then_inc(prep, 1)
                    dve.wait_ge(prep, at_("h0"))
                    v.tensor_copy(soft[:, 0, :], bank(3, C, B)).then_inc(prep, 1)
                    dve.wait_ge(prep, at_("hmax"))
                    v.tensor_tensor(soft[:, 5, :], bank(3, P, B)[:, C:P], soft[:, 0, :], ALU.max).then_inc(prep, 1)
                    dve.wait_ge(prep, at_("l0"))
                    v.tensor_tensor(soft[:, 1, :], soft[:, 0, :], soft[:, 5, :], ALU.subtract)
                    v.tensor_tensor(soft[:, 2, :], bank(3, P, B)[:, C:P], soft[:, 5, :], ALU.subtract).then_inc(prep, 1)
                    dve.wait_ge(prep, at_("esum"))
                    v.tensor_tensor(soft[:, 0, :], soft[:, 3, :], soft[:, 4, :], ALU.add).then_inc(prep, 1)
                    dve.wait_ge(prep, at_("rsum"))
                    v.reciprocal(soft[:, 5, :], soft[:, 0, :]).then_inc(prep, 1)
                    dve.wait_ge(prep, at_("bar"))
                    v.tensor_tensor(soft[:, 1, :], soft[:, 3, :], soft[:, 5, :], ALU.mult)
                    v.tensor_tensor(soft[:, 2, :], soft[:, 4, :], soft[:, 5, :], ALU.mult).then_inc(prep, 1)
                    dve.wait_ge(prep, at_("bart"))
                    v.tensor_copy(bart[:, :], bank(0, B)).then_inc(prep, 1)
                    dve.wait_ge(prep, at_("z"))
                    v.tensor_scalar(sm[:, 13, :], bank(1, B), b1c[:, :], None, ALU.add).then_inc(prep, 1)
                    dve.wait_ge(prep, at_("zb"))
                    v.tensor_tensor(sm[:, 14, :], sm[:, 13, :], bart[:, :], ALU.mult).then_inc(prep, 1)
                    dve.wait_ge(prep, at_("mask"))
                    v.tensor_tensor(mb[:, :, :], bart[:, :].unsqueeze(2).to_broadcast([P, B, NS]),
                                    dmask.unsqueeze(1).to_broadcast([P, B, NS]), ALU.mult).then_inc(prep, 1)
                    dve.wait_ge(prep, at_("w2s"))
                    v.tensor_tensor(w2s[:, :, :], bank(2).rearrange('p (b c) -> p b c', b=B),
                                    w2t[:, 0, :].unsqueeze(1).to_broadcast([P, B, C]), ALU.mult).then_inc(prep, 1)
                    dve.wait_ge(prep, at_("cb"))
                    v.tensor_scalar(sm[:, 15, :], bank(3, B), vec[:, 0:1], None, ALU.add).then_inc(prep, 1)
                    dve.wait_ge(prep, at_("cbr"))
                    v.tensor_tensor(params[:, 0:B, 3], sm[:, 15, :], r, ALU.mult).then_inc(prep, 1)
                    dve.wait_ge(prep, at_("rhs"))
                    for b in range(B):
                        last = v.tensor_tensor(rhs[:, b, :, :], w2s[:, b, :].unsqueeze(1).to_broadcast([P, NS, C]),
                                               mb[:, b, :].unsqueeze(2).to_broadcast([P, NS, C]), ALU.mult)
                    last.then_inc(prep, 1)
                    dve.wait_ge(prep, at_("wall"))
                    mats = psum[:, 0:B * 256].rearrange("p (b d o) -> p b d o", b=B, d=NS)
                    for b in range(B):
                        for half, slot, d in LAYOUT:
                            h = slice(half * C, (half + 1) * C)
                            v.tensor_scalar(wall[h, b, slot * C:(slot + 1) * C], mats[h, b, d, :],
                                            sm[h, 6, b:b + 1], None, ALU.mult)

        ph = ExitStack()
        with ph:
            NX = 4
            XT = [sb(ph, f"mix_x{i}", [P, MR + 1, PITCH]) for i in range(NX)]
            XC = [sb(ph, f"centred{i}", [P, SC]) for i in range(NX)]
            G = [sb(ph, f"gated{i}", [P, SC]) for i in range(NX)]
            XO = [sb(ph, f"mix_out{i}", [P, SC]) for i in range(2)]
            SQ = sb(ph, "square", [P, SC])
            one = sb(ph, "one", [P, MR + 1])
            wcur = [sb(ph, f"wcur{i}", [P, P]) for i in range(2)]
            pcur = [sb(ph, f"pcur{i}", [P, 6]) for i in range(2)]
            loaded = [sem(f"mix_loaded{i}") for i in range(NX)]
            stored = [sem(f"mix_stored{i}") for i in range(2)]
            one_set = sem("mix_one_set")
            doubled, padded, batch_ready = sem("mix_doubled"), sem("mix_padded"), sem("mix_batch_ready")
            xc_done, sig_done, conv_done, sq_done = (sem("mix_" + n) for n in ("xc", "sig", "conv", "sq"))
            h_done, o_done, xc_dve = sem("mix_h"), sem("mix_o"), sem("mix_xc_dve")
            NB = H // MR
            NI = 2 * NB
            ITER = B // 2
            x1_par = x1.rearrange("b c (r e) w -> (b c) r e w", e=2)

            def split(n):
                return n % 2 == 1

            def loaded_by(i, n):
                q, t = n % NX, n % NB
                edge = 16 if q in (0, NX - 1) else 0
                batch = NB // NX * 32 + edge
                return i * (2 * batch) + n // NB * batch + (t // NX + 1) * 32 + (edge if q == 0 or t == NB - 1 else 0)

            def iterations(engine, body):
                with engine.Fori(0, ITER - 1) as i:
                    body(i, False)
                body(ITER - 1, True)

            with nc.Block() as block:
                @block.sync
                def _(sp):
                    with sp.Fori(0, ITER) as i:
                        for n in range(NI):
                            ch = bass.ds((i * 2 + n // NB) * C, C)
                            t, xt = n % NB, XT[n % NX]
                            sp.wait_ge(conv_done, i * NI + n + 1)
                            sp.wait_ge(sig_done, i * NI + n + 1)
                            r0 = t * MR - 1
                            lo = max(r0, 0)
                            sp.dma_start(xt[0:C, lo - r0:MR // 2 + 1, 1:W + 1],
                                         x_rows[ch, lo:r0 + MR // 2 + 1, :]).then_inc(loaded[n % NX], 16)
                            hi = min(r0 + MR + 2, H)
                            sp.dma_start(xt[C:P, MR // 2:hi - r0 - 1, 0:W],
                                         x_rows[ch, r0 + 1 + MR // 2:hi, :]).then_inc(loaded[n % NX], 16)
                            if t == 0:
                                sp.dma_start(xt[0:C, 0:1, 1:W + 1], x_rows[ch, 0:1, :]).then_inc(loaded[n % NX], 16)
                            if t == NB - 1:
                                sp.dma_start(xt[C:P, MR:MR + 1, 0:W], x_rows[ch, H - 1:H, :]
                                             ).then_inc(loaded[n % NX], 16)
                    for k in range(2):
                        sp.wait_ge(stored[k], B * NB // 2 * 32 + 16)

                @block.gpsimd
                def _(pool):
                    nc.gpsimd.memset(one[:, :], 1.0).then_inc(one_set, 1)
                    pool.wait_ge(one_set, 1)

                    def pad(i, n):
                        pool.wait_ge(doubled, i * NI + n + 1)
                        for half, to, of in ((0, 0, 1), (1, W, W - 1)):
                            h = slice(half * C, (half + 1) * C)
                            last = nc.gpsimd.tensor_tensor(XT[n % NX][h, :, to], XT[n % NX][h, :, of],
                                                           one[h, :], ALU.mult)
                        last.then_inc(padded, 1)

                    pad(0, 0)
                    pad(0, 1)

                    def body(i, final):
                        for n in range(NI - 2 * final):
                            pad(i, n + 2)

                    iterations(pool, body)

                @block.tensor
                def _(pe):
                    pe.sem_inc(conv_done, NX)
                    with pe.Fori(0, ITER) as i:
                        for n in range(NI):
                            j, k = n // NB, n % 2
                            if n % NB == 0:
                                pe.wait_ge(batch_ready, i * 2 + j + 1)
                            pe.wait_ge(padded, i * NI + n + 1)
                            pe.wait_ge(h_done, i * NI + n + 1)
                            for m in range(2):
                                for q in range(4):
                                    for par in range(2):
                                        r0 = 1 - m + par + q * 4
                                        last = nc.tensor.matmul(bank(k * 4 + q, 512, C, par * C),
                                                                wcur[j][:, m * C:(m + 1) * C],
                                                                XT[n % NX][:, r0:r0 + 3:2, m:m + W],
                                                                start=(m == 0), stop=(m == 1))
                            last.then_inc(conv_done, 1)

                @block.scalar
                def _(act):
                    act.sem_inc(sq_done, 2)
                    act.sem_inc(sig_done, NX)
                    for k in range(2):
                        act.sem_inc(stored[k], 16)

                    def gate(i, n):
                        j = n // NB % 2
                        if n % NB == 0:
                            act.wait_ge(batch_ready, i * 2 + n // NB + 1)
                        act.wait_ge(padded, i * NI + n + 1)
                        act.wait_ge(o_done, i * NI + n + 1)
                        for half in range(1 if split(n) else 2):
                            h = slice(half * C, (half + 1) * C)
                            last = nc.scalar.activation(
                                XC[n % NX][h, :].rearrange("p (r w) -> p r w", w=W),
                                XT[n % NX][h, 1:MR:2, 1 - half:1 - half + W],
                                ACT.Identity, bias=pcur[j][h, 4:5])
                        last.then_inc(xc_done, 1)
                        act.wait_ge(xc_done, i * NI + n + 1)
                        if split(n):
                            act.wait_ge(xc_dve, i * NB + n // 2 + 1)
                        nc.scalar.activation(G[n % NX][:, :], XC[n % NX][:, :], ACT.Sigmoid,
                                             bias=pcur[j][:, 1:2], scale=pcur[j][:, 0:1]).then_inc(sig_done, 1)

                    gate(0, 0)
                    gate(0, 1)

                    def body(i, final):
                        for n in range(NI):
                            j, k, y0 = n // NB, n % 2, n % NB * SP_
                            if not (final and n + 2 >= NI):
                                gate(i, n + 2)
                            act.wait_ge(o_done, i * NI + NX + n + 1)
                            for par in range(2):
                                act.dma_start(x1_par[bass.ds((i * 2 + j) * C, C), y0:y0 + SP_, par, :],
                                              XO[k][par * C:(par + 1) * C, :].rearrange("p (r w) -> p r w", w=W)
                                              ).then_inc(stored[k], 16)
                            act.wait_ge(sq_done, i * NI + n + 2)
                            nc.scalar.activation(SQ[:, :], XO[k][:, :], ACT.Square,
                                                 accum_out=sqs[:, bass.ds(i * NI + n, 1)]).then_inc(sq_done, 1)

                    iterations(act, body)

                @block.vector
                def _(dve):
                    def take(b, j):
                        nc.vector.tensor_copy(wcur[j][:, :], wall[:, bass.ds(b, 1), :].rearrange("p a k -> p (a k)"))
                        nc.vector.tensor_copy(pcur[j][:, 0:4], params[:, bass.ds(b, 1), :].rearrange("p a k -> p (a k)"))
                        nc.vector.tensor_scalar(pcur[j][:, 4:5],
                                                params[:, bass.ds(b, 1), 2:3].rearrange("p a k -> p (a k)"),
                                                -1.0, None, ALU.mult).then_inc(batch_ready, 1)

                    def up(i, n):
                        dve.wait_ge(loaded[n % NX], loaded_by(i, n))
                        xt, h = XT[n % NX], MR // 2
                        nc.vector.tensor_copy(xt[C:P, 0:h, 0:W], xt[0:C, 1:h + 1, 1:W + 1])

                    def down(n):
                        xt, h = XT[n % NX], MR // 2
                        nc.vector.tensor_copy(xt[0:C, h + 1:MR + 1, 1:W + 1], xt[C:P, h:MR, 0:W]).then_inc(doubled, 1)

                    def centre(i, n):
                        j = n // NB % 2
                        dve.wait_ge(doubled, i * NI + n + 1)
                        nc.vector.tensor_scalar(XC[n % NX][C:P, :].rearrange("p (r w) -> p r w", w=W),
                                                XT[n % NX][C:P, 1:MR:2, 0:W],
                                                pcur[j][C:P, 4:5], None, ALU.add).then_inc(xc_dve, 1)

                    dve.sem_inc(h_done, 2)
                    dve.sem_inc(o_done, NX)
                    take(0, 0)
                    dve.wait_ge(batch_ready, 1)
                    for n in range(2):
                        up(0, n)
                        down(n)
                    centre(0, 1)

                    def body(i, final):
                        for n in range(NI):
                            j, k = n // NB, n % 2
                            ahead = not (final and n + 2 >= NI)
                            if ahead:
                                up(i, n + 2)
                            dve.wait_ge(conv_done, i * NI + NX + n + 1)
                            dve.wait_ge(sig_done, i * NI + NX + n + 1)
                            nc.vector.scalar_tensor_tensor(out=G[n % NX][:, :], in0=psum[:, k * SC:(k + 1) * SC],
                                                           scalar=pcur[j][:, 3:4], in1=G[n % NX][:, :],
                                                           op0=ALU.add, op1=ALU.mult).then_inc(h_done, 1)
                            if ahead:
                                down(n + 2)
                            dve.wait_ge(h_done, i * NI + 2 + n + 1)
                            dve.wait_ge(stored[k], i * (NB * 32) + n // 2 * 32 + 16)
                            dve.wait_ge(sq_done, i * NI + n + 1)
                            nc.vector.scalar_tensor_tensor(out=XO[k][:, :], in0=G[n % NX][:, :],
                                                           scalar=1.0, in1=XC[n % NX][:, :],
                                                           op0=ALU.add, op1=ALU.mult,
                                                           accum_out=sums[:, bass.ds(i * NI + n, 1)]
                                                           ).then_inc(o_done, 1)
                            if ahead and split(n + 2):
                                centre(i, n + 2)
                            if n % NB == NB // 2:
                                take(i * 2 + j + 1, 1 - j)
                                dve.wait_ge(batch_ready, i * 2 + j + 2)

                    iterations(dve, body)

        ph = ExitStack()
        with ph:
            T = table(ph, ["group", "ident"])
            sv = sb(ph, "norm2_values", [P, 10, B])
            n2_tab, n2 = sem("norm2_table"), sem("norm2_steps")
            with nc.Block() as block:
                @block.sync
                def _(sp):
                    for n in ("group", "ident"):
                        sp.dma_start(*T[n]).then_inc(n2_tab, 16)

                @block.tensor
                def _(pe):
                    pe.wait_ge(n2_tab, 32)
                    for b in range(B):
                        nc.tensor.matmul(psum[0:1, 512 + b * C:512 + (b + 1) * C], params[0:C, b, 2:3],
                                         T["ident"][0][0:C, 0:C], start=True, stop=True)
                    pe.wait_ge(n2, 2)
                    nc.tensor.matmul(bank(0, 2 * B), T["group"][0], sv[:, 2:4, :].rearrange("p a b -> p (a b)"),
                                     start=True, stop=True).then_inc(n2, 1)

                @block.scalar
                def _(act):
                    act.wait_ge(n2, 6)
                    nc.scalar.activation(sv[:, 7, :], sv[:, 6, :], ACT.Sqrt).then_inc(n2, 1)

                @block.vector
                def _(dve):
                    v = nc.vector
                    inv = 1.0 / (HALF * W)
                    v.reduce_sum(sv[:, 0, :], sums[:, :].rearrange("p (b n) -> p b n", b=B), axis=AX_X)
                    v.reduce_sum(sv[:, 1, :], sqs[:, :].rearrange("p (b n) -> p b n", b=B), axis=AX_X).then_inc(n2, 1)
                    dve.wait_ge(n2, 1)
                    v.tensor_scalar(sv[:, 2, :], sv[:, 0, :], inv, None, ALU.mult)
                    v.tensor_scalar(sv[:, 3, :], sv[:, 1, :], inv, None, ALU.mult).then_inc(n2, 1)
                    dve.wait_ge(n2, 3)
                    v.tensor_copy(sv[:, 4, :], bank(0, B))
                    v.tensor_scalar(mrow[:, :], bank(1, B * C, 1), float(NPIX), None, ALU.mult).then_inc(n2, 1)
                    dve.wait_ge(n2, 4)
                    v.tensor_tensor(sv[:, 5, :], sv[:, 4, :], sv[:, 4, :], ALU.mult).then_inc(n2, 1)
                    dve.wait_ge(n2, 5)
                    v.scalar_tensor_tensor(out=sv[:, 6, :], in0=bank(0, 2 * B)[:, B:], scalar=EPS, in1=sv[:, 5, :],
                                           op0=ALU.add, op1=ALU.subtract).then_inc(n2, 1)
                    dve.wait_ge(n2, 7)
                    v.reciprocal(norm2[:, 0, :], sv[:, 7, :]).then_inc(n2, 1)
                    dve.wait_ge(n2, 8)
                    v.scalar_tensor_tensor(out=norm2[:, 1, :], in0=sv[:, 4, :], scalar=-float(NPIX),
                                           in1=norm2[:, 0, :], op0=ALU.mult, op1=ALU.mult)

        KEPT = 4
        x1_kept = [sb(top, f"x1_tile{i}", [P, 2, CG, W]) for i in range(KEPT)]
        ph = ExitStack()
        with ph:
            T = table(ph, ["ident", "frow", "fcol"])
            ident = T["ident"][0]
            frow = T["frow"][0].rearrange("p (a m) -> p a m", a=2)
            fcol = T["fcol"][0].rearrange("p (a k m) -> p a k m", a=2, k=2)
            NX, XW = KEPT, x1_kept
            ED = [[sb(ph, f"fwd_{n}{i}", [P, CG, W]) for n in ("sum", "diff")] for i in range(2)]
            RS = [sb(ph, f"fwd_rows{i}", [P, 512]) for i in range(2)]
            A = [sb(ph, f"fwd_cols{i}", [P, 2, 4 * NP, C]) for i in range(2)]
            XB = sb(ph, "fwd_modes", [C, 3, KX, M2])
            ncur = sb(ph, "ncur", [P, 2])
            tab, loaded = sem("fwd_tables"), [sem(f"fwd_loaded{i}") for i in range(NX)]
            sum_done, diff_done = sem("fwd_sum"), sem("fwd_diff")
            row_done, row_out, tr_done, tr_out = (sem("fwd_" + n) for n in ("row", "row_out", "tr", "tr_out"))
            col_done, col_act, col_dve = (sem("fwd_" + n) for n in ("col", "col_act", "col_dve"))
            cur, neg_done, modes_stored = (sem("fwd_" + n) for n in ("cur", "neg", "stored"))
            NR = C // 2
            PARTS = 5
            ON_ACT, ON_DVE = (0, 2), (1, 3, 4)

            def part_after(n):
                g = n % NR
                return g // 4 + 1 if g % 4 == 3 and g // 4 + 1 < PARTS else None

            def copy_after(n):
                g = n % NR
                return g // 4 if g % 4 == 2 and g // 4 < PARTS else None

            with nc.Block() as block:
                @block.sync
                def _(sp):
                    for n in ("ident", "frow", "fcol"):
                        sp.dma_start(*T[n]).then_inc(tab, 16)
                    with sp.Fori(0, B // 2) as i:
                        for G0 in range(2 * NG):
                            sp.wait_ge(sum_done, i * (2 * NG) + G0 + 1)
                            sp.wait_ge(diff_done, i * (2 * NG) + G0 + 1)
                            for a in range(2):
                                sp.dma_start(XW[G0 % NX][:, a, :, :],
                                             x1_rows[a * P:(a + 1) * P, bass.ds(i * 2 * C + G0 * CG, CG), :]
                                             ).then_inc(loaded[G0 % NX], 16)

                def loaded_by(i, G0):
                    return i * (2 * NG // NX * 32) + (G0 // NX + 1) * 32

                @block.tensor
                def _(pe):
                    pe.sem_inc(row_done, 8)
                    pe.sem_inc(tr_done, 2)
                    pe.wait_ge(tab, 48)

                    def rows(i, n):
                        G0, cp = n // 4, n % 4
                        if cp == 0:
                            pe.wait_ge(sum_done, i * (2 * NG) + G0 + NX + 1)
                            pe.wait_ge(diff_done, i * (2 * NG) + G0 + NX + 1)
                        pe.wait_ge(row_out, i * (2 * NR) + n + 1)
                        for par in range(2):
                            last = nc.tensor.matmul(bank(n % 2, 512, C, par * C), frow[:, par, :],
                                                    ED[G0 % 2][par][:, 2 * cp:2 * cp + 2, :],
                                                    start=True, stop=True)
                        last.then_inc(row_done, 1)

                    def transposes(i, n):
                        pe.wait_ge(row_out, i * (2 * NR) + 2 + n + 1)
                        pe.wait_ge(tr_out, i * (2 * NR) + n + 1)
                        for q in range(4):
                            at = (2 + n % 2) * 512 + q * P
                            last = nc.tensor.transpose(psum[:, at:at + P], RS[n % 2][:, q * P:(q + 1) * P], ident)
                        last.then_inc(tr_done, 1)

                    def columns(c, buf, m, first=False):
                        if m == 0:
                            pe.wait_ge(tr_out, c * NR + NR + 2)
                            if not first:
                                pe.wait_ge(col_act, c * len(ON_ACT))
                                pe.wait_ge(col_dve, c * len(ON_DVE))
                        if m == 4:
                            pe.wait_ge(col_act, c * len(ON_ACT) + 1)
                        for p in range(4 * m, min(4 * m + 4, 17)):
                            wide = 2 if p < 16 else 1
                            at = (4 + m % 4) * 512 + p % 4 * P
                            for q in range(4):
                                a, k = q // 2, q % 2
                                mode = k * 2 * NP + 2 * p
                                last = nc.tensor.matmul(
                                    psum[0:wide * C, at:at + P],
                                    A[buf][:, a, mode:mode + wide, :].rearrange("p m c -> p (m c)"),
                                    fcol[:, a, k, :], start=(q == 0), stop=(q == 3))
                        last.then_inc(col_done, 1)

                    def body(i, first):
                        for j in range(2):
                            c, skip = i * 2 + j - 1, first and j == 0
                            one = first and j == 1
                            if j == 1:
                                rows(i, NR)
                            if not skip:
                                columns(c, 1 - j, 0, one)
                            if j == 0:
                                rows(i, 0)
                            for n in range(j * NR, (j + 1) * NR):
                                m = None if skip else part_after(n)
                                if n + 1 < (j + 1) * NR:
                                    rows(i, n + 1)
                                transposes(i, n)
                                if m is not None:
                                    columns(c, 1 - j, m, one)

                    body(0, True)
                    with pe.Fori(1, B // 2) as i:
                        body(i, False)
                    for m in range(PARTS):
                        columns(B - 1, 1, m)

                def col_copies(m):
                    if m == 4:
                        return [(0, 0, 1, 1, 63)]
                    got = []
                    for par in range(2):
                        k = 8 * m + par
                        got.append((par, 0, 4, 0, k))
                        if k == 0:
                            got.append((par, 1, 3, 1, 31 + 2))
                        else:
                            got.append((par, 0, 4, 1, 31 + k))
                    return got

                def col_views(m, par, first, count, sign, pos):
                    src = psum[par * C:(par + 1) * C, (4 + m % 4) * 512:(5 + m % 4) * 512] \
                        .rearrange("p (s g r k) -> p s g r k", s=4, g=2, r=2)[:, first:first + count, sign, :, :]
                    dst = XB[:, 0:2, pos:pos + 2 * count - 1:2, :].rearrange("p r s k -> p s r k")
                    return dst, src

                @block.scalar
                def _(act):
                    act.sem_inc(row_out, 2)

                    def copies(c, m, first=False):
                        if m == ON_ACT[0]:
                            act.wait_ge(cur, c + 1)
                            if not first:
                                act.wait_ge(modes_stored, c * 48)
                        act.wait_ge(col_done, c * PARTS + m + 1)
                        for par, slot, count, sign, pos in col_copies(m):
                            dst, src = col_views(m, par, slot, count, sign, pos)
                            last = nc.scalar.activation(dst, src, ACT.Copy, scale=ncur[par * C:(par + 1) * C, 0:1])
                        last.then_inc(col_act, 1)

                    def store(c, cs):
                        act.wait_ge(neg_done, c + 1)
                        for p0, r, q, w in ((0, 0, 0, 2), (C, 0, 2, 1), (C, 1, 0, 1)):
                            act.dma_start(xd[p0:p0 + C, cs, r:r + w, :, :].rearrange("p b r k m -> p (b r k m)"),
                                          XB[:, q:q + w, :, :].rearrange("p r k m -> p (r k m)")).then_inc(modes_stored, 16)

                    def body(i, first):
                        for j in range(2):
                            c, skip = i * 2 + j - 1, first and j == 0
                            for n in range(j * NR, (j + 1) * NR):
                                act.wait_ge(row_done, i * (2 * NR) + 8 + n + 1)
                                act.wait_ge(tr_done, i * (2 * NR) + n + 1)
                                nc.scalar.activation(RS[n % 2][:, :], bank(n % 2), ACT.Copy).then_inc(row_out, 1)
                                if not skip:
                                    if copy_after(n) in ON_ACT:
                                        copies(c, copy_after(n), first)
                                    if n % NR == 4 * PARTS + 2:
                                        store(c, bass.ds(c, 1))

                    body(0, True)
                    with act.Fori(1, B // 2) as i:
                        body(i, False)
                    for m in ON_ACT:
                        copies(B - 1, m)
                    store(B - 1, slice(B - 1, B))
                    act.wait_ge(modes_stored, B * 48)

                @block.vector
                def _(dve):
                    dve.sem_inc(tr_out, 2)
                    dve.sem_inc(sum_done, NX)

                    def sums_of(i, G0):
                        dve.wait_ge(loaded[G0 % NX], loaded_by(i, G0))
                        dve.wait_ge(row_done, i * (2 * NR) + 4 * G0 + 4)
                        nc.vector.tensor_tensor(ED[G0 % 2][0][:, :, :], XW[G0 % NX][:, 0, :, :],
                                                XW[G0 % NX][:, 1, :, :], ALU.add).then_inc(sum_done, 1)

                    def take(c, cs):
                        nc.vector.tensor_copy(ncur[:, :], norm2[:, :, cs].rearrange("p a b -> p (a b)")).then_inc(cur, 1)
                        dve.wait_ge(cur, c + 1)

                    def copies(c, m, first=False):
                        if m == ON_DVE[0] and not first:
                            dve.wait_ge(modes_stored, c * 48)
                        dve.wait_ge(col_done, c * PARTS + m + 1)
                        for par, slot, count, sign, pos in col_copies(m):
                            dst, src = col_views(m, par, slot, count, sign, pos)
                            last = nc.vector.tensor_scalar(dst, src, ncur[par * C:(par + 1) * C, 0:1], None, ALU.mult)
                        last.then_inc(col_dve, 1)

                    def finish(c):
                        dve.wait_ge(col_act, (c + 1) * len(ON_ACT))
                        dve.wait_ge(col_dve, (c + 1) * len(ON_DVE))
                        nc.vector.tensor_tensor(XB[:, 0, 0, 0:1], XB[:, 0, 0, 0:1], ncur[0:C, 1:2], ALU.add)
                        nc.vector.tensor_scalar(XB[:, 2, :, :], XB[:, 1, :, :], -1.0, None,
                                                ALU.mult).then_inc(neg_done, 1)

                    def body(i, first):
                        sums_of(i, 0)
                        for j in range(2):
                            c, skip = i * 2 + j - 1, first and j == 0
                            if not skip:
                                take(c, bass.ds(c, 1))
                            if not first:
                                dve.wait_ge(col_done, c * PARTS)
                            for n in range(j * NR, (j + 1) * NR):
                                if n % 4 == 1 and n // 4 + 1 < 2 * NG:
                                    sums_of(i, n // 4 + 1)
                                c0 = n % NR * 2
                                dve.wait_ge(tr_done, i * (2 * NR) + 2 + n + 1)
                                src = bank(2 + n % 2).rearrange("p (c a m) -> p c a m", c=2, a=2)
                                dst = A[j][:, :, :, c0:c0 + 2].rearrange("p a m c -> p c a m")
                                for par in range(2):
                                    last = nc.vector.tensor_copy(dst[:, :, :, par::2],
                                                                 src[:, :, :, par * C:par * C + 2 * NP])
                                last.then_inc(tr_out, 1)
                                if not skip:
                                    if copy_after(n) in ON_DVE:
                                        copies(c, copy_after(n), first)
                                    if n % NR == 4 * PARTS:
                                        finish(c)

                    body(0, True)
                    with dve.Fori(1, B // 2) as i:
                        body(i, False)
                    take(B - 1, slice(B - 1, B))
                    for m in ON_DVE:
                        copies(B - 1, m)
                    finish(B - 1)

                @block.gpsimd
                def _(pool):
                    pool.sem_inc(diff_done, NX)
                    with pool.Fori(0, B // 2) as i:
                        for G0 in range(2 * NG):
                            pool.wait_ge(loaded[G0 % NX], loaded_by(i, G0))
                            pool.wait_ge(row_done, i * (2 * NR) + 4 * G0 + 4)
                            nc.gpsimd.tensor_tensor(ED[G0 % 2][1][:, :, :], XW[G0 % NX][:, 0, :, :],
                                                    XW[G0 % NX][:, 1, :, :], ALU.subtract).then_inc(diff_done, 1)

        ph = ExitStack()
        with ph:
            WT = [sb(ph, f"mode_w{i}", [P, C, P]) for i in range(2)]
            XM = [sb(ph, f"mode_x{i}", [P, 2 * B, P]) for i in range(2)]
            YS = [sb(ph, f"mode_y{i}", [P, M2 * C]) for i in range(2)]
            loaded = [sem(f"mode_loaded{i}") for i in range(2)]
            stored = [sem(f"mode_stored{i}") for i in range(2)]
            mixed, out_act, out_dve, zero = sem("mode_mixed"), sem("mode_out_act"), sem("mode_out_dve"), sem("mode_zero")
            views = [[a.rearrange("i o x y -> i o (x y)") for a in pair] for pair in ((wr1, wi1), (wr2, wi2))]
            xm = xd.rearrange("p b r k m -> p (b r) (k m)")
            with nc.Block() as block:
                @block.sync
                def _(sp):
                    for s in range(2):
                        with sp.Fori(0, 4) as i:
                            for j in range(2):
                                sp.wait_ge(mixed, (i * 2 + j) + 8 * s + 1)
                                cw = i * 2 + j
                                for q in range(2):
                                    sp.dma_start(WT[j][q * C:(q + 1) * C, :, :],
                                                 views[s][q][:, :, bass.ds(cw * P, P)]).then_inc(loaded[j], 16)
                                pos = cw * P if s == 0 else cw * (-P) + (KX - 4) * M2
                                sp.dma_start(XM[j][:, :, :], xm[:, :, bass.ds(pos, P)]).then_inc(loaded[j], 16)

                @block.tensor
                def _(pe):
                    pe.sem_inc(mixed, 2)
                    pe.wait_ge(zero, 1)
                    for s in range(2):
                        with pe.Fori(0, 4) as i:
                            for j in range(2):
                                pe.wait_ge(loaded[j], i * 48 + 48 * (4 * s + 1))
                                pe.wait_ge(out_act, i * 2 + j + 8 * s + 1)
                                pe.wait_ge(out_dve, i * 2 + j + 8 * s + 1)
                                for ky in range(M2):
                                    for k in range(4):
                                        kx = k if s == 0 else 3 - k
                                        at = j * 2048 + ky * C
                                        last = nc.tensor.matmul(psum[32 * k:32 * k + 2 * B, at:at + C],
                                                                XM[j][:, :, kx * M2 + ky],
                                                                WT[j][:, :, k * M2 + ky], start=True, stop=True)
                                last.then_inc(mixed, 1)

                @block.scalar
                def _(act):
                    act.sem_inc(out_act, 2)
                    for j in range(2):
                        act.sem_inc(stored[j], 16)
                    for s in range(2):
                        with act.Fori(0, 4) as i:
                            for j in range(2):
                                act.wait_ge(mixed, i * 2 + j + 8 * s + 3)
                                act.wait_ge(stored[j], i * 64 + 256 * s + 16)
                                nc.scalar.activation(YS[j][:, 0:1024], psum[:, j * 2048:j * 2048 + 1024],
                                                     ACT.Copy).then_inc(out_act, 1)
                                act.wait_ge(out_act, i * 2 + j + 8 * s + 3)
                                act.wait_ge(out_dve, i * 2 + j + 8 * s + 3)
                                for k in range(4):
                                    act.dma_start(yd[:, bass.ds((i * 2 + j) * 4 + 32 * s + k, 1), :, :]
                                                  .rearrange("q k m c -> q (k m c)"),
                                                  YS[j][32 * k:32 * k + 2 * B, :]).then_inc(stored[j], 16)
                    for j in range(2):
                        act.wait_ge(stored[j], 8 * 64 + 16)

                @block.vector
                def _(dve):
                    dve.sem_inc(out_dve, 2)
                    nc.vector.memset(psum[:, :], 0.0).then_inc(zero, 1)
                    for s in range(2):
                        with dve.Fori(0, 4) as i:
                            for j in range(2):
                                dve.wait_ge(mixed, i * 2 + j + 8 * s + 3)
                                dve.wait_ge(stored[j], i * 64 + 256 * s + 16)
                                nc.vector.tensor_copy(YS[j][:, 1024:2048], psum[:, j * 2048 + 1024:j * 2048 + 2048]
                                                      ).then_inc(out_dve, 1)

        ph = ExitStack()
        with ph:
            T = table(ph, ["irow", "icol", "sign"])
            irow, icol, sign = (T[n][0] for n in ("irow", "icol", "sign"))
            NX = 2 * KEPT
            XW = x1_kept + [sb(ph, f"inv_x{i}", [P, 2, CG, W]) for i in range(NX - KEPT)]
            YA = sb(ph, "inv_ya", [P, M2, C])
            YB = sb(ph, "inv_yb", [P, M2, C])
            YY = [sb(ph, f"inv_yy{i}", [P, C, 2, M2]) for i in range(2)]
            TS = [sb(ph, f"inv_t{i}", [P, W]) for i in range(2)]
            tab, y_loaded = sem("inv_tables"), sem("inv_y_loaded")
            loaded = [sem(f"inv_loaded{i}") for i in range(NX)]
            stored = [sem(f"inv_stored{i}") for i in range(NX)]
            x_free = sem("inv_x_free")
            y_mean, y_ready, row_done, row_out, col_done, added = (
                sem("inv_" + n) for n in ("y_mean", "y", "row", "row_out", "col", "added"))
            NR = C // 2

            def batch(i, j):
                return B - 1 - j - i * 2 if isinstance(i, int) else i * -2 + (B - 1 - j)

            def group_at(n):
                return (n + KEPT) % NG * CG

            with nc.Block() as block:
                @block.sync
                def _(sp):
                    for n in ("irow", "icol", "sign"):
                        sp.dma_start(*T[n]).then_inc(tab, 16)

                    def body(i, first):
                        for j in range(2):
                            sp.wait_ge(y_ready, i * 2 + j + 1)
                            for n, dst in enumerate((YA, YB)):
                                for half in range(2):
                                    q = half if n == 0 else 1 - half
                                    sp.dma_start(dst[half * C:(half + 1) * C, :, :],
                                                 yd[bass.ds(batch(i, j) * 2 + q, 1), :, :, :]
                                                 .rearrange("q k m c -> (q k) m c")).then_inc(y_loaded, 16)
                            for g in range(NG):
                                G0 = j * NG + g
                                if first and G0 < KEPT:
                                    sp.sem_inc(loaded[g], 32)
                                    continue
                                sp.wait_ge(x_free, i * (2 * NG) + G0 + 1)
                                for a in range(2):
                                    sp.dma_start(XW[g % NX][:, a, :, :],
                                                 x1_rows[a * P:(a + 1) * P,
                                                         bass.ds(batch(i, j) * C + group_at(g), CG), :]
                                                 ).then_inc(loaded[g % NX], 16)

                    body(0, True)
                    with sp.Fori(1, B // 2) as i:
                        body(i, False)

                @block.tensor
                def _(pe):
                    pe.sem_inc(row_done, 2 * NR)
                    pe.sem_inc(col_done, 2)
                    pe.wait_ge(tab, 48)
                    with pe.Fori(0, B // 2) as i:
                        def rows(n):
                            j, o = n // NR, group_at(n % NR // 4) + n % 4 * 2
                            if n % NR == 0:
                                pe.wait_ge(y_ready, i * 2 + j + 2)
                            pe.wait_ge(row_out, i * (2 * NR) + n + 1)
                            nc.tensor.matmul(bank(6 + n % 2, W),
                                             YY[j][:, o:o + 2, :, :].rearrange("p o r k -> p (o r k)"),
                                             irow, start=True, stop=True).then_inc(row_done, 1)

                        def cols(n):
                            pe.wait_ge(row_out, i * (2 * NR) + 2 + n + 1)
                            pe.wait_ge(added, i * (2 * NR) + n + 1)
                            for a in range(2):
                                last = nc.tensor.matmul(bank(n % 2 * 2 + a), TS[n % 2][:, a * P:(a + 1) * P], icol,
                                                        start=True, stop=True)
                            last.then_inc(col_done, 1)

                        rows(0)
                        for n in range(2 * NR):
                            if n + 1 < 2 * NR:
                                rows(n + 1)
                            cols(n)

                @block.scalar
                def _(act):
                    act.sem_inc(row_out, 2)
                    act.sem_inc(y_ready, 1)
                    act.wait_ge(tab, 48)
                    with act.Fori(0, B // 2) as i:
                        for j in range(2):
                            act.wait_ge(y_mean, i * 2 + j + 1)
                            act.wait_ge(row_done, i * (2 * NR) + j * NR + NR)
                            nc.scalar.activation(YY[j][:, :, 0, :], YA[:, :, :].rearrange("p k c -> p c k"), ACT.Copy)
                            nc.scalar.activation(YY[j][:, :, 1, :], YB[:, :, :].rearrange("p k c -> p c k"), ACT.Copy,
                                                 scale=sign[:, 0:1]).then_inc(y_ready, 1)
                            for n in range(j * NR, (j + 1) * NR):
                                act.wait_ge(row_done, i * (2 * NR) + 2 * NR + n + 1)
                                act.wait_ge(col_done, i * (2 * NR) + n + 1)
                                nc.scalar.activation(TS[n % 2][:, :], bank(6 + n % 2, W), ACT.Copy).then_inc(row_out, 1)

                @block.vector
                def _(dve):
                    dve.sem_inc(added, 2)
                    with dve.Fori(0, B // 2) as i:
                        for n in range(2 * NR):
                            if n in (0, NR - 2):
                                j = int(n > 0)
                                dve.wait_ge(y_loaded, (i * 2 + j) * 64 + 64)
                                nc.vector.tensor_tensor(YA[0:1, 0, :], YA[0:1, 0, :],
                                                        mrow[:, bass.ds(batch(i, j) * C, C)],
                                                        ALU.add).then_inc(y_mean, 1)
                            G0, cp = n // 4, n % 4
                            xw = XW[G0 % NX][:, :, 2 * cp:2 * cp + 2, :].rearrange("p a c w -> p a (c w)")
                            if cp == 0:
                                dve.wait_ge(loaded[G0 % NX], i * (2 * NG // NX * 32) + G0 // NX * 32 + 32)
                            dve.wait_ge(col_done, i * (2 * NR) + 2 + n + 1)
                            nc.vector.tensor_tensor(xw, xw, psum[:, n % 2 * 1024:n % 2 * 1024 + 1024]
                                                    .rearrange("p (a k) -> p a k", a=2), ALU.add).then_inc(added, 1)

                @block.gpsimd
                def _(pool):
                    pool.sem_inc(x_free, NX)
                    with pool.Fori(0, B // 2) as i:
                        for G0 in range(2 * NG + 1):
                            if G0 < 2 * NG:
                                pool.wait_ge(added, i * (2 * NR) + 2 + 4 * (G0 + 1))
                                for a in range(2):
                                    pool.dma_start(out_rows[a * P:(a + 1) * P,
                                                            bass.ds(batch(i, G0 // NG) * C + group_at(G0), CG), :],
                                                   XW[G0 % NX][:, a, :, :]).then_inc(stored[G0 % NX], 16)
                            if G0 >= 1:
                                G1 = G0 - 1
                                pool.wait_ge(stored[G1 % NX], i * (2 * NG // NX * 32) + (G1 // NX + 1) * 32)
                                pool.sem_inc(x_free, 1)
                    for q in range(NX):
                        pool.wait_ge(stored[q], B * NG // NX * 32)


_INS = ["x", "L0_conv_mlp1_w", "L0_conv_mlp1_b", "L0_conv_mlp2_w", "L0_conv_mlp2_b", "L0_conv_sa1_w",
        "L0_conv_sa2_w", "L0_conv_bn_gamma", "L0_conv_bn_beta", "L1_conv_w1_real", "L1_conv_w1_imag",
        "L1_conv_w2_real", "L1_conv_w2_imag"]


def kernel(**inputs):
    import numpy as _np
    import concourse.bacc as _bacc
    from concourse.bass_utils import run_bass_kernel_spmd as _run

    nc = _bacc.Bacc("TRN2", target_bir_lowering=False, num_devices=1)
    arrays, args = {}, []
    for name in _INS:
        a = _np.ascontiguousarray(inputs[name])
        arrays[name] = a
        args.append(nc.dram_tensor(name, a.shape, F32, kind="ExternalInput").ap())
    arrays["tables"] = CONST
    args.append(nc.dram_tensor("tables", CONST.shape, F32, kind="ExternalInput").ap())
    args.append(nc.dram_tensor("out", (B, C, H, W), F32, kind="ExternalOutput").ap())
    program(nc, *args)
    r = _run(nc, [arrays], core_ids=[0])
    return r.results[0]["out"]
```
